# Optimizing a Trainium2 kernel written in Bass

```python
import numpy as np
import jax
import jax.numpy as jnp

def _softmax(x, axis=-1):
    return jax.nn.softmax(x, axis=axis)

def _gelu(x):
    return jax.nn.gelu(x, approximate=True)

def _silu(x):
    return jax.nn.silu(x)

def _sigmoid(x):
    return jax.nn.sigmoid(x)

def _layernorm(x, axis=-1, eps=1e-05):
    m = jnp.mean(x, axis=axis, keepdims=True)
    v = jnp.var(x, axis=axis, keepdims=True)
    return (x - m) / jnp.sqrt(v + eps)

def _scatter_add(tgt, idx, src, axis=0):
    return tgt.at[idx].add(src)

def _segment_sum(src, seg, n):
    return jax.ops.segment_sum(src, seg, n)
kernel_name = 'mk_perceiver_d4_seqx_r8_1a6461'

def setup_inputs(seed: int=0):
    np.random.seed(seed)
    _w = jnp.asarray

    def _rec_inputs():
        import jax
        import jax.numpy as jnp
        _rk = jax.random.key(seed)
        x = -0.0002928 + 1 * jax.random.normal(jax.random.fold_in(_rk, 1), (16, 64, 128), jnp.float32)
        _lenS = 64 - jax.random.randint(jax.random.fold_in(_rk, 7), (16,), 0, max(1, 64 // 4) + 1, jnp.int32)
        _lenS2 = 1601 - jax.random.randint(jax.random.fold_in(_rk, 8), (16,), 0, max(1, 1601 // 4) + 1, jnp.int32)
        _ctx_1024P = jax.random.normal(jax.random.fold_in(_rk, 11), (16, 16, 128), jnp.float32)
        _ctx_1024c = jax.random.dirichlet(jax.random.fold_in(_rk, 511), 0.3 * jnp.ones((16,), jnp.float32), (16, 1601))
        _ctx_1024t = jnp.einsum('bsk,bkd->bsd', _ctx_1024c, _ctx_1024P)
        _ctx_1024t = _ctx_1024t * jax.lax.rsqrt(jnp.mean(jnp.square(_ctx_1024t)) + 1e-12) * 0.953939
        ctx_1024 = -1.39393e-06 + 0.999914 * (_ctx_1024t + 0.3 * jax.random.normal(jax.random.fold_in(_rk, 611), (16, 1601, 128), jnp.float32))
        _validS = jnp.arange(64)[None, :] < _lenS[:, None]
        _validS2 = jnp.arange(1601)[None, :] < _lenS2[:, None]
        _causal = jnp.tril(jnp.ones((64, 64), dtype=bool))
        mask_BxS2_bk0 = jnp.logical_not(jnp.broadcast_to(_validS2[:, :], (16, 1601)))
        mask_BxSxS2_bk1 = jnp.broadcast_to(_validS2[:, None, :], (16, 64, 1601))
        return (x, ctx_1024, mask_BxS2_bk0, mask_BxSxS2_bk1)
    x, ctx_1024, mask_BxS2_bk0, mask_BxSxS2_bk1 = _rec_inputs()

    def _L0_xattn_setup():
        import jax, jax.numpy as jnp
        import numpy as np
        import math
        EMBED_DIM = 128
        NUM_HEADS = 16
        HEAD_DIM = EMBED_DIM // NUM_HEADS
        SUB_HEAD_DIM = HEAD_DIM // 2
        SCALING = 1.0 / math.sqrt(SUB_HEAD_DIM)
        LAMBDA_INIT = 0.8 - 0.6 * math.exp(-0.3 * 0)
        key = jax.random.key(seed)
        ks = jax.random.split(key, 10)
        B, T, D = (2, 256, EMBED_DIM)
        xav = math.sqrt(6.0 / (D + D))
        return {'query': jax.random.normal(ks[0], (B, T, D), jnp.float32), 'key': jax.random.normal(ks[1], (B, T, D), jnp.float32), 'value': jax.random.normal(ks[2], (B, T, D), jnp.float32), 'in_proj_weight': jax.random.uniform(ks[3], (3 * D, D), jnp.float32, -xav, xav), 'in_proj_bias': jnp.zeros((3 * D,), jnp.float32), 'out_proj_weight': jax.random.uniform(ks[4], (D, D), jnp.float32, -xav, xav), 'out_proj_bias': jnp.zeros((D,), jnp.float32), 'lambda_q1': 0.1 * jax.random.normal(ks[5], (SUB_HEAD_DIM,), jnp.float32), 'lambda_k1': 0.1 * jax.random.normal(ks[6], (SUB_HEAD_DIM,), jnp.float32), 'lambda_q2': 0.1 * jax.random.normal(ks[7], (SUB_HEAD_DIM,), jnp.float32), 'lambda_k2': 0.1 * jax.random.normal(ks[8], (SUB_HEAD_DIM,), jnp.float32)}
    _L0_xattn_all = _L0_xattn_setup()
    _L0_xattn_in = {k: v for k, v in _L0_xattn_all.items() if k in ('in_proj_weight', 'in_proj_bias', 'out_proj_weight', 'out_proj_bias', 'lambda_q1', 'lambda_k1', 'lambda_q2', 'lambda_k2')}
    del _L0_xattn_all

    def _L0_attn_setup():
        import jax, jax.numpy as jnp
        import numpy as np
        HIDDEN = 128
        N_HEAD = 16
        HEAD_DIM = HIDDEN // N_HEAD

        def _rope(q, k):
            S, D = (q.shape[-2], q.shape[-1])
            pos = jnp.arange(S, dtype=jnp.float32)[:, None]
            ids = jnp.arange(D // 2, dtype=jnp.float32)
            theta = jnp.power(jnp.float32(10000.0), 2.0 * ids / D)
            ang = pos / theta
            sin = jnp.repeat(jnp.sin(ang), 2, axis=-1)
            cos = jnp.repeat(jnp.cos(ang), 2, axis=-1)

            def rot(t):
                t2 = jnp.stack([-t[..., 1::2], t[..., 0::2]], axis=-1).reshape(t.shape)
                return t * cos + t2 * sin
            return (rot(q), rot(k))
        key = jax.random.key(seed)
        k1, k2, k3 = jax.random.split(key, 3)
        B, S = (4, 256)
        x = jax.random.normal(k1, (B, S, HIDDEN), dtype=jnp.float32)
        w_qkv = jax.random.normal(k2, (3 * HIDDEN, HIDDEN), dtype=jnp.float32) * HIDDEN ** (-0.5)
        w_out = jax.random.normal(k3, (HIDDEN, HIDDEN), dtype=jnp.float32) * HIDDEN ** (-0.5)
        return {'x': x, 'w_qkv': w_qkv, 'w_out': w_out}
    _L0_attn_all = _L0_attn_setup()
    _L0_attn_in = {k: v for k, v in _L0_attn_all.items() if k in ('w_qkv', 'w_out')}
    del _L0_attn_all

    def _L0_ffn_setup():
        import jax, jax.numpy as jnp
        import numpy as np
        B, S, D, F, E, K = (4, 256, 128, 512, 4, 2)
        key = jax.random.key(seed)
        k = jax.random.split(key, 6)
        x = jax.random.normal(k[0], (B, S, D), jnp.float32)
        router_w = jax.random.normal(k[1], (D, E), jnp.float32) * D ** (-0.5)
        router_b = jnp.zeros((E,), jnp.float32)
        w1 = jax.random.normal(k[2], (E, D, F), jnp.float32) * 0.02
        w3 = jax.random.normal(k[3], (E, D, F), jnp.float32) * 0.02
        w2 = jax.random.normal(k[4], (E, F, D), jnp.float32) * 0.02
        return {'x': x, 'router_w': router_w, 'router_b': router_b, 'w1': w1, 'w3': w3, 'w2': w2}
    _L0_ffn_all = _L0_ffn_setup()
    _L0_ffn_in = {k: v for k, v in _L0_ffn_all.items() if k in ('router_w', 'router_b', 'w1', 'w3', 'w2')}
    del _L0_ffn_all

    def _L1_xattn_setup():
        import jax, jax.numpy as jnp
        import numpy as np
        DIM, DIM_HEAD, HEADS, SCALE = (128, 64, 8, 8.0)
        INNER = DIM_HEAD * HEADS
        LN_EPS = 1e-05
        L2_EPS = 1e-12

        def layer_norm(x, w, b):
            mu = jnp.mean(x, axis=-1, keepdims=True)
            var = jnp.mean(jnp.square(x - mu), axis=-1, keepdims=True)
            return (x - mu) * jax.lax.rsqrt(var + LN_EPS) * w + b

        def l2norm(t):
            n = jnp.sqrt(jnp.sum(jnp.square(t), axis=-1, keepdims=True))
            return t / jnp.maximum(n, L2_EPS)
        key = jax.random.key(seed)
        ks = jax.random.split(key, 8)
        b, n, m = (8, 1024, 64)
        x = jax.random.normal(ks[0], (b, n, DIM), dtype=jnp.float32)
        latents = jax.random.normal(ks[1], (b, m, DIM), dtype=jnp.float32)
        mask = jax.random.randint(ks[2], (b, n), 0, 2) > 0
        Wq = jax.random.normal(ks[3], (DIM, INNER), dtype=jnp.float32) * DIM ** (-0.5)
        Wkv = jax.random.normal(ks[4], (DIM, 2 * INNER), dtype=jnp.float32) * DIM ** (-0.5)
        Wo = jax.random.normal(ks[5], (INNER, DIM), dtype=jnp.float32) * INNER ** (-0.5)
        return {'x': x, 'latents': latents, 'mask': mask, 'ln_x_w': jnp.ones((DIM,)), 'ln_x_b': jnp.zeros((DIM,)), 'ln_l_w': jnp.ones((DIM,)), 'ln_l_b': jnp.zeros((DIM,)), 'Wq': Wq, 'Wkv': Wkv, 'q_scale': jnp.ones((DIM_HEAD,)), 'k_scale': jnp.ones((DIM_HEAD,)), 'Wo': Wo, 'ln_o_w': jnp.ones((DIM,)), 'ln_o_b': jnp.zeros((DIM,))}
    _L1_xattn_all = _L1_xattn_setup()
    _L1_xattn_in = {k: v for k, v in _L1_xattn_all.items() if k in ('ln_x_w', 'ln_x_b', 'ln_l_w', 'ln_l_b', 'Wq', 'Wkv', 'q_scale', 'k_scale', 'Wo', 'ln_o_w', 'ln_o_b')}
    del _L1_xattn_all

    def _L1_attn_setup():
        import jax, jax.numpy as jnp
        import numpy as np
        D_MODEL = 128
        B, T = (8, 512)

        def _diag_scan(decays, injections):

            def combine(e1, e2):
                a1, b1 = e1
                a2, b2 = e2
                return (a1 * a2, a2 * b1 + b2)
            _, states = jax.lax.associative_scan(combine, (decays, injections), axis=1)
            return states
        key = jax.random.key(seed)
        k_x, k_wd, k_wi, k_bi = jax.random.split(key, 4)
        lim = 1.0 / np.sqrt(D_MODEL)
        x_seq = jax.random.normal(k_x, (B, T, D_MODEL), dtype=jnp.float32)
        W_decay = jax.random.uniform(k_wd, (D_MODEL, D_MODEL), minval=-lim, maxval=lim, dtype=jnp.float32)
        b_decay = jnp.full((D_MODEL,), 1.4, dtype=jnp.float32)
        W_input = jax.random.uniform(k_wi, (D_MODEL, D_MODEL), minval=-lim, maxval=lim, dtype=jnp.float32)
        b_input = jax.random.uniform(k_bi, (D_MODEL,), minval=-lim, maxval=lim, dtype=jnp.float32)
        return {'x_seq': x_seq, 'W_decay': W_decay, 'b_decay': b_decay, 'W_input': W_input, 'b_input': b_input}
    _L1_attn_all = _L1_attn_setup()
    _L1_attn_in = {k: v for k, v in _L1_attn_all.items() if k in ('W_decay', 'b_decay', 'W_input', 'b_input')}
    del _L1_attn_all

    def _L1_ffn_setup():
        import jax, jax.numpy as jnp
        import numpy as np
        B, N, C, F, E, K = (2, 256, 128, 512, 8, 2)
        key = jax.random.key(seed)
        k = jax.random.split(key, 6)
        xavier1 = float(np.sqrt(6.0 / (C + F)))
        xavier2 = float(np.sqrt(6.0 / (F + C)))
        return {'x': jax.random.normal(k[0], (B, N, C), dtype=jnp.float32), 'router_w': jax.random.normal(k[1], (E, C), dtype=jnp.float32) * 0.01, 'w1': jax.random.uniform(k[2], (E, F, C), dtype=jnp.float32, minval=-xavier1, maxval=xavier1), 'b1': jnp.zeros((E, F), dtype=jnp.float32), 'w2': jax.random.uniform(k[3], (E, C, F), dtype=jnp.float32, minval=-xavier2, maxval=xavier2), 'b2': jnp.zeros((E, C), dtype=jnp.float32)}
    _L1_ffn_all = _L1_ffn_setup()
    _L1_ffn_in = {k: v for k, v in _L1_ffn_all.items() if k in ('router_w', 'w1', 'b1', 'w2', 'b2')}
    del _L1_ffn_all

    def _L2_xattn_setup():
        import jax, jax.numpy as jnp
        import numpy as np
        HIDDEN = 128
        key = jax.random.key(seed)
        kq, kk, kwq, kwk, kwv = jax.random.split(key, 5)
        B, S, D = (4, 256, HIDDEN)
        query = jax.random.normal(kq, (B, S, D), dtype=jnp.float32)
        key_t = jax.random.normal(kk, (B, S, D), dtype=jnp.float32)
        scale = 1.0 / np.sqrt(D)
        Wq = jax.random.normal(kwq, (D, D), dtype=jnp.float32) * scale
        Wk = jax.random.normal(kwk, (D, D), dtype=jnp.float32) * scale
        Wv = jax.random.normal(kwv, (D, D), dtype=jnp.float32) * scale
        return {'query': query, 'key': key_t, 'Wq': Wq, 'Wk': Wk, 'Wv': Wv}
    _L2_xattn_all = _L2_xattn_setup()
    _L2_xattn_in = {k: v for k, v in _L2_xattn_all.items() if k in ('Wq', 'Wk', 'Wv')}
    del _L2_xattn_all

    def _L2_attn_setup():
        import jax, jax.numpy as jnp
        import numpy as np
        import math
        B, T, D, H = (4, 256, 128, 16)
        HD = D // H
        ROPE_BASE = 10000.0

        def apply_rope(x):
            t, hd = (x.shape[2], x.shape[3])
            half = hd // 2
            theta = 1.0 / ROPE_BASE ** (jnp.arange(0, hd, 2, dtype=jnp.float32) / hd)
            pos = jnp.arange(1, t + 1, dtype=jnp.float32)
            ang = pos[:, None] * theta[None, :]
            ang = jnp.concatenate([ang, ang], axis=-1)
            sin, cos = (jnp.sin(ang), jnp.cos(ang))
            rot = jnp.concatenate([-x[..., half:], x[..., :half]], axis=-1)
            return x * cos[None, None, :, :] + rot * sin[None, None, :, :]
        key = jax.random.key(seed)
        ks = jax.random.split(key, 9)
        s = 1.0 / math.sqrt(D)
        return {'x': jax.random.normal(ks[0], (B, T, D), dtype=jnp.float32), 'Wq': jax.random.normal(ks[1], (D, D), dtype=jnp.float32) * s, 'bq': jax.random.normal(ks[2], (D,), dtype=jnp.float32) * 0.01, 'Wk': jax.random.normal(ks[3], (D, D), dtype=jnp.float32) * s, 'bk': jax.random.normal(ks[4], (D,), dtype=jnp.float32) * 0.01, 'Wv': jax.random.normal(ks[5], (D, D), dtype=jnp.float32) * s, 'bv': jax.random.normal(ks[6], (D,), dtype=jnp.float32) * 0.01, 'Wo': jax.random.normal(ks[7], (D, D), dtype=jnp.float32) * s, 'bo': jax.random.normal(ks[8], (D,), dtype=jnp.float32) * 0.01}
    _L2_attn_all = _L2_attn_setup()
    _L2_attn_in = {k: v for k, v in _L2_attn_all.items() if k in ('Wq', 'bq', 'Wk', 'bk', 'Wv', 'bv', 'Wo', 'bo')}
    del _L2_attn_all

    def _L2_ffn_setup():
        import jax, jax.numpy as jnp
        import numpy as np
        B, T, H = (8, 256, 128)
        F = 512
        E = 8
        TOP_K = 2
        key = jax.random.key(seed)
        ks = jax.random.split(key, 6)
        s_h = 1.0 / np.sqrt(H)
        s_f = 1.0 / np.sqrt(F)
        return {'hidden_states': jax.random.normal(ks[0], (B, T, H), dtype=jnp.float32), 'gate_w': jax.random.uniform(ks[1], (H, E), minval=-s_h, maxval=s_h, dtype=jnp.float32), 'w1': jax.random.uniform(ks[2], (E, H, F), minval=-s_h, maxval=s_h, dtype=jnp.float32), 'b1': jax.random.uniform(ks[3], (E, F), minval=-s_h, maxval=s_h, dtype=jnp.float32), 'w2': jax.random.uniform(ks[4], (E, F, H), minval=-s_f, maxval=s_f, dtype=jnp.float32), 'b2': jax.random.uniform(ks[5], (E, H), minval=-s_f, maxval=s_f, dtype=jnp.float32)}
    _L2_ffn_all = _L2_ffn_setup()
    _L2_ffn_in = {k: v for k, v in _L2_ffn_all.items() if k in ('gate_w', 'w1', 'b1', 'w2', 'b2')}
    del _L2_ffn_all

    def _L3_xattn_setup():
        import jax, jax.numpy as jnp
        import numpy as np
        B, S, D_MODEL, N_HEADS, D_K, D_V = (2, 256, 128, 16, 64, 64)
        key = jax.random.key(seed)
        k1, k2, k3, k4, k5, k6, k7 = jax.random.split(key, 7)
        scale = 1.0 / np.sqrt(D_MODEL)
        inputs = {'input_Q': jax.random.normal(k1, (B, S, D_MODEL), dtype=jnp.float32), 'input_K': jax.random.normal(k2, (B, S, D_MODEL), dtype=jnp.float32), 'input_V': jax.random.normal(k3, (B, S, D_MODEL), dtype=jnp.float32), 'attn_mask': jnp.broadcast_to(~jnp.tril(jnp.ones((S, S), dtype=bool)), (B, S, S)), 'flag': 0, 'W_Q': jax.random.normal(k4, (D_MODEL, N_HEADS * D_K), dtype=jnp.float32) * scale, 'W_K': jax.random.normal(k5, (D_MODEL, N_HEADS * D_K), dtype=jnp.float32) * scale, 'W_V': jax.random.normal(k6, (D_MODEL, N_HEADS * D_V), dtype=jnp.float32) * scale, 'W_O': jax.random.normal(k7, (N_HEADS * D_V, D_MODEL), dtype=jnp.float32) * scale}
        return inputs
    _L3_xattn_all = _L3_xattn_setup()
    _L3_xattn_in = {k: v for k, v in _L3_xattn_all.items() if k in ('W_Q', 'W_K', 'W_V', 'W_O')}
    del _L3_xattn_all

    def _L3_attn_setup():
        import math
        import jax, jax.numpy as jnp
        import numpy as np
        D_MODEL = 128
        NUM_HEADS = 16
        D_HEAD = D_MODEL // NUM_HEADS
        K_S = 32
        B, N = (2, 256)

        def _attn(x, Wq, bq, Wk, bk, Wv, bv, Wo, bo):
            b, n, _ = x.shape
            q = (x @ Wq.T + bq).reshape(b, n, NUM_HEADS, D_HEAD).transpose(0, 2, 1, 3)
            k = (x @ Wk.T + bk).reshape(b, n, NUM_HEADS, D_HEAD).transpose(0, 2, 1, 3)
            v = (x @ Wv.T + bv).reshape(b, n, NUM_HEADS, D_HEAD).transpose(0, 2, 1, 3)
            scores = jnp.einsum('bhqd,bhkd->bhqk', q, k) / math.sqrt(D_HEAD)
            causal = jnp.triu(jnp.ones((n, n), dtype=bool), k=1)
            neg_inf = jnp.array(-jnp.inf, dtype=scores.dtype)
            scores = jnp.where(causal, neg_inf, scores)
            vals, idx = jax.lax.top_k(scores, K_S)
            masked = jnp.full_like(scores, -jnp.inf)
            masked = jnp.put_along_axis(masked, idx, vals, axis=-1, inplace=False)
            attn = jax.nn.softmax(masked, axis=-1)
            out = jnp.einsum('bhqk,bhkd->bhqd', attn, v)
            out = out.transpose(0, 2, 1, 3).reshape(b, n, D_MODEL)
            y = out @ Wo.T + bo
            return (y, attn.mean(axis=1))

        def _reference_tuple_inner(x, Wq, bq, Wk, bk, Wv, bv, Wo, bo):
            return _attn(x, Wq, bq, Wk, bk, Wv, bv, Wo, bo)
        key = jax.random.key(seed)
        ks = jax.random.split(key, 9)
        s = 1.0 / math.sqrt(D_MODEL)
        return {'x': jax.random.normal(ks[0], (B, N, D_MODEL), dtype=jnp.float32), 'Wq': jax.random.normal(ks[1], (D_MODEL, D_MODEL), dtype=jnp.float32) * s, 'bq': jnp.zeros((D_MODEL,), dtype=jnp.float32), 'Wk': jax.random.normal(ks[2], (D_MODEL, D_MODEL), dtype=jnp.float32) * s, 'bk': jnp.zeros((D_MODEL,), dtype=jnp.float32), 'Wv': jax.random.normal(ks[3], (D_MODEL, D_MODEL), dtype=jnp.float32) * s, 'bv': jnp.zeros((D_MODEL,), dtype=jnp.float32), 'Wo': jax.random.normal(ks[4], (D_MODEL, D_MODEL), dtype=jnp.float32) * s, 'bo': jnp.zeros((D_MODEL,), dtype=jnp.float32)}
    _L3_attn_all = _L3_attn_setup()
    _L3_attn_in = {k: v for k, v in _L3_attn_all.items() if k in ('Wq', 'bq', 'Wk', 'bk', 'Wv', 'bv', 'Wo', 'bo')}
    del _L3_attn_all

    def _L3_ffn_setup():
        import jax, jax.numpy as jnp
        import numpy as np
        INT4_QMAX = 7.0

        def simulate_quantize_int4(w):
            scale = jnp.max(jnp.abs(w)) / INT4_QMAX
            q = jnp.clip(jnp.round(w / scale), -8.0, 7.0)
            return q * scale
        key = jax.random.key(seed)
        k_x, k_w, k_bias, k_a, k_b = jax.random.split(key, 5)
        d_in, features, rank = (128, 128, 16)
        x = jax.random.normal(k_x, (4, 1024, d_in), dtype=jnp.float32)
        kernel = jax.random.normal(k_w, (d_in, features), dtype=jnp.float32)
        bias = jax.random.normal(k_bias, (features,), dtype=jnp.float32)
        a = jax.random.normal(k_a, (d_in, rank), dtype=jnp.float32) * (1.0 / np.sqrt(d_in))
        b = jax.random.normal(k_b, (rank, features), dtype=jnp.float32) * 0.01
        return {'x': x, 'kernel': kernel, 'bias': bias, 'a': a, 'b': b}
    _L3_ffn_all = _L3_ffn_setup()
    _L3_ffn_in = {k: v for k, v in _L3_ffn_all.items() if k in ('kernel', 'bias', 'a', 'b')}
    del _L3_ffn_all
    return {'x': x, 'ctx_1024': ctx_1024, 'mask_BxS2_bk0': mask_BxS2_bk0, 'mask_BxSxS2_bk1': mask_BxSxS2_bk1, 'L0_xattn_in_proj_weight': _L0_xattn_in['in_proj_weight'], 'L0_xattn_in_proj_bias': _L0_xattn_in['in_proj_bias'], 'L0_xattn_out_proj_weight': _L0_xattn_in['out_proj_weight'], 'L0_xattn_out_proj_bias': _L0_xattn_in['out_proj_bias'], 'L0_xattn_lambda_q1': _L0_xattn_in['lambda_q1'], 'L0_xattn_lambda_k1': _L0_xattn_in['lambda_k1'], 'L0_xattn_lambda_q2': _L0_xattn_in['lambda_q2'], 'L0_xattn_lambda_k2': _L0_xattn_in['lambda_k2'], 'L0_attn_w_qkv': _L0_attn_in['w_qkv'], 'L0_attn_w_out': _L0_attn_in['w_out'], 'L0_ffn_router_w': _L0_ffn_in['router_w'], 'L0_ffn_router_b': _L0_ffn_in['router_b'], 'L0_ffn_w1': _L0_ffn_in['w1'], 'L0_ffn_w3': _L0_ffn_in['w3'], 'L0_ffn_w2': _L0_ffn_in['w2'], 'L1_xattn_ln_x_w': _L1_xattn_in['ln_x_w'], 'L1_xattn_ln_x_b': _L1_xattn_in['ln_x_b'], 'L1_xattn_ln_l_w': _L1_xattn_in['ln_l_w'], 'L1_xattn_ln_l_b': _L1_xattn_in['ln_l_b'], 'L1_xattn_Wq': _L1_xattn_in['Wq'], 'L1_xattn_Wkv': _L1_xattn_in['Wkv'], 'L1_xattn_q_scale': _L1_xattn_in['q_scale'], 'L1_xattn_k_scale': _L1_xattn_in['k_scale'], 'L1_xattn_Wo': _L1_xattn_in['Wo'], 'L1_xattn_ln_o_w': _L1_xattn_in['ln_o_w'], 'L1_xattn_ln_o_b': _L1_xattn_in['ln_o_b'], 'L1_attn_W_decay': _L1_attn_in['W_decay'], 'L1_attn_b_decay': _L1_attn_in['b_decay'], 'L1_attn_W_input': _L1_attn_in['W_input'], 'L1_attn_b_input': _L1_attn_in['b_input'], 'L1_ffn_router_w': _L1_ffn_in['router_w'], 'L1_ffn_w1': _L1_ffn_in['w1'], 'L1_ffn_b1': _L1_ffn_in['b1'], 'L1_ffn_w2': _L1_ffn_in['w2'], 'L1_ffn_b2': _L1_ffn_in['b2'], 'L2_xattn_Wq': _L2_xattn_in['Wq'], 'L2_xattn_Wk': _L2_xattn_in['Wk'], 'L2_xattn_Wv': _L2_xattn_in['Wv'], 'L2_attn_Wq': _L2_attn_in['Wq'], 'L2_attn_bq': _L2_attn_in['bq'], 'L2_attn_Wk': _L2_attn_in['Wk'], 'L2_attn_bk': _L2_attn_in['bk'], 'L2_attn_Wv': _L2_attn_in['Wv'], 'L2_attn_bv': _L2_attn_in['bv'], 'L2_attn_Wo': _L2_attn_in['Wo'], 'L2_attn_bo': _L2_attn_in['bo'], 'L2_ffn_gate_w': _L2_ffn_in['gate_w'], 'L2_ffn_w1': _L2_ffn_in['w1'], 'L2_ffn_b1': _L2_ffn_in['b1'], 'L2_ffn_w2': _L2_ffn_in['w2'], 'L2_ffn_b2': _L2_ffn_in['b2'], 'L3_xattn_W_Q': _L3_xattn_in['W_Q'], 'L3_xattn_W_K': _L3_xattn_in['W_K'], 'L3_xattn_W_V': _L3_xattn_in['W_V'], 'L3_xattn_W_O': _L3_xattn_in['W_O'], 'L3_attn_Wq': _L3_attn_in['Wq'], 'L3_attn_bq': _L3_attn_in['bq'], 'L3_attn_Wk': _L3_attn_in['Wk'], 'L3_attn_bk': _L3_attn_in['bk'], 'L3_attn_Wv': _L3_attn_in['Wv'], 'L3_attn_bv': _L3_attn_in['bv'], 'L3_attn_Wo': _L3_attn_in['Wo'], 'L3_attn_bo': _L3_attn_in['bo'], 'L3_ffn_kernel': _L3_ffn_in['kernel'], 'L3_ffn_bias': _L3_ffn_in['bias'], 'L3_ffn_a': _L3_ffn_in['a'], 'L3_ffn_b': _L3_ffn_in['b']}

def reference(x, ctx_1024, mask_BxS2_bk0, mask_BxSxS2_bk1, L0_xattn_in_proj_weight, L0_xattn_in_proj_bias, L0_xattn_out_proj_weight, L0_xattn_out_proj_bias, L0_xattn_lambda_q1, L0_xattn_lambda_k1, L0_xattn_lambda_q2, L0_xattn_lambda_k2, L0_attn_w_qkv, L0_attn_w_out, L0_ffn_router_w, L0_ffn_router_b, L0_ffn_w1, L0_ffn_w3, L0_ffn_w2, L1_xattn_ln_x_w, L1_xattn_ln_x_b, L1_xattn_ln_l_w, L1_xattn_ln_l_b, L1_xattn_Wq, L1_xattn_Wkv, L1_xattn_q_scale, L1_xattn_k_scale, L1_xattn_Wo, L1_xattn_ln_o_w, L1_xattn_ln_o_b, L1_attn_W_decay, L1_attn_b_decay, L1_attn_W_input, L1_attn_b_input, L1_ffn_router_w, L1_ffn_w1, L1_ffn_b1, L1_ffn_w2, L1_ffn_b2, L2_xattn_Wq, L2_xattn_Wk, L2_xattn_Wv, L2_attn_Wq, L2_attn_bq, L2_attn_Wk, L2_attn_bk, L2_attn_Wv, L2_attn_bv, L2_attn_Wo, L2_attn_bo, L2_ffn_gate_w, L2_ffn_w1, L2_ffn_b1, L2_ffn_w2, L2_ffn_b2, L3_xattn_W_Q, L3_xattn_W_K, L3_xattn_W_V, L3_xattn_W_O, L3_attn_Wq, L3_attn_bq, L3_attn_Wk, L3_attn_bk, L3_attn_Wv, L3_attn_bv, L3_attn_Wo, L3_attn_bo, L3_ffn_kernel, L3_ffn_bias, L3_ffn_a, L3_ffn_b):
    import jax
    import jax.numpy as jnp

    def _L0_xattn_ref(query, key, value, in_proj_weight, in_proj_bias, out_proj_weight, out_proj_bias, lambda_q1, lambda_k1, lambda_q2, lambda_k2):
        import jax, jax.numpy as jnp
        import numpy as np
        import math
        EMBED_DIM = 128
        NUM_HEADS = 16
        HEAD_DIM = EMBED_DIM // NUM_HEADS
        SUB_HEAD_DIM = HEAD_DIM // 2
        SCALING = 1.0 / math.sqrt(SUB_HEAD_DIM)
        LAMBDA_INIT = 0.8 - 0.6 * math.exp(-0.3 * 0)
        B, T, D = query.shape
        S = key.shape[1]
        H, hd, sd = (NUM_HEADS, HEAD_DIM, SUB_HEAD_DIM)
        qw, kw, vw = jnp.split(in_proj_weight, 3, axis=0)
        qb, kb, vb = jnp.split(in_proj_bias, 3, axis=0)
        q = query @ qw.T + qb
        k = key @ kw.T + kb
        v = value @ vw.T + vb
        q = q.reshape(B, T, H, hd).transpose(0, 2, 1, 3)
        k = k.reshape(B, S, H, hd).transpose(0, 2, 1, 3)
        v = v.reshape(B, S, H, hd).transpose(0, 2, 1, 3)
        q1, q2 = (q[..., :sd], q[..., sd:])
        k1, k2 = (k[..., :sd], k[..., sd:])
        logits_1 = jnp.einsum('bhtd,bhsd->bhts', q1, k1) * SCALING
        logits_2 = jnp.einsum('bhtd,bhsd->bhts', q2, k2) * SCALING
        a1 = jax.nn.softmax(logits_1, axis=-1)
        a2 = jax.nn.softmax(logits_2, axis=-1)
        lam = jnp.exp(jnp.dot(lambda_q1, lambda_k1)) - jnp.exp(jnp.dot(lambda_q2, lambda_k2)) + LAMBDA_INIT
        diff_weights = a1 - lam * a2
        attn_output = jnp.einsum('bhts,bhsd->bhtd', diff_weights, v)
        attn_output = attn_output * (1.0 - LAMBDA_INIT)
        attn_output = attn_output.transpose(0, 2, 1, 3).reshape(B, T, D)
        output = attn_output @ out_proj_weight.T + out_proj_bias
        return output

    def _L0_attn_ref(x, w_qkv, w_out):
        import jax, jax.numpy as jnp
        import numpy as np
        HIDDEN = 128
        N_HEAD = 16
        HEAD_DIM = HIDDEN // N_HEAD

        def _rope(q, k):
            S, D = (q.shape[-2], q.shape[-1])
            pos = jnp.arange(S, dtype=jnp.float32)[:, None]
            ids = jnp.arange(D // 2, dtype=jnp.float32)
            theta = jnp.power(jnp.float32(10000.0), 2.0 * ids / D)
            ang = pos / theta
            sin = jnp.repeat(jnp.sin(ang), 2, axis=-1)
            cos = jnp.repeat(jnp.cos(ang), 2, axis=-1)

            def rot(t):
                t2 = jnp.stack([-t[..., 1::2], t[..., 0::2]], axis=-1).reshape(t.shape)
                return t * cos + t2 * sin
            return (rot(q), rot(k))
        B, S, _ = x.shape
        qkv = jnp.einsum('bsd,ed->bse', x, w_qkv)
        qkv = qkv.reshape(B, S, N_HEAD, 3 * HEAD_DIM).transpose(0, 2, 1, 3)
        q, k, v = jnp.split(qkv, 3, axis=-1)
        q, k = _rope(q, k)
        scores = jnp.einsum('bhqd,bhkd->bhqk', q, k)
        probs = jax.nn.softmax(scores, axis=-1)
        out = jnp.einsum('bhqk,bhkd->bhqd', probs, v)
        out = out.transpose(0, 2, 1, 3).reshape(B, S, HIDDEN)
        return jnp.einsum('bsd,ed->bse', out, w_out)

    def _L0_ffn_ref(x, router_w, router_b, w1, w3, w2):
        import jax, jax.numpy as jnp
        import numpy as np
        B, S, D, F, E, K = (4, 256, 128, 512, 4, 2)
        b, s, d = x.shape
        T = b * s
        e = router_w.shape[1]
        xf = x.reshape(T, d)
        logits = xf @ router_w + router_b
        probs = jax.nn.softmax(logits, axis=-1)
        top_p, top_i = jax.lax.top_k(probs, K)
        top_p = top_p / jnp.sum(top_p, axis=-1, keepdims=True)
        gates = jnp.zeros((T, e), xf.dtype).at[jnp.arange(T)[:, None], top_i].add(top_p)
        h = jax.nn.silu(jnp.einsum('td,edf->etf', xf, w1)) * jnp.einsum('td,edf->etf', xf, w3)
        expert_out = jnp.einsum('etf,efd->etd', h, w2)
        out = jnp.einsum('te,etd->td', gates, expert_out)
        return out.reshape(b, s, d)

    def _L1_xattn_ref(x, latents, mask, ln_x_w, ln_x_b, ln_l_w, ln_l_b, Wq, Wkv, q_scale, k_scale, Wo, ln_o_w, ln_o_b):
        import jax, jax.numpy as jnp
        import numpy as np
        DIM, DIM_HEAD, HEADS, SCALE = (128, 64, 8, 8.0)
        INNER = DIM_HEAD * HEADS
        LN_EPS = 1e-05
        L2_EPS = 1e-12

        def layer_norm(x, w, b):
            mu = jnp.mean(x, axis=-1, keepdims=True)
            var = jnp.mean(jnp.square(x - mu), axis=-1, keepdims=True)
            return (x - mu) * jax.lax.rsqrt(var + LN_EPS) * w + b

        def l2norm(t):
            n = jnp.sqrt(jnp.sum(jnp.square(t), axis=-1, keepdims=True))
            return t / jnp.maximum(n, L2_EPS)
        b, n, _ = x.shape
        m = latents.shape[1]
        x = layer_norm(x, ln_x_w, ln_x_b)
        latents = layer_norm(latents, ln_l_w, ln_l_b)
        q = latents @ Wq
        kv_input = jnp.concatenate([x, latents], axis=1)
        kv = kv_input @ Wkv
        k, v = jnp.split(kv, 2, axis=-1)

        def to_heads(t):
            return t.reshape(t.shape[0], t.shape[1], HEADS, DIM_HEAD).transpose(0, 2, 1, 3)
        q, k, v = map(to_heads, (q, k, v))
        q = l2norm(q) * q_scale
        k = l2norm(k) * k_scale
        sim = jnp.einsum('bhid,bhjd->bhij', q, k) * SCALE
        full_mask = jnp.concatenate([mask, jnp.ones((b, m), dtype=bool)], axis=1)[:, None, None, :]
        max_neg = -jnp.finfo(sim.dtype).max
        sim = jnp.where(full_mask, sim, max_neg)
        attn = jax.nn.softmax(sim.astype(jnp.float32), axis=-1).astype(sim.dtype)
        out = jnp.einsum('bhij,bhjd->bhid', attn, v)
        out = out.transpose(0, 2, 1, 3).reshape(b, m, INNER)
        return layer_norm(out @ Wo, ln_o_w, ln_o_b)

    def _L1_attn_ref(x_seq, W_decay, b_decay, W_input, b_input):
        import jax, jax.numpy as jnp
        import numpy as np
        D_MODEL = 128
        B, T = (8, 512)

        def _diag_scan(decays, injections):

            def combine(e1, e2):
                a1, b1 = e1
                a2, b2 = e2
                return (a1 * a2, a2 * b1 + b2)
            _, states = jax.lax.associative_scan(combine, (decays, injections), axis=1)
            return states
        decays = jax.nn.sigmoid(jnp.einsum('btd,ed->bte', x_seq, W_decay) + b_decay)
        injections = jnp.einsum('btd,ed->bte', x_seq, W_input) + b_input
        return _diag_scan(decays, injections)

    def _L1_ffn_ref(x, router_w, w1, b1, w2, b2):
        import jax, jax.numpy as jnp
        import numpy as np
        B, N, C, F, E, K = (2, 256, 128, 512, 8, 2)
        Bb, Nn, Cc = x.shape
        x_flat = x.reshape(-1, Cc)
        logits = jnp.einsum('tc,ec->te', x_flat, router_w)
        probs = jax.nn.softmax(logits, axis=-1)
        top_w, top_idx = jax.lax.top_k(probs, K)
        top_w = top_w / (jnp.sum(top_w, axis=-1, keepdims=True) + 1e-09)
        h = jnp.einsum('tc,efc->tef', x_flat, w1) + b1[None]
        h = jax.nn.relu(h)
        y = jnp.einsum('tef,ecf->tec', h, w2) + b2[None]
        sel = jnp.take_along_axis(y, top_idx[:, :, None], axis=1)
        out = jnp.einsum('tkc,tk->tc', sel, top_w)
        return out.reshape(Bb, Nn, Cc)

    def _L2_xattn_ref(query, key, Wq, Wk, Wv):
        import jax, jax.numpy as jnp
        import numpy as np
        HIDDEN = 128
        Q = jnp.einsum('bsd,ed->bse', query, Wq)
        K = jnp.einsum('bsd,ed->bse', key, Wk)
        V = jnp.einsum('bsd,ed->bse', key, Wv)
        alpha = jnp.einsum('bqd,bkd->bqk', Q, K)
        alpha = jax.nn.softmax(alpha, axis=2)
        out = jnp.einsum('bqk,bkd->bqd', alpha, V)
        return out

    def _L2_attn_ref(x, Wq, bq, Wk, bk, Wv, bv, Wo, bo):
        import jax, jax.numpy as jnp
        import numpy as np
        import math
        B, T, D, H = (4, 256, 128, 16)
        HD = D // H
        ROPE_BASE = 10000.0

        def apply_rope(x):
            t, hd = (x.shape[2], x.shape[3])
            half = hd // 2
            theta = 1.0 / ROPE_BASE ** (jnp.arange(0, hd, 2, dtype=jnp.float32) / hd)
            pos = jnp.arange(1, t + 1, dtype=jnp.float32)
            ang = pos[:, None] * theta[None, :]
            ang = jnp.concatenate([ang, ang], axis=-1)
            sin, cos = (jnp.sin(ang), jnp.cos(ang))
            rot = jnp.concatenate([-x[..., half:], x[..., :half]], axis=-1)
            return x * cos[None, None, :, :] + rot * sin[None, None, :, :]
        b, t, d = x.shape
        h, hd = (H, HD)
        q = x @ Wq.T + bq
        k = x @ Wk.T + bk
        v = x @ Wv.T + bv
        split = lambda z: z.reshape(b, t, h, hd).transpose(0, 2, 1, 3)
        q, k, v = (split(q), split(k), split(v))
        q = apply_rope(q)
        k = apply_rope(k)
        scale = math.sqrt(hd)
        att = jnp.einsum('bhqd,bhkd->bhqk', q, k) / scale
        mask = jnp.tril(jnp.ones((t, t), dtype=bool))
        att = jnp.where(mask[None, None, :, :], att, -jnp.inf)
        att = jax.nn.softmax(att, axis=-1)
        y = jnp.einsum('bhqk,bhkd->bhqd', att, v)
        y = y.transpose(0, 2, 1, 3).reshape(b, t, d)
        y = y @ Wo.T + bo
        return y

    def _L2_ffn_ref(hidden_states, gate_w, w1, b1, w2, b2):
        import jax, jax.numpy as jnp
        import numpy as np
        B, T, H = (8, 256, 128)
        F = 512
        E = 8
        TOP_K = 2
        b, t, h = hidden_states.shape
        seq_rep = hidden_states.mean(axis=1)
        router_logits = seq_rep @ gate_w
        probs = jax.nn.softmax(router_logits.astype(jnp.float32), axis=-1)
        top_w, top_i = jax.lax.top_k(probs, TOP_K)
        top_w = top_w / top_w.sum(axis=-1, keepdims=True)
        top_w = top_w.astype(hidden_states.dtype)
        combine = jnp.zeros((b, E), dtype=hidden_states.dtype)
        combine = combine.at[jnp.arange(b)[:, None], top_i].set(top_w)
        out = jnp.zeros_like(hidden_states)
        for e in range(E):
            hmid = jax.nn.gelu(jnp.einsum('bth,hf->btf', hidden_states, w1[e]) + b1[e], approximate=False)
            y = jnp.einsum('btf,fh->bth', hmid, w2[e]) + b2[e]
            out = out + combine[:, e][:, None, None] * y
        return out

    def _L3_xattn_ref(input_Q, input_K, input_V, attn_mask, flag, W_Q, W_K, W_V, W_O):
        import jax, jax.numpy as jnp
        import numpy as np
        B, S, D_MODEL, N_HEADS, D_K, D_V = (2, 256, 128, 16, 64, 64)
        b = input_Q.shape[0]
        Q = (input_Q @ W_Q).reshape(b, -1, N_HEADS, D_K).transpose(0, 2, 1, 3)
        K = (input_K @ W_K).reshape(b, -1, N_HEADS, D_K).transpose(0, 2, 1, 3)
        V = (input_V @ W_V).reshape(b, -1, N_HEADS, D_V).transpose(0, 2, 1, 3)
        scores = jnp.einsum('bhqd,bhkd->bhqk', Q, K) / np.sqrt(D_K).astype(np.float32)
        scores = jnp.where(attn_mask[:, None, :, :], jnp.float32(-1000000000.0), scores)
        attn = jax.nn.softmax(scores, axis=-1)
        context = jnp.einsum('bhqk,bhkd->bhqd', attn, V)
        context = context.transpose(0, 2, 1, 3).reshape(b, -1, N_HEADS * D_V)
        return context @ W_O

    def _L3_attn_ref(x, Wq, bq, Wk, bk, Wv, bv, Wo, bo):
        import math
        import jax, jax.numpy as jnp
        import numpy as np
        D_MODEL = 128
        NUM_HEADS = 16
        D_HEAD = D_MODEL // NUM_HEADS
        K_S = 32
        B, N = (2, 256)

        def _attn(x, Wq, bq, Wk, bk, Wv, bv, Wo, bo):
            b, n, _ = x.shape
            q = (x @ Wq.T + bq).reshape(b, n, NUM_HEADS, D_HEAD).transpose(0, 2, 1, 3)
            k = (x @ Wk.T + bk).reshape(b, n, NUM_HEADS, D_HEAD).transpose(0, 2, 1, 3)
            v = (x @ Wv.T + bv).reshape(b, n, NUM_HEADS, D_HEAD).transpose(0, 2, 1, 3)
            scores = jnp.einsum('bhqd,bhkd->bhqk', q, k) / math.sqrt(D_HEAD)
            causal = jnp.triu(jnp.ones((n, n), dtype=bool), k=1)
            neg_inf = jnp.array(-jnp.inf, dtype=scores.dtype)
            scores = jnp.where(causal, neg_inf, scores)
            vals, idx = jax.lax.top_k(scores, K_S)
            masked = jnp.full_like(scores, -jnp.inf)
            masked = jnp.put_along_axis(masked, idx, vals, axis=-1, inplace=False)
            attn = jax.nn.softmax(masked, axis=-1)
            out = jnp.einsum('bhqk,bhkd->bhqd', attn, v)
            out = out.transpose(0, 2, 1, 3).reshape(b, n, D_MODEL)
            y = out @ Wo.T + bo
            return (y, attn.mean(axis=1))

        def _reference_tuple_inner(x, Wq, bq, Wk, bk, Wv, bv, Wo, bo):
            return _attn(x, Wq, bq, Wk, bk, Wv, bv, Wo, bo)
        return _reference_tuple_inner(x, Wq, bq, Wk, bk, Wv, bv, Wo, bo)[0]

    def _L3_ffn_ref(x, kernel, bias, a, b):
        import jax, jax.numpy as jnp
        import numpy as np
        INT4_QMAX = 7.0

        def simulate_quantize_int4(w):
            scale = jnp.max(jnp.abs(w)) / INT4_QMAX
            q = jnp.clip(jnp.round(w / scale), -8.0, 7.0)
            return q * scale
        w = simulate_quantize_int4(kernel)
        y = jnp.einsum('bsd,df->bsf', x, w) + bias
        lora = jnp.einsum('bsr,rf->bsf', jnp.einsum('bsd,dr->bsr', x, a), b)
        return y + lora
    x = x + _L0_xattn_ref(_layernorm(x, axis=-1), ctx_1024, ctx_1024, L0_xattn_in_proj_weight, L0_xattn_in_proj_bias, L0_xattn_out_proj_weight, L0_xattn_out_proj_bias, L0_xattn_lambda_q1, L0_xattn_lambda_k1, L0_xattn_lambda_q2, L0_xattn_lambda_k2)
    x = x + _L0_attn_ref(_layernorm(x, axis=-1), L0_attn_w_qkv, L0_attn_w_out)
    x = x + _L0_ffn_ref(_layernorm(x, axis=-1), L0_ffn_router_w, L0_ffn_router_b, L0_ffn_w1, L0_ffn_w3, L0_ffn_w2)
    x = x + _L1_xattn_ref(ctx_1024, _layernorm(x, axis=-1), mask_BxS2_bk0, L1_xattn_ln_x_w, L1_xattn_ln_x_b, L1_xattn_ln_l_w, L1_xattn_ln_l_b, L1_xattn_Wq, L1_xattn_Wkv, L1_xattn_q_scale, L1_xattn_k_scale, L1_xattn_Wo, L1_xattn_ln_o_w, L1_xattn_ln_o_b)
    x = x + _L1_attn_ref(_layernorm(x, axis=-1), L1_attn_W_decay, L1_attn_b_decay, L1_attn_W_input, L1_attn_b_input)
    x = x + _L1_ffn_ref(_layernorm(x, axis=-1), L1_ffn_router_w, L1_ffn_w1, L1_ffn_b1, L1_ffn_w2, L1_ffn_b2)
    x = x + _L2_xattn_ref(_layernorm(x, axis=-1), ctx_1024, L2_xattn_Wq, L2_xattn_Wk, L2_xattn_Wv)
    x = x + _L2_attn_ref(_layernorm(x, axis=-1), L2_attn_Wq, L2_attn_bq, L2_attn_Wk, L2_attn_bk, L2_attn_Wv, L2_attn_bv, L2_attn_Wo, L2_attn_bo)
    x = x + _L2_ffn_ref(_layernorm(x, axis=-1), L2_ffn_gate_w, L2_ffn_w1, L2_ffn_b1, L2_ffn_w2, L2_ffn_b2)
    x = x + _L3_xattn_ref(_layernorm(x, axis=-1), ctx_1024, ctx_1024, mask_BxSxS2_bk1, 0, L3_xattn_W_Q, L3_xattn_W_K, L3_xattn_W_V, L3_xattn_W_O)
    x = x + _L3_attn_ref(_layernorm(x, axis=-1), L3_attn_Wq, L3_attn_bq, L3_attn_Wk, L3_attn_bk, L3_attn_Wv, L3_attn_bv, L3_attn_Wo, L3_attn_bo)
    x = x + _L3_ffn_ref(_layernorm(x, axis=-1), L3_ffn_kernel, L3_ffn_bias, L3_ffn_a, L3_ffn_b)
    return x

_drawn_inputs = setup_inputs


def setup_inputs(seed=0):
    import zlib

    import numpy as np

    out = dict(_drawn_inputs(seed))
    spreads = {'L0_xattn_in_proj_bias': (0.0, 0.1),
     'L0_xattn_out_proj_bias': (0.0, 0.1),
     'L0_ffn_router_b': (0.0, 0.8),
     'L1_xattn_ln_x_w': (1.0, 0.2),
     'L1_xattn_ln_x_b': (0.0, 0.1),
     'L1_xattn_ln_l_w': (1.0, 0.2),
     'L1_xattn_ln_l_b': (0.0, 0.1),
     'L1_xattn_q_scale': (1.0, 0.2),
     'L1_xattn_k_scale': (1.0, 0.2),
     'L1_xattn_ln_o_w': (1.0, 0.2),
     'L1_xattn_ln_o_b': (0.0, 0.1),
     'L1_attn_b_decay': (1.399999976158142, 0.2),
     'L1_ffn_b1': (0.0, 0.439),
     'L1_ffn_b2': (0.0, 0.411),
     'L3_attn_bq': (0.0, 0.8),
     'L3_attn_bk': (0.0, 2.0),
     'L3_attn_bv': (0.0, 0.339),
     'L3_attn_bo': (0.0, 0.306)}
    factors = {'L0_xattn_lambda_q1': 6.36,
     'L0_xattn_lambda_k1': 6.36,
     'L0_xattn_lambda_q2': 2.802,
     'L0_xattn_lambda_k2': 2.802,
     'L0_ffn_router_w': 7.462,
     'L0_ffn_w1': 6.563,
     'L0_ffn_w3': 7.506,
     'L0_ffn_w2': 5.403,
     'L2_attn_bq': 64.0,
     'L2_attn_bk': 64.0,
     'L2_attn_bv': 8.0,
     'L2_attn_bo': 25.486,
     'L2_ffn_b1': 8.0,
     'L2_ffn_b2': 8.0,
     'L3_ffn_a': 8.0,
     'L3_ffn_b': 8.0}
    for name, (base, spread) in spreads.items():
        noise = np.random.default_rng([zlib.crc32(name.encode()), seed]).standard_normal(out[name].shape)
        drawn = base * np.exp(spread * noise) if base else spread * noise
        out[name] = jnp.asarray(drawn.astype(out[name].dtype))
    for name, factor in factors.items():
        out[name] = (out[name] * factor).astype(out[name].dtype)
    return out
```

```python
import math
from contextlib import ExitStack

import numpy as np

import concourse.bass as bass
from concourse import mybir

F32 = mybir.dt.float32
U8 = mybir.dt.uint8
BF16 = mybir.dt.bfloat16
ACT = mybir.ActivationFunctionType
ALU = mybir.AluOpType
AX = mybir.AxisListType

P = 128
B, T, S = 16, 64, 1601
H, HD = 16, 8
NPAIR = B // 2
NT = 13
TAIL = S - 12 * P
F = 512
EPS = 1e-5
LAMBDA_INIT = 0.2
GONE = -1e30

CTX_TILES = [(P * j, P) for j in range(12)] + [(12 * P, TAIL)]
KV_TILES = CTX_TILES + [(S, T)]


def rotations():
    f = np.float32
    row = np.arange(P) % HD
    tok = np.arange(P) % T
    theta0 = np.power(f(10000.0), (f(2.0) * (row // 2).astype(f) / f(HD)).astype(f)).astype(f)
    ang0 = (tok.astype(f)[None, :] / theta0[:, None]).astype(f)
    sign0 = np.where(row % 2 == 0, -1, 1).astype(f)[:, None]
    half = HD // 2
    theta1 = (f(1.0) / np.power(f(10000.0), (2 * (row % half)).astype(f) / f(HD)).astype(f)).astype(f)
    ang1 = ((tok + 1).astype(f)[None, :] * theta1[:, None]).astype(f)
    sign1 = np.where(row < half, -1, 1).astype(f)[:, None]
    return (np.cos(ang0), np.sin(ang0) * sign0, np.cos(ang1), np.sin(ang1) * sign1)


def constants():
    f = np.float32
    row = np.arange(P)
    cos0, sin0, cos1, sin1 = rotations()
    head = (row[:, None] // HD == np.arange(H)[None, :]).astype(f)
    c = np.arange(2 * H)
    sub = (row[:, None] // (HD // 2) == (2 * (2 * (c // 4) + c % 2) + (c // 2) % 2)[None, :]).astype(f)
    t = row % T
    causal = np.where(np.arange(T)[None, :] <= t[:, None], 0.0, GONE).astype(f)
    same = (row[:, None] // T == row[None, :] // T).astype(f) / f(T)
    return {
        "ident": np.eye(P, dtype=f), "head_mask": head, "sub_mask": sub, "causal": causal,
        "free": np.zeros((P, T), f), "batch_mean": same, "neg_half": np.full((P, 16), -0.5, f),
        "cos0": cos0, "sin0": sin0, "cos1": cos1, "sin1": sin1,
    }


class Count:

    def __init__(self, sem):
        self.sem, self.base = sem, 0

    def at(self, n):
        return self.base + n

    def passed(self, n):
        self.base += n


class Chain:

    def __init__(self, engine, count):
        self.engine, self.count, self.n = engine, count, 0

    def __call__(self, ins):
        self.n += 1
        ins.then_inc(self.count.sem, 1)
        self.engine.wait_ge(self.count.sem, self.count.at(self.n))

    def end(self):
        self.count.passed(self.n)


class Machine:

    def __init__(self, nc, ctx, regions, names):
        self.nc, self.ctx = nc, ctx
        self.counts = {}
        self.regions = regions
        sb, ps = self.sbuf, self.psum
        self.weights = sb("weights", [P, max(a + n for a, n in regions.values())])
        self.x = sb("x_state", [P, P])
        self.xn = sb("x_normed", [P, P])
        self.xnT = sb("x_normed_T", [P, P])
        self.stat = sb("stat", [P, 16])
        self.small = sb("small", [P, 64])
        self.row8 = sb("row8", [P, 96])
        self.ctxN = [sb(f"ctx_rows{b}", [P, NT, P]) for b in range(2)]
        self.ctxT = [sb(f"ctx_cols{b}", [P, S]) for b in range(2)]
        self.arena = sb("arena", [P, ARENA])
        self.psS = ps("scores_banks", [P, 2048])
        self.psA = ps("bank_a", [P, 512])
        self.psB = ps("bank_b", [P, 512])
        self.psC = ps("bank_c", [P, 512])
        self.psD = ps("bank_d", [P, 512])

    def sbuf(self, name, shape, dt=F32):
        return self.ctx.enter_context(self.nc.sbuf_tensor(name, shape, dt))

    def psum(self, name, shape):
        return self.ctx.enter_context(self.nc.psum_tensor(name, shape, F32))

    def count(self, name):
        if name not in self.counts:
            self.counts[name] = Count(self.ctx.enter_context(self.nc.semaphore(name)))
        return self.counts[name]

    def w(self, name, rows=P):
        a, n = self.regions[name]
        return self.weights[0:rows, a:a + n]

    def at(self, start, n, rows=P):
        return self.arena[0:rows, start:start + n]


ARENA = 16768
EXPERTS0 = 10624
ONLY0 = 4 * (4 * 3 * P)


def layer_norm(nc, M):
    var, rstd, normed, turned = (M.count(n) for n in ("ln_var", "ln_rstd", "ln_normed", "ln_turned"))
    chain_c = M.count("ln_dve_chain")
    with nc.Block(no_gpsimd_drain=True) as block:
        @block.vector
        def _(dve):
            link = Chain(dve, chain_c)
            link(dve.bn_stats(M.stat[:, 0:6], M.x[:, :]))
            link(dve.bn_aggr(M.stat[:, 6:8], M.stat[:, 0:6]))
            dve.tensor_scalar(M.stat[:, 8:9], M.stat[:, 7:8], EPS, None, ALU.add).then_inc(var.sem, 1)
            dve.wait_ge(rstd.sem, rstd.at(1))
            dve.tensor_scalar(M.xn[:, :], M.x[:, :], M.stat[:, 6:7], M.stat[:, 9:10],
                              ALU.subtract, ALU.mult).then_inc(normed.sem, 1)
            link.end()

        @block.gpsimd
        def _(pool):
            pool.wait_ge(var.sem, var.at(1))
            pool.tensor_tensor(M.stat[:, 9:10], M.stat[:, 8:9], M.w("neg_half")[:, 0:1], ALU.pow).then_inc(rstd.sem, 1)

        @block.tensor
        def _(pe):
            pe.wait_ge(normed.sem, normed.at(1))
            pe.transpose(M.psA[:, 0:P], M.xn[:, :], M.w("ident")).then_inc(turned.sem, 1)

        @block.scalar
        def _(act):
            act.wait_ge(turned.sem, turned.at(1))
            act.activation(M.xnT[:, :], M.psA[:, 0:P], ACT.Copy)
    for c in (var, rstd, normed, turned):
        c.passed(1)


def attend(nc, M, *, units, rows, tiles, subs, queries, keys, values, bufs, pt, consume, bias=None, keep=None,
           scale=1.0, split=None):
    width = tiles[-1][0] + tiles[-1][1]
    chunks = [list(range(4 * c, 4 * c + 4)) for c in range(3)] + [[j] for j in range(12, len(tiles))]
    NC = len(chunks)
    masked = bias is not None
    scores, used, negmax, probs, weights, turned, moved, weighed, consumed, formed = (
        M.count(n) for n in ("at_scores", "at_scores_used", "at_negmax", "at_probs", "at_weights", "at_turned",
                             "at_moved", "at_weighed", "at_consumed", "at_queries_formed"))
    chain_c = M.count("at_dve_chain")
    banks = [M.psA, M.psB, M.psC]
    nb = len(bufs)
    small = M.small

    def buf(u, s):
        return bufs[(u + s) % nb][0:rows, 0:width]

    def col(kind, u, s):
        i = 16 * kind + 2 * (u % 4) + s
        return small[0:rows, i:i + 1]

    with nc.Block(no_gpsimd_drain=True) as block:
        @block.tensor
        def _(pe):
            def score(u, s):
                n = u * subs + s
                if n >= 1:
                    pe.wait_ge(used.sem, used.at(n))
                if split is not None and s == 0:
                    pe.wait_ge(formed.sem, formed.at(u + 1))
                for a in range(0, width, 512):
                    m = min(512, width - a)
                    mm = pe.matmul(M.psS[0:rows, a:a + m], queries(u, s), keys(u, a, m), start=True, stop=True)
                mm.then_inc(scores.sem, 1)

            def turn(u):
                pe.wait_ge(weights.sem, weights.at(u + 1))
                for c, js in enumerate(chunks):
                    g = u * NC + c
                    if g >= 3:
                        pe.wait_ge(moved.sem, moved.at(g - 2))
                    for i, j in enumerate(js):
                        a, m = tiles[j]
                        mm = pe.transpose(banks[g % 3][0:m, i * P:i * P + rows], buf(u, 0)[:, a:a + m],
                                          M.w("ident")[0:rows, 0:rows])
                    mm.then_inc(turned.sem, 1)

            def weigh(u):
                if u >= 1:
                    pe.wait_ge(consumed.sem, consumed.at(u))
                for c, js in enumerate(chunks):
                    pe.wait_ge(moved.sem, moved.at(u * NC + c + 1))
                    for j in js:
                        m = tiles[j][1]
                        mm = pe.matmul(M.psD[:, 0:rows], values(j), pt[0:m, j * P:j * P + rows],
                                       start=(j == 0), stop=(j == len(tiles) - 1))
                mm.then_inc(weighed.sem, 1)

            for u in range(units + 1):
                if u < units:
                    score(u, 0)
                if u >= 1:
                    turn(u - 1)
                if u < units and subs == 2:
                    score(u, 1)
                if u >= 1:
                    weigh(u - 1)

        @block.scalar
        def _(act):
            for u in range(units + 1):
                if u >= 1:
                    for c, js in enumerate(chunks):
                        g = (u - 1) * NC + c
                        m = tiles[js[0]][1]
                        act.wait_ge(turned.sem, turned.at(g + 1))
                        if u >= 2 and c == 0:
                            act.wait_ge(weighed.sem, weighed.at(u - 1))
                        src = banks[g % 3][0:m, 0:len(js) * P].rearrange("p (j r) -> p j r", r=P)[:, :, 0:rows]
                        dst = pt[0:m, js[0] * P:(js[-1] + 1) * P].rearrange("p (j r) -> p j r", r=P)[:, :, 0:rows]
                        act.activation(dst, src, ACT.Copy).then_inc(moved.sem, 1)
                if u < units:
                    for s in range(subs):
                        n = u * subs + s
                        act.wait_ge(negmax.sem, negmax.at(n + 1))
                        if subs == 2 and s == 0 and u >= 1:
                            act.wait_ge(weights.sem, weights.at(u))
                        if not masked and (subs == 1 or s == 1) and u >= 2:
                            act.wait_ge(turned.sem, turned.at(NC * (u - 1)))
                        src = buf(u, s) if masked else M.psS[0:rows, 0:width]
                        ex = act.activation(buf(u, s), src, ACT.Exp, bias=col(0, u, s), scale=scale,
                                            accum_out=col(1, u, s))
                        if not masked:
                            ex.then_inc(used.sem, 1)
                        else:
                            ex.then_inc(probs.sem, 1)

        @block.vector
        def _(dve):
            link = Chain(dve, chain_c)

            def maximum(u, s):
                dve.wait_ge(scores.sem, scores.at(u * subs + s + 1))
                if not masked:
                    dve.tensor_reduce(col(0, u, s), M.psS[0:rows, 0:width], AX.X, ALU.max,
                                      negate=True).then_inc(negmax.sem, 1)
                    return
                if u >= 2:
                    dve.wait_ge(turned.sem, turned.at(NC * (u - 1)))
                if keep is not None:
                    link(dve.tensor_tensor(buf(u, s), M.psS[0:rows, 0:width], keep, ALU.mult))
                    used_here = dve.tensor_tensor_reduce(buf(u, s), buf(u, s), bias, 1.0, -3e38, ALU.add, ALU.max,
                                                         col(2, u, s))
                else:
                    used_here = dve.tensor_tensor_reduce(buf(u, s), M.psS[0:rows, 0:width], bias, 1.0, -3e38,
                                                         ALU.add, ALU.max, col(2, u, s))
                used_here.then_inc(used.sem, 1)
                dve.wait_ge(used.sem, used.at(u + 1))
                dve.tensor_scalar(col(0, u, s), col(2, u, s), -scale, None, ALU.mult).then_inc(negmax.sem, 1)

            def weight(u):
                done = used if not masked else probs
                dve.wait_ge(done.sem, done.at(subs * (u + 1)))
                for s in range(subs):
                    link(dve.reciprocal(col(1, u, s), col(1, u, s)))
                if subs == 1:
                    dve.tensor_scalar(buf(u, 0), buf(u, 0), col(1, u, 0), None, ALU.mult).then_inc(weights.sem, 1)
                else:
                    link(dve.tensor_scalar(col(1, u, 0), col(1, u, 0), 1.0 - LAMBDA_INIT, None, ALU.mult))
                    link(dve.tensor_scalar(col(1, u, 1), col(1, u, 1), split, None, ALU.mult))
                    link(dve.tensor_scalar(buf(u, 1), buf(u, 1), col(1, u, 1), None, ALU.mult))
                    dve.scalar_tensor_tensor(buf(u, 0), buf(u, 0), col(1, u, 0), buf(u, 1), ALU.mult,
                                             ALU.add).then_inc(weights.sem, 1)

            for u in range(units + 1):
                if u < units:
                    for s in range(subs):
                        maximum(u, s)
                    weight(u)
                if u >= 1:
                    dve.wait_ge(weighed.sem, weighed.at(u))
                    consume(dve, link, u - 1).then_inc(consumed.sem, 1)
            link.end()

        if split is not None:
            @block.gpsimd
            def _(pool):
                for u in range(units):
                    if u >= 2:
                        pool.wait_ge(scores.sem, scores.at(2 * (u - 1)))
                    src, mask, dst = split_operands(M, u)
                    pool.tensor_tensor(dst, src, mask, ALU.mult).then_inc(formed.sem, 1)
    scores.passed(units * subs)
    used.passed(units * subs)
    negmax.passed(units * subs)
    if masked:
        probs.passed(units * subs)
    weights.passed(units)
    turned.passed(units * NC)
    moved.passed(units * NC)
    weighed.passed(units)
    consumed.passed(units)
    if split is not None:
        formed.passed(units)


A0_BUF = [0, S, 2 * S]
A0_PT = 3 * S
A0_KT = A0_PT + NT * P
A0_V = A0_KT + S
A0_QT = A0_V + NT * P
A0_QB = A0_QT + P
A0_ATT = A0_QB + 512
assert A0_ATT + 128 <= EXPERTS0


def split_operands(M, u):
    b, p = M.batch, u
    src = M.at(A0_QT, P)[:, b * T:(b + 1) * T].unsqueeze(1).broadcast_to((P, 4, T))
    mask = M.w("sub_mask")[:, 4 * p:4 * p + 4].unsqueeze(2).broadcast_to((P, 4, T))
    dst = M.at(A0_QB + 256 * (u % 2), 256).rearrange("p (c t) -> p c t", t=T)
    return src, mask, dst


def project_out(nc, M, name, terms, bias=None):
    done = M.count("out_projected")
    chain_c = M.count("out_dve_chain")
    with nc.Block(no_gpsimd_drain=True) as block:
        @block.tensor
        def _(pe):
            for i, (lhs, rhs) in enumerate(terms):
                mm = pe.matmul(M.psA[:, 0:P], lhs, rhs, start=(i == 0), stop=(i == len(terms) - 1))
            mm.then_inc(done.sem, 1)

        @block.vector
        def _(dve):
            link = Chain(dve, chain_c)
            if bias is not None:
                link(dve.tensor_tensor(M.x[:, :], M.x[:, :], bias, ALU.add))
            dve.wait_ge(done.sem, done.at(1))
            dve.tensor_tensor(M.x[:, :], M.x[:, :], M.psA[:, 0:P], ALU.add)
            link.end()
    done.passed(1)


def cross0(nc, M):
    q_done, k_done, v_done = (M.count(n) for n in ("x0_q", "x0_k", "x0_v"))
    qT, kT, V, att = M.at(A0_QT, P), M.at(A0_KT, S), M.at(A0_V, NT * P), M.at(A0_ATT, P)
    for b in range(2):
        M.batch = b
        with nc.Block(no_gpsimd_drain=True) as block:
            @block.tensor
            def _(pe):
                if b == 0:
                    pe.matmul(M.psD[:, 0:P], M.w("x0_wq"), M.xnT[:, :], start=True, stop=True).then_inc(q_done.sem, 1)
                for a in range(0, S, 512):
                    m = min(512, S - a)
                    mm = pe.matmul(M.psS[:, a:a + m], M.w("x0_wk"), M.ctxT[b][:, a:a + m], start=True, stop=True)
                mm.then_inc(k_done.sem, 1)
                for c, bank in enumerate([M.psA, M.psB, M.psC]):
                    for j in range(4 * c, 4 * c + 4):
                        mm = pe.matmul(bank[:, (j % 4) * P:(j % 4 + 1) * P], M.ctxT[b][:, j * P:(j + 1) * P],
                                       M.w("x0_wv"), start=True, stop=True)
                    mm.then_inc(v_done.sem, 1)
                if b == 0:
                    pe.wait_ge(q_done.sem, q_done.at(2))
                pe.matmul(M.psD[0:TAIL, P:2 * P], M.ctxT[b][:, 12 * P:S], M.w("x0_wv"), start=True,
                          stop=True).then_inc(v_done.sem, 1)

            @block.scalar
            def _(act):
                act.wait_ge(k_done.sem, k_done.at(1))
                act.activation(kT, M.psS[:, 0:S], ACT.Identity, bias=M.w("x0_bk"))

            @block.vector
            def _(dve):
                if b == 0:
                    dve.wait_ge(q_done.sem, q_done.at(1))
                    dve.tensor_scalar(qT, M.psD[:, 0:P], M.w("x0_bq"), 0.5, ALU.add, ALU.mult).then_inc(q_done.sem, 1)
                for c, bank in enumerate([M.psA, M.psB, M.psC]):
                    dve.wait_ge(v_done.sem, v_done.at(c + 1))
                    dve.tensor_tensor(V[:, 512 * c:512 * (c + 1)].rearrange("p (j d) -> p j d", d=P),
                                      bank[:, :].rearrange("p (j d) -> p j d", d=P),
                                      M.w("x0_bv").unsqueeze(1).broadcast_to((P, 4, P)), ALU.add)
                dve.wait_ge(v_done.sem, v_done.at(4))
                dve.tensor_tensor(V[0:TAIL, 12 * P:NT * P], M.psD[0:TAIL, P:2 * P], M.w("x0_bv", TAIL), ALU.add)
        if b == 0:
            q_done.passed(2)
        k_done.passed(1)
        v_done.passed(4)

        def gather(dve, link, u):
            out = att[:, b * T:(b + 1) * T]
            for h in range(2):
                mask = M.w("head_mask")[:, 2 * u + h:2 * u + h + 1]
                src = M.psD[:, h * T:(h + 1) * T]
                if u == 0 and h == 0:
                    ins = dve.tensor_scalar(out, src, mask, None, ALU.mult)
                else:
                    ins = dve.scalar_tensor_tensor(out, src, mask, out, ALU.mult, ALU.add)
                if h == 0:
                    link(ins)
            return ins

        attend(nc, M, units=8, rows=P, tiles=CTX_TILES, subs=2,
               queries=lambda u, s: M.at(A0_QB + 256 * (u % 2) + P * s, P),
               keys=lambda u, a, m: kT[:, a:a + m],
               values=lambda j: V[0:CTX_TILES[j][1], j * P:(j + 1) * P],
               bufs=[M.at(a, S) for a in A0_BUF], pt=M.at(A0_PT, 1664), consume=gather,
               split=M.lam[:, 0:1])
    project_out(nc, M, "x0", [(att, M.w("x0_wo"))], M.w("x0_bo"))


SA_Q, SA_K, SA_T1, SA_T2 = 0, 128, 256, 384
SA_QB, SA_V, SA_S, SA_W, SA_PT, SA_ATT = 512, 2560, 2816, 3840, 4864, 6912
SA_M = 7040
assert SA_M + 16 <= EXPERTS0


def self_attention(nc, M, n, *, rope=None, biased, causal, scale, top=None):
    proj, formed, queries, scored, packed, expd, weights, turned, moved, weighed, gathered, vals = (
        M.count("sa_" + k) for k in ("projected", "qk_formed", "queries", "scored", "packed", "exponentials",
                                     "weights", "turned", "moved", "weighed", "gathered", "values"))
    chain_c = M.count("sa_dve_chain")
    pre = n + "_"
    q, k, t1, t2 = (M.at(a, P) for a in (SA_Q, SA_K, SA_T1, SA_T2))
    qb = M.at(SA_QB, H * P).rearrange("p (h t) -> p h t", t=P)
    v = M.at(SA_V, 2 * P, T)
    s = M.at(SA_S, H * T).rearrange("p (h s) -> p h s", s=T)
    w = M.at(SA_W, H * T).rearrange("p (h s) -> p h s", s=T)
    pt = M.at(SA_PT, H * P, T).rearrange("p (h t) -> p h t", t=P)
    att = M.at(SA_ATT, P)
    mx = M.at(SA_M, H)
    ps = M.psS[:, :].rearrange("p (h s) -> p h s", s=P)
    mask = M.w("head_mask")
    with nc.Block(no_gpsimd_drain=True) as block:
        @block.tensor
        def _(pe):
            names = ["wq", "wk"] + (["wq_turned", "wk_turned"] if rope else [])
            for i, name in enumerate(names):
                mm = pe.matmul(M.psA[:, i * P:(i + 1) * P], M.w(pre + name), M.xnT[:, :], start=True, stop=True)
            mm.then_inc(proj.sem, 1)
            for b in range(2):
                mm = pe.matmul(M.psB[0:T, b * P:(b + 1) * P], M.xnT[:, b * T:(b + 1) * T], M.w(pre + "wv"),
                               start=True, stop=True)
            mm.then_inc(vals.sem, 1)
            pe.wait_ge(formed.sem, formed.at(1))
            for g in range(2):
                pe.wait_ge(queries.sem, queries.at(g + 1))
                for h in range(8 * g, 8 * g + 8):
                    mm = pe.matmul(ps[:, h, :], qb[:, h, :], k, start=True, stop=True)
            mm.then_inc(scored.sem, 1)
            pe.wait_ge(weights.sem, weights.at(1))
            banks = [M.psA, M.psC, M.psB, M.psD]
            for c in range(4):
                for i in range(4):
                    mm = pe.transpose(banks[c][0:T, i * P:(i + 1) * P], s[:, 4 * c + i, :], M.w("ident"))
                mm.then_inc(turned.sem, 1)
            pe.wait_ge(moved.sem, moved.at(4))
            for b in range(2):
                for g in range(2):
                    mm = pe.matmul(M.psS[:, 512 * (2 * b + g):512 * (2 * b + g + 1)], v[:, b * P:(b + 1) * P],
                                   pt[:, 8 * g:8 * g + 8, b * T:(b + 1) * T], start=True, stop=True)
                mm.then_inc(weighed.sem, 1)

        @block.scalar
        def _(act):
            act.wait_ge(packed.sem, packed.at(1))
            act.activation(s, s, ACT.Exp).then_inc(expd.sem, 1)
            banks = [M.psA, M.psC, M.psB, M.psD]
            for c in range(4):
                act.wait_ge(turned.sem, turned.at(c + 1))
                act.activation(pt[:, 4 * c:4 * c + 4, :], banks[c][0:T, :].rearrange("p (h t) -> p h t", t=P),
                               ACT.Copy).then_inc(moved.sem, 1)

        @block.gpsimd
        def _(pool):
            pool.wait_ge(formed.sem, formed.at(2))
            for g in range(2):
                hs = slice(8 * g, 8 * g + 8)
                pool.tensor_tensor(qb[:, hs, :], q.unsqueeze(1).broadcast_to((P, 8, P)),
                                   mask[:, hs].unsqueeze(2).broadcast_to((P, 8, P)), ALU.mult).then_inc(queries.sem, 1)

        @block.vector
        def _(dve):
            link = Chain(dve, chain_c)
            dve.wait_ge(proj.sem, proj.at(1))
            for i, (dst, bias) in ((1, (k, "bk")), (0, (q, "bq"))):
                src = M.psA[:, i * P:(i + 1) * P]
                if rope:
                    cos, sin = M.w("cos" + rope), M.w("sin" + rope)
                    other = M.psA[:, (2 + i) * P:(3 + i) * P]
                    if biased:
                        link(dve.scalar_tensor_tensor(t1, src, M.w(pre + bias), cos, ALU.add, ALU.mult))
                        link(dve.scalar_tensor_tensor(t2, other, M.w(pre + bias + "_turned"), sin, ALU.add, ALU.mult))
                    else:
                        link(dve.tensor_tensor(t1, src, cos, ALU.mult))
                        link(dve.tensor_tensor(t2, other, sin, ALU.mult))
                    if i == 1 or scale == 1.0:
                        dve.tensor_tensor(dst, t1, t2, ALU.add).then_inc(formed.sem, 1)
                        dve.wait_ge(formed.sem, formed.at(2 - i))
                    else:
                        link(dve.tensor_tensor(t1, t1, t2, ALU.add))
                        dve.tensor_scalar(dst, t1, scale, None, ALU.mult).then_inc(formed.sem, 1)
                else:
                    dve.tensor_scalar(dst, src, M.w(pre + bias), 1.0 if i else scale, ALU.add,
                                      ALU.mult).then_inc(formed.sem, 1)
            dve.wait_ge(vals.sem, vals.at(1))
            for b in range(2):
                src, dst = M.psB[0:T, b * P:(b + 1) * P], v[:, b * P:(b + 1) * P]
                if biased:
                    link(dve.tensor_tensor(dst, src, M.w(pre + "bv", T), ALU.add))
                else:
                    link(dve.tensor_copy(dst, src))
            dve.wait_ge(scored.sem, scored.at(1))
            seen = M.w("causal" if causal else "free")
            for b in range(2):
                r = slice(b * T, (b + 1) * T)
                link(dve.tensor_tensor(s[r], ps[r, :, r], seen[r].unsqueeze(1).broadcast_to((T, H, T)), ALU.add))
            link(dve.tensor_reduce(mx, s, AX.X, ALU.max))
            if top:
                src = s
                for _ in range(top // 8):
                    for h in range(H):
                        ins = dve.max(M.row8[:, 0:8] if h % 2 else M.row8[:, 8:16], src[:, h, :])
                        link(ins)
                        link(dve.match_replace(w[:, h, :], M.row8[:, 0:8] if h % 2 else M.row8[:, 8:16],
                                               src[:, h, :], -3e38))
                    src = w
                link(dve.tensor_tensor(w, w, s, ALU.not_equal))
            dve.tensor_tensor(s, s, mx.unsqueeze(2).broadcast_to((P, H, T)), ALU.subtract).then_inc(packed.sem, 1)
            dve.wait_ge(expd.sem, expd.at(1))
            if top:
                link(dve.tensor_tensor(s, s, w, ALU.mult))
            link(dve.tensor_reduce(mx, s, AX.X, ALU.add))
            link(dve.reciprocal(mx, mx))
            dve.tensor_tensor(s, s, mx.unsqueeze(2).broadcast_to((P, H, T)), ALU.mult).then_inc(weights.sem, 1)
            for b in range(2):
                dve.wait_ge(weighed.sem, weighed.at(b + 1))
                out = M.psS[:, 1024 * b:1024 * (b + 1)].rearrange("p (h t) -> p h t", t=T)
                link(dve.tensor_tensor(w, out, mask.unsqueeze(2).broadcast_to((P, H, T)), ALU.mult))
                link(dve.tensor_reduce(att[:, b * T:(b + 1) * T], w.rearrange("p h t -> p t h"), AX.X, ALU.add))
            link.end()
    for c in (proj, scored, packed, expd, weights, vals):
        c.passed(1)
    formed.passed(2)
    queries.passed(2)
    turned.passed(4)
    moved.passed(4)
    weighed.passed(2)
    project_out(nc, M, n, [(att, M.w(pre + "wo"))], M.w(pre + "bo") if biased else None)


MO_H, MO_G, MO_GT, MO_MEAN = 0, 2048, 2176, 2304


def experts(nc, M, n, *, E, kind, up, up3, down, router, router_bias=None, b1=None, b2=None, floor=0.0, by_batch=False):
    pre = n + "_"
    logits, shifted, soft, gated, gT_ps, gT_sb, up_done, acted, prod, down_done, added, mean = (
        M.count("mo_" + k) for k in ("logits", "shifted", "softmax", "gates", "gates_turned", "gates_moved", "up",
                                     "activated", "product", "down", "added", "mean"))
    chain_c = M.count("mo_dve_chain")
    R = M.row8
    lg, top8, e16, rep, sel, g = (R[:, a:a + n_] for a, n_ in ((0, 8), (8, 8), (16, 16), (32, 16), (48, 8), (56, 8)))
    sc = R[:, 64:72]
    hT = [M.at(MO_H + 512 * i, 512) for i in range(4)]
    gT = M.at(MO_GT, P, 8)
    meanT = M.at(MO_MEAN, P)
    two = kind == "silu"
    with nc.Block(no_gpsimd_drain=True) as block:
        @block.tensor
        def _(pe):
            xr = M.xnT[:, :]
            if by_batch:
                pe.matmul(M.psB[:, 0:P], M.xn[:, :], M.w("batch_mean"), start=True, stop=True).then_inc(mean.sem, 1)
                pe.wait_ge(mean.sem, mean.at(2))
                xr = meanT
            pe.matmul(M.psA[:, 0:E], xr, router, start=True, stop=True).then_inc(logits.sem, 1)

            def raise_(e):
                if two:
                    if e >= 2:
                        pe.wait_ge(prod.sem, prod.at(e - 1))
                elif e >= 4:
                    pe.wait_ge(acted.sem, acted.at(e - 3))
                for w_, off in ((up, 0), (up3, 1))[:2 if two else 1]:
                    a = 512 * (2 * (e % 2) + off if two else e % 4)
                    for c in range(4):
                        mm = pe.matmul(M.psS[:, a + P * c:a + P * (c + 1)], w_(e, c), M.xnT[:, :], start=True,
                                       stop=True)
                mm.then_inc(up_done.sem, 1)

            raise_(0)
            for e in range(E):
                if e + 1 < E:
                    raise_(e + 1)
                ready = prod if two else acted
                pe.wait_ge(ready.sem, ready.at(e + 1))
                if e >= 2:
                    pe.wait_ge(added.sem, added.at(e - 1))
                bank = [M.psB, M.psC][e % 2]
                if by_batch and e == 0:
                    pe.wait_ge(mean.sem, mean.at(2))
                for c in range(4):
                    mm = pe.matmul(bank[:, 0:P], hT[e % 4][:, P * c:P * (c + 1)], down(e, c), start=(c == 0),
                                   stop=(c == 3))
                mm.then_inc(down_done.sem, 1)
            if b2 is not None:
                pe.wait_ge(gated.sem, gated.at(1))
                pe.transpose(M.psA[0:8, 128:256], g, M.w("ident")).then_inc(gT_ps.sem, 1)
                pe.wait_ge(gT_sb.sem, gT_sb.at(1))
                pe.matmul(M.psD[:, 0:P], gT, b2, start=True, stop=True).then_inc(gT_ps.sem, 1)

        @block.scalar
        def _(act):
            act.wait_ge(shifted.sem, shifted.at(1))
            act.activation(e16[:, 0:8], lg, ACT.Exp, bias=sc[:, 0:1], accum_out=sc[:, 1:2]).then_inc(soft.sem, 1)
            for e in range(E):
                act.wait_ge(up_done.sem, up_done.at(e + 1))
                if e >= 4:
                    act.wait_ge(down_done.sem, down_done.at(e - 3))
                if two:
                    act.activation(hT[e % 4], M.psS[:, 1024 * (e % 2):1024 * (e % 2) + 512],
                                   ACT.Silu).then_inc(acted.sem, 1)
                else:
                    for c in range(4):
                        fn = ACT.Relu if kind == "relu" else ACT.Gelu
                        ins = act.activation(hT[e % 4][:, P * c:P * (c + 1)],
                                             M.psS[:, 512 * (e % 4) + P * c:512 * (e % 4) + P * (c + 1)], fn,
                                             bias=b1[:, 4 * e + c:4 * e + c + 1])
                    ins.then_inc(acted.sem, 1)

        @block.vector
        def _(dve):
            link = Chain(dve, chain_c)
            link(dve.memset(lg, GONE))
            link(dve.memset(e16, -1.0))
            if by_batch:
                dve.wait_ge(mean.sem, mean.at(1))
                dve.tensor_copy(meanT, M.psB[:, 0:P]).then_inc(mean.sem, 1)
            dve.wait_ge(logits.sem, logits.at(1))
            if router_bias is not None:
                link(dve.tensor_tensor(lg[:, 0:E], M.psA[:, 0:E], router_bias, ALU.add))
            else:
                link(dve.tensor_copy(lg[:, 0:E], M.psA[:, 0:E]))
            dve.tensor_reduce(sc[:, 0:1], lg, AX.X, ALU.max, negate=True).then_inc(shifted.sem, 1)
            dve.wait_ge(soft.sem, soft.at(1))
            link(dve.reciprocal(sc[:, 2:3], sc[:, 1:2]))
            link(dve.tensor_scalar(e16[:, 0:8], e16[:, 0:8], sc[:, 2:3], None, ALU.mult))
            link(dve.max(top8, e16[:, 0:8]))
            link(dve.tensor_scalar(sc[:, 3:4], top8[:, 0:1], top8[:, 1:2], floor, ALU.add, ALU.add))
            link(dve.memset(top8[:, 2:8], -1.0))
            link(dve.match_replace(rep, top8, e16, -2.0))
            link(dve.tensor_tensor(sel, rep[:, 0:8], e16[:, 0:8], ALU.not_equal))
            link(dve.tensor_tensor(sel, sel, e16[:, 0:8], ALU.mult))
            link(dve.reciprocal(sc[:, 4:5], sc[:, 3:4]))
            dve.tensor_scalar(g, sel, sc[:, 4:5], None, ALU.mult).then_inc(gated.sem, 1)
            dve.wait_ge(gated.sem, gated.at(1))

            def add(e):
                dve.wait_ge(down_done.sem, down_done.at(e + 1))
                if e >= 1:
                    dve.wait_ge(added.sem, added.at(e))
                dve.scalar_tensor_tensor(M.x[:, :], [M.psB, M.psC][e % 2][:, 0:P], g[:, e:e + 1], M.x[:, :], ALU.mult,
                                         ALU.add).then_inc(added.sem, 1)

            for e in range(E):
                if two:
                    dve.wait_ge(acted.sem, acted.at(e + 1))
                    a = 1024 * (e % 2) + 512
                    dve.tensor_tensor(hT[e % 4], hT[e % 4], M.psS[:, a:a + 512], ALU.mult).then_inc(prod.sem, 1)
                if e >= 1:
                    add(e - 1)
            add(E - 1)
            if b2 is not None:
                dve.wait_ge(gT_ps.sem, gT_ps.at(1))
                dve.tensor_copy(gT, M.psA[0:8, 128:256]).then_inc(gT_sb.sem, 1)
                dve.wait_ge(gT_ps.sem, gT_ps.at(2))
                dve.wait_ge(added.sem, added.at(E))
                dve.tensor_tensor(M.x[:, :], M.x[:, :], M.psD[:, 0:P], ALU.add)
            link.end()
    for c in (logits, shifted, soft, gated):
        c.passed(1)
    for c in (up_done, acted, down_done, added):
        c.passed(E)
    if two:
        prod.passed(E)
    if by_batch:
        mean.passed(2)
    if b2 is not None:
        gT_ps.passed(2)
        gT_sb.passed(1)


WIDE = S + T
A1_BUF = [0, 1792]
A1_PT, A1_ROWS, A1_KT = 3584, 5376, 7168
A1_T, A1_K, A1_LAT, A1_LATT = 0, 512, 1536, 1664
A1_Q, A1_QT, A1_SQ = 1792, 2304, 3584
A1_QB = A1_KT + 4 * WIDE
A1_MASK = A1_QB + 1024
A1_UT = A1_MASK + (WIDE + 1) // 2
A1_SEEN = 2816
assert A1_UT + 8 * P <= ARENA, A1_UT + 8 * P


def cross1(nc, M, batch_seen):
    chain_c = M.count("x1_dve_chain")
    rows = M.at(A1_ROWS, 14 * P).rearrange("p (j d) -> p j d", d=P)
    kT = M.at(A1_KT, 4 * WIDE).rearrange("p (c s) -> p c s", s=WIDE)
    qb = M.at(A1_QB, 1024).rearrange("p (b c t) -> p b c t", b=2, c=4)
    lat, latT = M.at(A1_LAT, P), M.at(A1_LATT, P)
    q, qT, sq = M.at(A1_Q, 512), M.at(A1_QT, 512), M.at(A1_SQ, 512)
    mask = M.at(A1_MASK, (WIDE + 1) // 2).bitcast(BF16)[:, 0:WIDE]
    seen = M.at(A1_SEEN, (S + 3) // 4).bitcast(U8)[:, 0:S]
    UT = M.at(A1_UT, 8 * P).rearrange("p (h t) -> p h t", t=P)
    st = M.small
    var, rstd, normed, turned, moved, projected, norm2, rnorm, scaled, q_turned = (
        M.count("x1_" + k) for k in ("var", "rstd", "lat_normed", "lat_turned", "lat_moved", "q_projected",
                                     "q_norm2", "q_rnorm", "q_scaled", "q_turned"))
    with nc.Block(no_gpsimd_drain=True) as block:
        @block.vector
        def _(dve):
            link = Chain(dve, chain_c)
            link(dve.bn_stats(M.stat[:, 0:6], M.xn[:, :]))
            link(dve.bn_aggr(M.stat[:, 6:8], M.stat[:, 0:6]))
            dve.tensor_scalar(M.stat[:, 8:9], M.stat[:, 7:8], EPS, None, ALU.add).then_inc(var.sem, 1)
            link(dve.memset(qb, 0.0))
            dve.wait_ge(rstd.sem, rstd.at(1))
            link(dve.tensor_scalar(lat, M.xn[:, :], M.stat[:, 6:7], M.stat[:, 9:10], ALU.subtract, ALU.mult))
            link(dve.tensor_tensor(lat, lat, M.w("x1_lat_w"), ALU.mult))
            dve.tensor_tensor(lat, lat, M.w("x1_lat_b"), ALU.add).then_inc(normed.sem, 1)
            dve.wait_ge(projected.sem, projected.at(1))
            link(dve.tensor_copy(q, M.psS[:, 0:512]))
            link(dve.tensor_tensor(sq, q, q, ALU.mult))
            link(dve.tensor_reduce(st[:, 0:8], sq.rearrange("p (h d) -> p h d", d=64), AX.X, ALU.add))
            dve.tensor_scalar(st[:, 0:8], st[:, 0:8], 1e-24, None, ALU.max).then_inc(norm2.sem, 1)
            dve.wait_ge(rnorm.sem, rnorm.at(1))
            q3 = q.rearrange("p (h d) -> p h d", d=64)
            link(dve.tensor_tensor(q3, q3, st[:, 8:16].unsqueeze(2).broadcast_to((P, 8, 64)), ALU.mult))
            for name in ("x1_q_scale", "x1_k_scale"):
                link(dve.tensor_tensor(q3, q3, M.w(name).unsqueeze(1).broadcast_to((P, 8, 64)), ALU.mult))
            dve.tensor_scalar(q, q, 8.0, None, ALU.mult).then_inc(scaled.sem, 1)
            dve.wait_ge(q_turned.sem, q_turned.at(1))
            for h in range(2):
                r = slice(64 * h, 64 * (h + 1))
                for b in range(2):
                    src = M.psS[r, 1024:1536].rearrange("p (c t) -> p c t", t=P)[:, :, b * T:(b + 1) * T]
                    link(dve.tensor_copy(qb[r, b, :, 64 * h:64 * (h + 1)], src))
            link.end()

        @block.gpsimd
        def _(pool):
            pool.wait_ge(var.sem, var.at(1))
            pool.tensor_tensor(M.stat[:, 9:10], M.stat[:, 8:9], M.w("neg_half")[:, 0:1], ALU.pow).then_inc(rstd.sem, 1)
            pool.wait_ge(norm2.sem, norm2.at(1))
            pool.tensor_tensor(st[:, 8:16], st[:, 0:8], M.w("neg_half")[:, 0:8], ALU.pow).then_inc(rnorm.sem, 1)

        @block.tensor
        def _(pe):
            pe.wait_ge(normed.sem, normed.at(1))
            pe.transpose(M.psA[:, 0:P], lat, M.w("ident")).then_inc(turned.sem, 1)
            pe.wait_ge(moved.sem, moved.at(1))
            pe.matmul(M.psS[:, 0:512], latT, M.w("x1_wq"), start=True, stop=True).then_inc(projected.sem, 1)
            pe.wait_ge(scaled.sem, scaled.at(1))
            for c in range(4):
                mm = pe.transpose(M.psS[:, 1024 + P * c:1024 + P * (c + 1)], q[:, P * c:P * (c + 1)], M.w("ident"))
            mm.then_inc(q_turned.sem, 1)

        @block.scalar
        def _(act):
            act.wait_ge(turned.sem, turned.at(1))
            act.activation(latT, M.psA[:, 0:P], ACT.Copy).then_inc(moved.sem, 1)
    for c in (var, rstd, normed, turned, moved, projected, norm2, rnorm, scaled, q_turned):
        c.passed(1)

    cvar, crstd, crows, ct, cm, ck, csq, cn2, crn, ckn, ckt, ckm = (
        M.count("x1k_" + k) for k in ("var", "rstd", "rows", "turned", "moved", "projected", "squared", "norm2",
                                      "rnorm", "normed", "keys_turned", "keys_moved"))
    cseen = M.count("x1k_seen_loaded")
    for b in range(2):
        ctx3 = M.ctxN[b][:, :, :]
        bs = slice(b * T, (b + 1) * T)
        pair = [M.at(A1_T, P), M.at(A1_T + P, P)]
        kn = [M.at(A1_K, 512), M.at(A1_K + 512, 512)]
        with nc.Block(no_gpsimd_drain=True) as block:
            @block.sync
            def _(sp):
                sp.dma_start(seen, batch_seen(b).broadcast_to((P, S))).then_inc(cseen.sem, 16)

            @block.vector
            def _(dve):
                link = Chain(dve, chain_c)
                for j in range(NT):
                    link(dve.bn_stats(M.row8[:, 0:6], ctx3[:, j, :]))
                    link(dve.bn_aggr(st[:, 2 * j:2 * j + 2], M.row8[:, 0:6]))
                stv = st[:, 0:26].rearrange("p (j k) -> p k j", k=2)
                dve.tensor_scalar(st[:, 32:45], stv[:, 1, :], EPS, None, ALU.add).then_inc(cvar.sem, 1)
                dve.wait_ge(cseen.sem, cseen.at(16))
                link(dve.tensor_scalar(mask[:, 0:S], seen, -GONE, GONE, ALU.mult, ALU.add))
                link(dve.memset(mask[:, S:WIDE], 0.0))
                link(dve.tensor_copy(rows[0:T, 13, :], lat[bs, :]))
                dve.wait_ge(crstd.sem, crstd.at(1))
                r3 = rows[:, 0:NT, :]
                link(dve.tensor_tensor(r3, ctx3, stv[:, 0, :].unsqueeze(2).broadcast_to((P, NT, P)), ALU.subtract))
                link(dve.tensor_tensor(r3, r3, st[:, 48:61].unsqueeze(2).broadcast_to((P, NT, P)), ALU.mult))
                link(dve.tensor_tensor(r3, r3, M.w("x1_ctx_w").unsqueeze(1).broadcast_to((P, NT, P)), ALU.mult))
                link(dve.tensor_tensor(r3, r3, M.w("x1_ctx_b").unsqueeze(1).broadcast_to((P, NT, P)), ALU.add))
                link.end()

            @block.gpsimd
            def _(pool):
                pool.wait_ge(cvar.sem, cvar.at(1))
                pool.tensor_tensor(st[:, 48:61], st[:, 32:45], M.w("neg_half")[:, 0:13], ALU.pow).then_inc(crstd.sem, 1)
        cvar.passed(1)
        cseen.passed(16)
        crstd.passed(1)
        with nc.Block(no_gpsimd_drain=True) as block:
            NK = len(KV_TILES)
            sqb = [M.at(A1_SQ, 512), M.at(A1_SQ + 512, 512)]

            @block.tensor
            def _(pe):
                for j in range(NK + 1):
                    if j < NK:
                        m = KV_TILES[j][1]
                        if j >= 1:
                            pe.wait_ge(cm.sem, cm.at(j))
                        pe.transpose(M.psA[:, 0:m], rows[0:m, j, :], M.w("ident")[0:m, 0:m]).then_inc(ct.sem, 1)
                    if j >= 1:
                        a, m = KV_TILES[j - 1]
                        pe.wait_ge(ckn.sem, ckn.at(j))
                        if j >= 3:
                            pe.wait_ge(ckm.sem, ckm.at(j - 2))
                        for c in range(4):
                            mm = pe.transpose(M.psS[:, 512 * (j % 2) + P * c:512 * (j % 2) + P * c + m],
                                              kn[(j - 1) % 2][0:m, P * c:P * (c + 1)], M.w("ident")[0:m, 0:m])
                        mm.then_inc(ckt.sem, 1)
                    if j < NK:
                        m = KV_TILES[j][1]
                        pe.wait_ge(cm.sem, cm.at(j + 1))
                        if j >= 2:
                            pe.wait_ge(ckn.sem, ckn.at(j - 1))
                        pe.matmul([M.psB, M.psC][j % 2][0:m, :], pair[j % 2][:, 0:m], M.w("x1_wk"), start=True,
                                  stop=True).then_inc(ck.sem, 1)

            @block.scalar
            def _(act):
                for j in range(NK + 1):
                    if j < NK:
                        m = KV_TILES[j][1]
                        act.wait_ge(ct.sem, ct.at(j + 1))
                        if j >= 2:
                            act.wait_ge(ck.sem, ck.at(j - 1))
                        act.activation(pair[j % 2][:, 0:m], M.psA[:, 0:m], ACT.Copy).then_inc(cm.sem, 1)
                        act.wait_ge(ck.sem, ck.at(j + 1))
                        if j >= 2:
                            act.wait_ge(cn2.sem, cn2.at(j - 1))
                        act.activation(sqb[j % 2][0:m, :], [M.psB, M.psC][j % 2][0:m, :],
                                       ACT.Square).then_inc(csq.sem, 1)
                    if j >= 1:
                        a, m = KV_TILES[j - 1]
                        act.wait_ge(ckt.sem, ckt.at(j))
                        src = M.psS[:, 512 * (j % 2):512 * (j % 2) + 512].rearrange("p (c s) -> p c s", s=P)
                        act.activation(kT[:, :, a:a + m], src[:, :, 0:m], ACT.Copy).then_inc(ckm.sem, 1)

            @block.gpsimd
            def _(pool):
                for j in range(NK):
                    m = KV_TILES[j][1]
                    s_ = 16 * (j % 2)
                    pool.wait_ge(cn2.sem, cn2.at(j + 1))
                    if j >= 2:
                        pool.wait_ge(ckn.sem, ckn.at(j - 1))
                    pool.tensor_tensor(st[0:m, s_ + 8:s_ + 16], st[0:m, s_:s_ + 8], M.w("neg_half")[0:m, 0:8],
                                       ALU.pow).then_inc(crn.sem, 1)

            @block.vector
            def _(dve):
                link = Chain(dve, chain_c)
                for j in range(NK):
                    m = KV_TILES[j][1]
                    s_ = 16 * (j % 2)
                    dve.wait_ge(csq.sem, csq.at(j + 1))
                    if j >= 2:
                        dve.wait_ge(crn.sem, crn.at(j - 1))
                    link(dve.tensor_reduce(st[0:m, s_:s_ + 8], sqb[j % 2][0:m, :].rearrange("p (h d) -> p h d", d=64),
                                           AX.X, ALU.add))
                    dve.tensor_scalar(st[0:m, s_:s_ + 8], st[0:m, s_:s_ + 8], 1e-24, None, ALU.max).then_inc(cn2.sem, 1)
                    dve.wait_ge(crn.sem, crn.at(j + 1))
                    if j >= 2:
                        dve.wait_ge(ckt.sem, ckt.at(j - 1))
                    dve.tensor_tensor(kn[j % 2][0:m, :].rearrange("p (h d) -> p h d", d=64),
                                      [M.psB, M.psC][j % 2][0:m, :].rearrange("p (h d) -> p h d", d=64),
                                      st[0:m, s_ + 8:s_ + 16].unsqueeze(2).broadcast_to((m, 8, 64)),
                                      ALU.mult).then_inc(ckn.sem, 1)
                link.end()
        for c in (ct, cm, ck, csq, cn2, crn, ckn, ckt, ckm):
            c.passed(NK)

        def keep_rows(dve, link, u):
            return dve.tensor_copy(UT[:, 2 * u:2 * u + 2, bs], M.psD[:, 0:P].rearrange("p (h t) -> p h t", t=T))

        if b == 0:
            keep = M.count("x1_lat_kept")
            with nc.Block(no_gpsimd_drain=True) as block:
                @block.vector
                def _(dve):
                    dve.tensor_copy(M.xn[:, :], lat).then_inc(keep.sem, 1)
            keep.passed(1)
            lat = M.xn[:, :]
        attend(nc, M, units=4, rows=P, tiles=KV_TILES, subs=1,
               queries=lambda u, s: qb[:, b, u, :],
               keys=lambda u, a, m: kT[:, u, a:a + m],
               values=lambda j: rows[0:KV_TILES[j][1], j, :],
               bufs=[M.at(a, 1792) for a in A1_BUF], pt=M.at(A1_PT, 14 * P), consume=keep_rows, bias=mask)

    done, var, rstd = (M.count("x1o_" + k) for k in ("projected", "var", "rstd"))
    y = M.at(A1_LAT, P)
    with nc.Block(no_gpsimd_drain=True) as block:
        @block.tensor
        def _(pe):
            for h in range(8):
                mm = pe.matmul(M.psA[:, 0:P], UT[:, h, :], M.w("x1_vo")[:, P * h:P * (h + 1)], start=(h == 0),
                               stop=(h == 7))
            mm.then_inc(done.sem, 1)

        @block.vector
        def _(dve):
            link = Chain(dve, chain_c)
            dve.wait_ge(done.sem, done.at(1))
            link(dve.bn_stats(M.stat[:, 0:6], M.psA[:, 0:P]))
            link(dve.bn_aggr(M.stat[:, 6:8], M.stat[:, 0:6]))
            dve.tensor_scalar(M.stat[:, 8:9], M.stat[:, 7:8], EPS, None, ALU.add).then_inc(var.sem, 1)
            dve.wait_ge(rstd.sem, rstd.at(1))
            link(dve.tensor_scalar(y, M.psA[:, 0:P], M.stat[:, 6:7], M.stat[:, 9:10], ALU.subtract, ALU.mult))
            link(dve.tensor_tensor(y, y, M.w("x1_out_w"), ALU.mult))
            link(dve.tensor_tensor(y, y, M.w("x1_out_b"), ALU.add))
            link(dve.tensor_tensor(M.x[:, :], M.x[:, :], y, ALU.add))
            link.end()

        @block.gpsimd
        def _(pool):
            pool.wait_ge(var.sem, var.at(1))
            pool.tensor_tensor(M.stat[:, 9:10], M.stat[:, 8:9], M.w("neg_half")[:, 0:1], ALU.pow).then_inc(rstd.sem, 1)
    for c in (done, var, rstd):
        c.passed(1)


def recurrence(nc, M):
    proj, shifted, expd, scanned, turned = (
        M.count("rc_" + k) for k in ("projected", "shifted", "exponential", "scanned", "turned"))
    chain_c = M.count("rc_dve_chain")
    z, inj, out = M.at(0, P), M.at(P, P), M.at(2 * P, P)
    with nc.Block(no_gpsimd_drain=True) as block:
        @block.tensor
        def _(pe):
            pe.matmul(M.psA[:, 0:P], M.w("rc_wd"), M.xnT[:, :], start=True, stop=True)
            pe.matmul(M.psA[:, P:2 * P], M.w("rc_wi"), M.xnT[:, :], start=True, stop=True).then_inc(proj.sem, 1)
            pe.wait_ge(scanned.sem, scanned.at(1))
            pe.transpose(M.psB[:, 0:P], out, M.w("ident")).then_inc(turned.sem, 1)

        @block.scalar
        def _(act):
            act.wait_ge(shifted.sem, shifted.at(1))
            act.activation(z, z, ACT.Exp, scale=-1.0).then_inc(expd.sem, 1)

        @block.vector
        def _(dve):
            link = Chain(dve, chain_c)
            dve.wait_ge(proj.sem, proj.at(1))
            dve.tensor_scalar(z, M.psA[:, 0:P], M.w("rc_bd"), None, ALU.add).then_inc(shifted.sem, 1)
            link(dve.tensor_scalar(inj, M.psA[:, P:2 * P], M.w("rc_bi"), None, ALU.add))
            dve.wait_ge(expd.sem, expd.at(1))
            link(dve.tensor_scalar(z, z, 1.0, None, ALU.add))
            link(dve.reciprocal(z, z))
            link(dve.tensor_tensor_scan(out[:, 0:T], z[:, 0:T], inj[:, 0:T], 0.0, ALU.mult, ALU.add))
            dve.tensor_tensor_scan(out[:, T:P], z[:, T:P], inj[:, T:P], 0.0, ALU.mult, ALU.add).then_inc(scanned.sem, 1)
            dve.wait_ge(turned.sem, turned.at(1))
            dve.tensor_tensor(M.x[:, :], M.x[:, :], M.psB[:, 0:P], ALU.add)
            link.end()
    for c in (proj, shifted, expd, scanned, turned):
        c.passed(1)


A3_BUF = [0, 1664]
A3_PT, A3_Q, A3_UT, A3_KEEP, A3_BIAS, A3_MASKED = 3328, 4992, 7040, 9088, 10752, 12416


def fold_queries(nc, M, weights, heads, qp):
    done = M.count("fold_queries")
    with nc.Block(no_gpsimd_drain=True) as block:
        @block.tensor
        def _(pe):
            for h in range(heads):
                mm = pe.matmul(M.psS[:, h * P:(h + 1) * P], weights[:, h * P:(h + 1) * P], M.xnT[:, :],
                               start=True, stop=True)
            mm.then_inc(done.sem, 1)

        @block.scalar
        def _(act):
            act.wait_ge(done.sem, done.at(1))
            act.activation(qp.rearrange("p (b h t) -> p h b t", b=2, t=T),
                           M.psS[:, 0:heads * P].rearrange("p (h b t) -> p h b t", b=2, t=T), ACT.Copy)
    done.passed(1)


def cross2(nc, M):
    qp, UT = M.at(A3_Q, P), M.at(A3_UT, P)
    fold_queries(nc, M, M.w("x2_qk"), 1, qp)
    for b in range(2):
        bs = slice(b * T, (b + 1) * T)
        attend(nc, M, units=1, rows=T, tiles=CTX_TILES, subs=1,
               queries=lambda u, s: qp[:, bs], keys=lambda u, a, m: M.ctxT[b][:, a:a + m],
               values=lambda j: M.ctxN[b][0:CTX_TILES[j][1], j, :],
               bufs=[M.at(a, 1664) for a in A3_BUF], pt=M.at(A3_PT, 1664),
               consume=lambda dve, link, u: dve.tensor_copy(UT[:, bs], M.psD[:, 0:T]))
    project_out(nc, M, "x2", [(UT, M.w("x2_wv"))])


def cross3(nc, M, batch_masked):
    qp = M.at(A3_Q, H * P)
    UT = M.at(A3_UT, H * P).rearrange("p (h t) -> p h t", t=P)
    keep, gone = M.at(A3_KEEP, S), M.at(A3_BIAS, S)
    masked = M.at(A3_MASKED, (S + 3) // 4).bitcast(U8)[:, 0:S]
    loaded = M.count("x3_mask_loaded")
    fold_queries(nc, M, M.w("x3_qk"), H, qp)
    for b in range(2):
        bs = slice(b * T, (b + 1) * T)
        with nc.Block(no_gpsimd_drain=True) as block:
            @block.sync
            def _(sp):
                for h in range(2):
                    sp.dma_start(masked[h * T:(h + 1) * T], batch_masked(b)).then_inc(loaded.sem, 16)

            @block.vector
            def _(dve):
                dve.wait_ge(loaded.sem, loaded.at(32))
                dve.tensor_scalar(keep, masked, -1.0, 1.0, ALU.mult, ALU.add)
                dve.tensor_scalar(gone, masked, -8e9, None, ALU.mult)

        loaded.passed(32)

        def keep_rows(dve, link, u):
            return dve.tensor_copy(UT[:, 2 * u:2 * u + 2, bs], M.psD[:, 0:P].rearrange("p (h t) -> p h t", t=T))

        attend(nc, M, units=8, rows=P, tiles=CTX_TILES, subs=1,
               queries=lambda u, s: qp[:, (b * H + 2 * u) * T:(b * H + 2 * u + 2) * T], keys=lambda u, a, m: M.ctxT[b][:, a:a + m],
               values=lambda j: M.ctxN[b][0:CTX_TILES[j][1], j, :],
               bufs=[M.at(a, 1664) for a in A3_BUF], pt=M.at(A3_PT, 1664), consume=keep_rows,
               bias=gone, keep=keep, scale=0.125)
    vo = M.w("x3_vo")
    project_out(nc, M, "x3", [(UT[:, h, :], vo[:, P * h:P * (h + 1)]) for h in range(H)])


def quantised(nc, M):
    low, low_moved, done = (M.count("qf_" + k) for k in ("low_rank", "low_rank_moved", "done"))
    chain_c = M.count("qf_dve_chain")
    xa = M.at(0, P, 16)
    with nc.Block(no_gpsimd_drain=True) as block:
        @block.tensor
        def _(pe):
            pe.matmul(M.psB[0:16, 0:P], M.w("qf_a"), M.xnT[:, :], start=True, stop=True).then_inc(low.sem, 1)
            pe.matmul(M.psA[:, 0:P], M.xnT[:, :], M.w("qf_w"), start=True, stop=False)
            pe.wait_ge(low_moved.sem, low_moved.at(1))
            pe.matmul(M.psA[:, 0:P], xa, M.w("qf_b", 16), start=False, stop=True).then_inc(done.sem, 1)

        @block.vector
        def _(dve):
            link = Chain(dve, chain_c)
            link(dve.tensor_tensor(M.x[:, :], M.x[:, :], M.w("qf_bias"), ALU.add))
            dve.wait_ge(low.sem, low.at(1))
            dve.tensor_copy(xa, M.psB[0:16, 0:P]).then_inc(low_moved.sem, 1)
            dve.wait_ge(done.sem, done.at(1))
            dve.tensor_tensor(M.x[:, :], M.x[:, :], M.psA[:, 0:P], ALU.add)
            link.end()
    for c in (low, low_moved, done):
        c.passed(1)


def prepare(nc, M, blob, folds):
    loaded, folded, moved, exps, absmax, allmax, half = (
        M.count("pr_" + k) for k in ("loaded", "folded", "moved", "exponentials", "absmax", "allmax", "dots"))
    chain_c = M.count("pr_dve_chain")
    n_blob = blob.shape[1]
    cols = folds.shape[1]
    fold = M.at(0, cols)
    q3, k3, v3, o3, v1, o1 = (fold[0:64, a:b] for a, b in (
        (0, 2048), (2048, 4096), (4096, 6144), (6144, 8192), (8192, 9216), (9216, 10240)))
    jobs = [(q3, k3, M.w("x3_qk"), H), (v3, o3, M.w("x3_vo"), H), (v1, o1, M.w("x1_vo"), 8)]
    with nc.Block(no_gpsimd_drain=True) as block:
        @block.sync
        def _(sp):
            sp.dma_start(fold, folds).then_inc(loaded.sem, 16)
            sp.dma_start(M.weights[:, 0:n_blob], blob).then_inc(loaded.sem, 16)

        @block.tensor
        def _(pe):
            pe.wait_ge(loaded.sem, loaded.at(32))
            for i, (lhs, rhs, _, heads) in enumerate(jobs):
                if i:
                    pe.wait_ge(moved.sem, moved.at(i))
                for h in range(heads):
                    c = slice(h * P, (h + 1) * P)
                    mm = pe.matmul(M.psS[:, c], lhs[:, c], rhs[:, c], start=True, stop=True)
                mm.then_inc(folded.sem, 1)
            pe.matmul(M.psA[:, 0:P], fold[:, 10240:10240 + P], fold[:, 10240 + P:10240 + 2 * P], start=True,
                      stop=True).then_inc(folded.sem, 1)

        @block.scalar
        def _(act):
            for i, (_, _, dst, heads) in enumerate(jobs):
                act.wait_ge(folded.sem, folded.at(i + 1))
                act.activation(dst, M.psS[:, 0:heads * P], ACT.Copy).then_inc(moved.sem, 1)
            act.wait_ge(folded.sem, folded.at(4))
            act.activation(M.w("x2_qk"), M.psA[:, 0:P], ACT.Copy)
            act.wait_ge(half.sem, half.at(1))
            act.activation(M.small[:, 2:4], M.small[:, 0:2], ACT.Exp).then_inc(exps.sem, 1)

        @block.gpsimd
        def _(pool):
            pool.wait_ge(absmax.sem, absmax.at(1))
            pool.partition_all_reduce(M.small[:, 9:10], M.small[:, 8:9], P, bass.bass_isa.ReduceOp.max).then_inc(allmax.sem, 1)

        @block.vector
        def _(dve):
            link = Chain(dve, chain_c)
            for b in range(2):
                link(dve.memset(M.ctxN[b][:, NT - 1, :], 0.0))
            dve.wait_ge(loaded.sem, loaded.at(32))
            lam = M.w("x0_lambda").rearrange("p (a b d) -> p a b d", a=2, b=2)
            link(dve.tensor_tensor(M.small[:, 16:24].rearrange("p (a d) -> p a d", a=2), lam[:, :, 0, :],
                                   lam[:, :, 1, :], ALU.mult))
            dve.tensor_reduce(M.small[:, 0:2], M.small[:, 16:24].rearrange("p (a d) -> p a d", a=2), AX.X,
                              ALU.add).then_inc(half.sem, 1)
            dve.wait_ge(exps.sem, exps.at(1))
            link(dve.tensor_tensor(M.small[:, 4:5], M.small[:, 3:4], M.small[:, 2:3], ALU.subtract))
            link(dve.tensor_scalar(M.lam[:, :], M.small[:, 4:5], LAMBDA_INIT, 1.0 - LAMBDA_INIT, ALU.subtract, ALU.mult))
            w = M.w("qf_w")
            dve.tensor_reduce(M.small[:, 8:9], w, AX.X, ALU.max, apply_absolute_value=True).then_inc(absmax.sem, 1)
            dve.wait_ge(allmax.sem, allmax.at(1))
            link(dve.tensor_scalar(M.small[:, 10:11], M.small[:, 9:10], 1.0 / 7.0, None, ALU.mult))
            link(dve.reciprocal(M.small[:, 11:12], M.small[:, 10:11]))
            half_ulp = 1.5 * 2.0 ** 23
            link(dve.tensor_scalar(w, w, M.small[:, 11:12], half_ulp, ALU.mult, ALU.add))
            link(dve.tensor_scalar(w, w, half_ulp, 7.0, ALU.subtract, ALU.min))
            link(dve.tensor_scalar(w, w, -8.0, M.small[:, 10:11], ALU.max, ALU.mult))
            link.end()
    loaded.passed(32)
    folded.passed(4)
    moved.passed(3)
    for c in (exps, absmax, allmax, half):
        c.passed(1)


def load_pair(nc, M, i, A):
    loaded = M.count("pair_loaded")
    with nc.Block(no_gpsimd_drain=True) as block:
        @block.sync
        def _(sp):
            sp.dma_start(M.x[:, :], A["x"][bass.ds(i, 1)].rearrange("o t d -> (o t) d")).then_inc(loaded.sem, 16)
            for b in range(2):
                sp.dma_start(M.ctxT[b][:, :], A["ctxT"][bass.ds(2 * i + b, 1)].rearrange("o d s -> (o d) s")).then_inc(loaded.sem, 16)
            sp.dma_start(M.at(EXPERTS0, ONLY0), A["experts0"]).then_inc(loaded.sem, 16)
            for b in range(2):
                ctx = A["ctx"][bass.ds(2 * i + b, 1)].rearrange("o s d -> (o s) d")
                sp.dma_start(M.ctxN[b][:, 0:12, :], ctx[0:12 * P].rearrange("(j p) d -> p j d", p=P)).then_inc(loaded.sem, 16)
                sp.dma_start(M.ctxN[b][0:TAIL, 12, :], ctx[12 * P:S]).then_inc(loaded.sem, 16)
            sp.wait_ge(loaded.sem, loaded.at(16 * 8))
    loaded.passed(16 * 8)


def store_pair(nc, M, i, out):
    stored = M.count("pair_stored")
    with nc.Block(no_gpsimd_drain=True) as block:
        @block.sync
        def _(sp):
            sp.dma_start(out[bass.ds(i, 1)].rearrange("o t d -> (o t) d"), M.x[:, :]).then_inc(stored.sem, 16)
            sp.wait_ge(stored.sem, stored.at(16))
    stored.passed(16)


def restart(nc, M):
    for c in M.counts.values():
        nc.gpsimd.sem_clear(c.sem)
        c.base = 0
    nc.all_engine_barrier(sem_only=True)


def program(nc, A, regions, out, upto=12):
    with ExitStack() as ctx:
        M = Machine(nc, ctx, regions, None)
        M.lam = M.sbuf("lambda_share", [P, 1])
        prepare(nc, M, A["weights"], A["folds"])
        restart(nc, M)

        def wide(name):
            return lambda e, c: M.w(name)[:, 512 * e + P * c:512 * e + P * (c + 1)]

        def first(k):
            return lambda e, c: M.at(EXPERTS0 + 2048 * k + 512 * e + P * c, P)

        layers = [
            lambda i: cross0(nc, M),
            lambda i: self_attention(nc, M, "a0", rope="0", biased=False, causal=False, scale=1.0),
            lambda i: experts(nc, M, "m0", E=4, kind="silu", up=first(0), up3=first(1), down=first(2),
                            router=M.w("m0_router"), router_bias=M.w("m0_router_b")),
            lambda i: cross1(nc, M, lambda b: A["seen"][bass.ds(2 * i + b, 1)]),
            lambda i: recurrence(nc, M),
            lambda i: experts(nc, M, "m1", E=8, kind="relu", up=wide("m1_up"), up3=None, down=wide("m1_down"),
                            router=M.w("m1_router"), b1=M.w("m1_b1"), b2=M.w("m1_b2", 8), floor=1e-9),
            lambda i: cross2(nc, M),
            lambda i: self_attention(nc, M, "a2", rope="1", biased=True, causal=True, scale=1.0 / math.sqrt(HD)),
            lambda i: experts(nc, M, "m2", E=8, kind="gelu", up=wide("m2_up"), up3=None, down=wide("m2_down"),
                            router=M.w("m2_router"), b1=M.w("m2_b1"), b2=M.w("m2_b2", 8), by_batch=True),
            lambda i: cross3(nc, M, lambda b: A["masked"][bass.ds(2 * i + b, 1)].rearrange("o t s -> (o t) s")),
            lambda i: self_attention(nc, M, "a3", biased=True, causal=True, scale=1.0 / math.sqrt(HD), top=32),
            lambda i: quantised(nc, M),
        ]
        with nc.Fori(0, A["x"].shape[0]) as i:
            load_pair(nc, M, i, A)
            for n, layer in enumerate(layers[:upto]):
                layer_norm(nc, M)
                layer(i)
            store_pair(nc, M, i, out)
            restart(nc, M)


def layout(w):
    import numpy as np
    T_ = lambda a: np.ascontiguousarray(np.asarray(a).T)
    row = lambda a, p=P: np.broadcast_to(np.asarray(a)[None, :], (p, np.asarray(a).shape[0]))
    col = lambda a: np.asarray(a)[:, None]
    idx = np.arange(P)
    swap0 = (idx // HD) * HD + (idx % HD ^ 1)
    swap1 = (idx // HD) * HD + (idx % HD + HD // 2) % HD
    qkv0 = np.asarray(w["L0_attn_w_qkv"]).reshape(H, 3, HD, P)
    wq0, wk0, wv0 = (qkv0[:, j].reshape(P, P) for j in range(3))
    ip, ib = np.asarray(w["L0_xattn_in_proj_weight"]), np.asarray(w["L0_xattn_in_proj_bias"])
    up = lambda a: np.asarray(a).transpose(1, 0, 2).reshape(P, -1)
    down = lambda a: np.asarray(a).reshape(-1, 4, P, P).transpose(2, 0, 1, 3).reshape(P, -1)
    b1 = lambda a: np.asarray(a).reshape(8, 4, P).transpose(2, 0, 1).reshape(P, 32)
    head_t = lambda a, h: np.asarray(a).reshape(P, h, 64).transpose(2, 1, 0).reshape(64, -1)
    head_r = lambda a, h: np.asarray(a).reshape(h, 64, P).transpose(1, 0, 2).reshape(64, -1)
    wkv = np.asarray(w["L1_xattn_Wkv"])
    blocks = dict(constants())
    blocks.update({
        "x0_wq": T_(ip[0:P]), "x0_wk": T_(ip[P:2 * P]), "x0_wv": T_(ip[2 * P:]), "x0_wo": T_(w["L0_xattn_out_proj_weight"]),
        "x0_bq": col(ib[0:P]), "x0_bk": col(ib[P:2 * P]), "x0_bv": row(ib[2 * P:]),
        "x0_bo": row(w["L0_xattn_out_proj_bias"]),
        "x0_lambda": np.concatenate([row(w["L0_xattn_lambda_" + k]) for k in ("q1", "k1", "q2", "k2")], axis=1),
        "a0_wq": T_(wq0), "a0_wk": T_(wk0), "a0_wv": T_(wv0), "a0_wq_turned": T_(wq0[swap0]),
        "a0_wk_turned": T_(wk0[swap0]), "a0_wo": T_(w["L0_attn_w_out"]),
        "m0_router": w["L0_ffn_router_w"], "m0_router_b": row(w["L0_ffn_router_b"]),
        "x1_ctx_w": row(w["L1_xattn_ln_x_w"]), "x1_ctx_b": row(w["L1_xattn_ln_x_b"]),
        "x1_lat_w": row(w["L1_xattn_ln_l_w"]), "x1_lat_b": row(w["L1_xattn_ln_l_b"]),
        "x1_wq": w["L1_xattn_Wq"], "x1_wk": wkv[:, 0:512],
        "x1_q_scale": row(w["L1_xattn_q_scale"]), "x1_k_scale": row(w["L1_xattn_k_scale"]),
        "x1_out_w": row(w["L1_xattn_ln_o_w"]), "x1_out_b": row(w["L1_xattn_ln_o_b"]),
        "rc_wd": T_(w["L1_attn_W_decay"]), "rc_wi": T_(w["L1_attn_W_input"]),
        "rc_bd": col(w["L1_attn_b_decay"]), "rc_bi": col(w["L1_attn_b_input"]),
        "m1_router": T_(w["L1_ffn_router_w"]), "m1_up": up(np.asarray(w["L1_ffn_w1"]).transpose(0, 2, 1)),
        "m1_down": down(np.asarray(w["L1_ffn_w2"]).transpose(0, 2, 1)), "m1_b1": b1(w["L1_ffn_b1"]),
        "m1_b2": w["L1_ffn_b2"],
        "x2_wv": T_(w["L2_xattn_Wv"]),
        "m2_router": w["L2_ffn_gate_w"], "m2_up": up(w["L2_ffn_w1"]), "m2_down": down(w["L2_ffn_w2"]),
        "m2_b1": b1(w["L2_ffn_b1"]), "m2_b2": w["L2_ffn_b2"],
        "qf_w": w["L3_ffn_kernel"], "qf_a": w["L3_ffn_a"], "qf_b": w["L3_ffn_b"], "qf_bias": row(w["L3_ffn_bias"]),
    })
    for n, L in (("a2", "L2_attn_"), ("a3", "L3_attn_")):
        blocks.update({n + "_w" + k: T_(w[L + "W" + k]) for k in "qkvo"})
        blocks.update({n + "_b" + k: col(w[L + "b" + k]) for k in "qk"})
        blocks.update({n + "_b" + k: row(w[L + "b" + k]) for k in "vo"})
    for k in "qk":
        blocks["a2_w" + k + "_turned"] = T_(np.asarray(w["L2_attn_W" + k])[swap1])
        blocks["a2_b" + k + "_turned"] = col(np.asarray(w["L2_attn_b" + k])[swap1])
    regions, a = {}, 0
    for name, block in blocks.items():
        regions[name] = (a, np.asarray(block).shape[1])
        a += np.asarray(block).shape[1]
    blob = np.zeros((P, a), np.float32)
    for name, block in blocks.items():
        block = np.asarray(block)
        s, n = regions[name]
        blob[0:block.shape[0], s:s + n] = block
    for name, n in (("x3_qk", H * P), ("x3_vo", H * P), ("x1_vo", 8 * P), ("x2_qk", P)):
        regions[name] = (a, n)
        a += n
    narrow = np.concatenate([head_t(w["L3_xattn_W_Q"], H), head_t(w["L3_xattn_W_K"], H), head_t(w["L3_xattn_W_V"], H),
                             head_r(w["L3_xattn_W_O"], H), head_t(wkv[:, 512:], 8), head_r(w["L1_xattn_Wo"], 8)], axis=1)
    folds = np.zeros((P, narrow.shape[1] + 2 * P), np.float32)
    folds[0:64, 0:narrow.shape[1]] = narrow
    folds[:, narrow.shape[1]:] = np.concatenate([w["L2_xattn_Wq"], w["L2_xattn_Wk"]], axis=1)
    experts0 = np.concatenate([up(w["L0_ffn_w1"]), up(w["L0_ffn_w3"]), down(w["L0_ffn_w2"])], axis=1)
    return regions, blob, folds, experts0


UPTO = 12


def kernel(**inputs):
    import numpy as np
    import concourse.bacc as bacc
    from concourse import mybir
    from concourse.bass_utils import run_bass_kernel_spmd

    w = {k: np.asarray(v) for k, v in inputs.items()}
    regions, blob, folds, experts0 = layout(w)
    ctx = w["ctx_1024"]
    n = w["x"].shape[0] // 2
    arrays = {
        "x": np.ascontiguousarray(w["x"].reshape(n, P, P)),
        "ctx": ctx, "ctxT": np.ascontiguousarray(ctx.transpose(0, 2, 1)),
        "seen": w["mask_BxS2_bk0"], "masked": w["mask_BxSxS2_bk1"],
        "weights": blob, "folds": folds, "experts0": experts0,
    }
    nc = bacc.Bacc("TRN2", target_bir_lowering=False, num_devices=1)
    A = {k: nc.dram_tensor("in_" + k, v.shape, mybir.dt.from_np(v.dtype), kind="ExternalInput").ap()
         for k, v in arrays.items()}
    out = nc.dram_tensor("out", (n, P, P), mybir.dt.float32, kind="ExternalOutput").ap()
    program(nc, A, regions, out, UPTO)
    r = run_bass_kernel_spmd(nc, [{"in_" + k: np.ascontiguousarray(v) for k, v in arrays.items()}], core_ids=[0])
    return r.results[0]["out"].reshape(2 * n, T, P)
```

```python
import math
from contextlib import ExitStack

import numpy as np

import concourse.bass as bass
from concourse import mybir

F32 = mybir.dt.float32
U8 = mybir.dt.uint8
BF16 = mybir.dt.bfloat16
ACT = mybir.ActivationFunctionType
ALU = mybir.AluOpType
AX = mybir.AxisListType

P = 128
B, T, S = 16, 64, 1601
H, HD = 16, 8
NPAIR = B // 2
NT = 13
TAIL = S - 12 * P
F = 512
EPS = 1e-5
LAMBDA_INIT = 0.2
GONE = -1e30

CTX_TILES = [(P * j, P) for j in range(12)] + [(12 * P, TAIL)]
KV_TILES = CTX_TILES + [(S, T)]


def rotations():
    f = np.float32
    row = np.arange(P) % HD
    tok = np.arange(P) % T
    theta0 = np.power(f(10000.0), (f(2.0) * (row // 2).astype(f) / f(HD)).astype(f)).astype(f)
    ang0 = (tok.astype(f)[None, :] / theta0[:, None]).astype(f)
    sign0 = np.where(row % 2 == 0, -1, 1).astype(f)[:, None]
    half = HD // 2
    theta1 = (f(1.0) / np.power(f(10000.0), (2 * (row % half)).astype(f) / f(HD)).astype(f)).astype(f)
    ang1 = ((tok + 1).astype(f)[None, :] * theta1[:, None]).astype(f)
    sign1 = np.where(row < half, -1, 1).astype(f)[:, None]
    return (np.cos(ang0), np.sin(ang0) * sign0, np.cos(ang1), np.sin(ang1) * sign1)


def constants():
    f = np.float32
    row = np.arange(P)
    cos0, sin0, cos1, sin1 = rotations()
    head = (row[:, None] // HD == np.arange(H)[None, :]).astype(f)
    c = np.arange(4)
    sub = ((row[:, None] % 16) // (HD // 2) == (2 * (c % 2) + c // 2)[None, :]).astype(f)
    t = row % T
    causal = np.where(np.arange(T)[None, :] <= t[:, None], 0.0, GONE).astype(f)
    same = (row[:, None] // T == row[None, :] // T).astype(f) / f(T)
    return {
        "ident": np.eye(P, dtype=f), "head_mask": head, "sub_mask": sub, "causal": causal,
        "free": np.zeros((P, T), f), "batch_mean": same, "neg_half": np.full((P, 16), -0.5, f),
        "row_places": (row[:, None] % 16 == row[None, :] % 16).astype(f),
        "pair_mask": (row[:, None] // 16 == np.arange(8)[None, :]).astype(f),
        "same_token": (t[:, None] == np.arange(T)[None, :]).astype(f),
        "cos0": cos0, "sin0": sin0, "cos1": cos1, "sin1": sin1,
    }


class Count:

    def __init__(self, sem):
        self.sem, self.base = sem, 0

    def at(self, n):
        return self.base + n

    def passed(self, n):
        self.base += n


class Chain:

    def __init__(self, engine, count):
        self.engine, self.count, self.n = engine, count, 0

    def __call__(self, ins):
        self.n += 1
        ins.then_inc(self.count.sem, 1)
        self.engine.wait_ge(self.count.sem, self.count.at(self.n))

    def end(self):
        self.count.passed(self.n)


class Machine:

    def __init__(self, nc, ctx, regions, names):
        self.nc, self.ctx = nc, ctx
        self.counts = {}
        self.regions = regions
        sb, ps = self.sbuf, self.psum
        self.weights = sb("weights", [P, max(a + n for a, n in regions.values())])
        self.x = sb("x_state", [P, P])
        self.xn = sb("x_normed", [P, P])
        self.xnT = sb("x_normed_T", [P, P])
        self.stat = sb("stat", [P, 16])
        self.small = sb("small", [P, 64])
        self.row8 = sb("row8", [P, 96])
        self.ctxN = [sb(f"ctx_rows{b}", [P, NT, P]) for b in range(2)]
        self.ctxT = [sb(f"ctx_cols{b}", [P, S]) for b in range(2)]
        self.arena = sb("arena", [P, ARENA])
        self.psS = ps("scores_banks", [P, 2048])
        self.psA = ps("bank_a", [P, 512])
        self.psB = ps("bank_b", [P, 512])
        self.psC = ps("bank_c", [P, 512])
        self.psD = ps("bank_d", [P, 512])

    def sbuf(self, name, shape, dt=F32):
        return self.ctx.enter_context(self.nc.sbuf_tensor(name, shape, dt))

    def psum(self, name, shape):
        return self.ctx.enter_context(self.nc.psum_tensor(name, shape, F32))

    def count(self, name):
        if name not in self.counts:
            self.counts[name] = Count(self.ctx.enter_context(self.nc.semaphore(name)))
        return self.counts[name]

    def w(self, name, rows=P):
        a, n = self.regions[name]
        return self.weights[0:rows, a:a + n]

    def at(self, start, n, rows=P):
        return self.arena[0:rows, start:start + n]


ARENA = 16768
EXPERTS0 = 10624
ONLY0 = 4 * (4 * 3 * P)


def layer_norm(nc, M):
    var, rstd, normed, turned = (M.count(n) for n in ("ln_var", "ln_rstd", "ln_normed", "ln_turned"))
    chain_c = M.count("ln_dve_chain")
    with nc.Block(no_gpsimd_drain=True) as block:
        @block.vector
        def _(dve):
            link = Chain(dve, chain_c)
            link(dve.bn_stats(M.stat[:, 0:6], M.x[:, :]))
            link(dve.bn_aggr(M.stat[:, 6:8], M.stat[:, 0:6]))
            dve.tensor_scalar(M.stat[:, 8:9], M.stat[:, 7:8], EPS, None, ALU.add).then_inc(var.sem, 1)
            dve.wait_ge(rstd.sem, rstd.at(1))
            dve.tensor_scalar(M.xn[:, :], M.x[:, :], M.stat[:, 6:7], M.stat[:, 9:10],
                              ALU.subtract, ALU.mult).then_inc(normed.sem, 1)
            link.end()

        @block.gpsimd
        def _(pool):
            pool.wait_ge(var.sem, var.at(1))
            pool.tensor_tensor(M.stat[:, 9:10], M.stat[:, 8:9], M.w("neg_half")[:, 0:1], ALU.pow).then_inc(rstd.sem, 1)

        @block.tensor
        def _(pe):
            pe.wait_ge(normed.sem, normed.at(1))
            pe.transpose(M.psA[:, 0:P], M.xn[:, :], M.w("ident")).then_inc(turned.sem, 1)

        @block.scalar
        def _(act):
            act.wait_ge(turned.sem, turned.at(1))
            act.activation(M.xnT[:, :], M.psA[:, 0:P], ACT.Copy)
    for c in (var, rstd, normed, turned):
        c.passed(1)


def attend(nc, M, *, units, rows, tiles, subs, queries, keys, values, bufs, pt, consume, bias=None, keep=None,
           scale=1.0, split=None):
    width = tiles[-1][0] + tiles[-1][1]
    chunks = [list(range(4 * c, 4 * c + 4)) for c in range(3)] + [[j] for j in range(12, len(tiles))]
    NC = len(chunks)
    scores, used, negmax, probs, weights, turned, moved, weighed, consumed, formed = (
        M.count(n) for n in ("at_scores", "at_scores_used", "at_negmax", "at_probs", "at_weights", "at_turned",
                             "at_moved", "at_weighed", "at_consumed", "at_queries_formed"))
    chain_c = M.count("at_dve_chain")
    stacked = [M.count(f"at_keys_stacked{i}") for i in range(2)]
    banks = [M.psA, M.psB, M.psC]
    small = M.small

    def buf(u, s):
        return bufs[(u * subs + s) % (2 * subs)][0:rows, 0:width]

    def col(kind, u, s):
        i = 16 * kind + 2 * (u % 4) + s
        return small[0:rows, i:i + 1]

    with nc.Block(no_gpsimd_drain=True) as block:
        @block.tensor
        def _(pe):
            def score(u, s):
                n = u * subs + s
                if n >= 1:
                    pe.wait_ge(used.sem, used.at(n))
                if split is not None and s == 0:
                    pe.wait_ge(formed.sem, formed.at(u + 1))
                    pe.wait_ge(stacked[u % 2].sem, stacked[u % 2].at(128 * (u // 2 + 1)))
                for a in range(0, width, 512):
                    m = min(512, width - a)
                    mm = pe.matmul(M.psS[0:rows, a:a + m], queries(u, s), keys(u, a, m), start=True, stop=True)
                mm.then_inc(scores.sem, 1)

            def turn(u):
                pe.wait_ge(weights.sem, weights.at(u + 1))
                for c, js in enumerate(chunks):
                    g = u * NC + c
                    if g >= 3:
                        pe.wait_ge(moved.sem, moved.at(g - 2))
                    for i, j in enumerate(js):
                        a, m = tiles[j]
                        mm = pe.transpose(banks[g % 3][0:m, i * P:i * P + rows], buf(u, 0)[:, a:a + m],
                                          M.w("ident")[0:rows, 0:rows])
                    mm.then_inc(turned.sem, 1)

            def weigh(u):
                if u >= 1:
                    pe.wait_ge(consumed.sem, consumed.at(u))
                for c, js in enumerate(chunks):
                    pe.wait_ge(moved.sem, moved.at(u * NC + c + 1))
                    for j in js:
                        m = tiles[j][1]
                        mm = pe.matmul(M.psD[:, 0:rows], values(u, j), pt[0:m, j * P:j * P + rows],
                                       start=(j == 0), stop=(j == len(tiles) - 1))
                mm.then_inc(weighed.sem, 1)

            for u in range(units + 2):
                if u < units:
                    score(u, 0)
                if u >= 2:
                    weigh(u - 2)
                if u < units and subs == 2:
                    score(u, 1)
                if 1 <= u <= units:
                    turn(u - 1)

        @block.scalar
        def _(act):
            def exponential(u, s):
                act.wait_ge(negmax.sem, negmax.at(u * subs + s + 1))
                act.activation(buf(u, s), buf(u, s), ACT.Exp, bias=col(0, u, s), scale=scale,
                               accum_out=col(1, u, s)).then_inc(probs.sem, 1)

            def move(u):
                for c, js in enumerate(chunks):
                    g = u * NC + c
                    m = tiles[js[0]][1]
                    act.wait_ge(turned.sem, turned.at(g + 1))
                    if u >= 1 and c == 0:
                        act.wait_ge(weighed.sem, weighed.at(u))
                    src = banks[g % 3][0:m, 0:len(js) * P].rearrange("p (j r) -> p j r", r=P)[:, :, 0:rows]
                    dst = pt[0:m, js[0] * P:(js[-1] + 1) * P].rearrange("p (j r) -> p j r", r=P)[:, :, 0:rows]
                    act.activation(dst, src, ACT.Copy).then_inc(moved.sem, 1)

            for u in range(units + 1):
                if u < units and subs == 2:
                    exponential(u, 0)
                if u >= 1:
                    move(u - 1)
                if u < units:
                    exponential(u, subs - 1)

        @block.vector
        def _(dve):
            link = Chain(dve, chain_c)

            def maximum(u, s):
                n = u * subs + s
                dve.wait_ge(scores.sem, scores.at(n + 1))
                if s == 0 and u >= 2:
                    dve.wait_ge(turned.sem, turned.at(NC * (u - 1)))
                if s == 1 and u >= 2:
                    dve.wait_ge(weights.sem, weights.at(u - 1))
                ps = M.psS[0:rows, 0:width]
                if keep is not None:
                    dve.tensor_tensor(buf(u, s), ps, keep(u), ALU.mult).then_inc(used.sem, 1)
                    dve.wait_ge(used.sem, used.at(n + 1))
                    link(dve.tensor_tensor_reduce(buf(u, s), buf(u, s), bias(u), 1.0, -3e38, ALU.add, ALU.max,
                                                  col(2, u, s)))
                else:
                    if bias is not None:
                        ins = dve.tensor_tensor_reduce(buf(u, s), ps, bias(u), 1.0, -3e38, ALU.add, ALU.max, col(2, u, s))
                    else:
                        ins = dve.tensor_scalar(buf(u, s), ps, 1.0, None, ALU.mult, ALU.max, accum_out=col(2, u, s))
                    ins.then_inc(used.sem, 1)
                    dve.wait_ge(used.sem, used.at(n + 1))
                dve.tensor_scalar(col(0, u, s), col(2, u, s), -scale, None, ALU.mult).then_inc(negmax.sem, 1)

            def weight(u):
                dve.wait_ge(probs.sem, probs.at(subs * (u + 1)))
                if subs == 1:
                    link(dve.reciprocal(col(1, u, 0), col(1, u, 0)))
                    dve.tensor_scalar(buf(u, 0), buf(u, 0), col(1, u, 0), None, ALU.mult).then_inc(weights.sem, 1)
                else:
                    link(dve.reciprocal(col(1, u, 1), col(1, u, 1)))
                    link(dve.tensor_scalar(col(2, u, 1), col(1, u, 0), col(1, u, 1), split, ALU.mult, ALU.mult))
                    dve.scalar_tensor_tensor(buf(u, 0), buf(u, 1), col(2, u, 1), buf(u, 0), ALU.mult,
                                             ALU.add).then_inc(weights.sem, 1)
                    link(dve.reciprocal(M.row8[:, u:u + 1], col(1, u, 0)))

            for u in range(units + 2):
                if u < units and subs == 2:
                    maximum(u, 0)
                if 1 <= u <= units:
                    weight(u - 1)
                if u < units:
                    maximum(u, subs - 1)
                if u >= 2:
                    dve.wait_ge(weighed.sem, weighed.at(u - 1))
                    consume(dve, link, u - 2).then_inc(consumed.sem, 1)
            link.end()

        if split is not None:
            @block.sync
            def _(sp):
                for u in range(2, units):
                    sp.wait_ge(scores.sem, scores.at(2 * (u - 1)))
                    for part in range(3):
                        stack_keys(sp, M, u, part)

            @block.gpsimd
            def _(pool):
                for u in range(units):
                    if u >= 2:
                        pool.wait_ge(scores.sem, scores.at(2 * (u - 1)))
                    src, mask, dst = split_operands(M, u)
                    pool.tensor_tensor(dst, src, mask, ALU.mult).then_inc(formed.sem, 1)
    scores.passed(units * subs)
    used.passed(units * subs)
    negmax.passed(units * subs)
    probs.passed(units * subs)
    weights.passed(units)
    turned.passed(units * NC)
    moved.passed(units * NC)
    weighed.passed(units)
    consumed.passed(units)
    if split is not None:
        formed.passed(units)
        for c in stacked:
            c.passed(128 * units // 2)


A0_BUF = [0, S, 2 * S, 3 * S]
A0_PT = 4 * S
A0_V = A0_PT + NT * P
HALF_S = (S + 1) // 2
A0_KPART = [A0_V + NT * P + i * HALF_S for i in range(3)]
A0_KSTACK = [A0_KPART[2] + (i + 1) * HALF_S for i in range(2)]
A0_Q = A0_KSTACK[1] + HALF_S
A0_QPART = A0_Q + 2 * P
A0_QSTACK = A0_QPART + 3 * P // 2
A0_QB = A0_QSTACK + 4 * P
A0_ATT = A0_QB + 2 * P
A0_SPREAD = A0_ATT + P
assert A0_SPREAD + P <= ARENA

PART_PAIRS = [(0, 0), (1, 0), (2, 0), (0, 1), (1, 1), (2, 1), (0, 2), (1, 2)]


def split_operands(M, u):
    stack = M.at(A0_QSTACK, 4 * P).bitcast(BF16)
    src = stack[:, u * P + M.batch * T:u * P + (M.batch + 1) * T].unsqueeze(1).broadcast_to((P, 4, T))
    mask = M.w("sub_mask").unsqueeze(2).broadcast_to((P, 4, T))
    return src, mask, unit_queries(M, u).rearrange("p (c t) -> p c t", t=T)


def unit_queries(M, u):
    return M.at(A0_QB + P * (u % 2), P).bitcast(BF16)


def key_stack(M, u):
    return M.at(A0_KSTACK[u % 2], HALF_S).bitcast(BF16)[:, 0:S]


def stack_keys(sp, M, u, part):
    for c, (_, k) in enumerate(PART_PAIRS):
        if k == part:
            sp.dma_start(key_stack(M, u)[16 * c:16 * (c + 1), :],
                         key_part(M, part)[16 * u:16 * (u + 1), :]).then_inc(M.count(f"at_keys_stacked{u % 2}").sem, 16)


def key_part(M, i):
    return M.at(A0_KPART[i], HALF_S).bitcast(BF16)[:, 0:S]


def project_out(nc, M, name, terms, bias=None):
    done = M.count("out_projected")
    chain_c = M.count("out_dve_chain")
    with nc.Block(no_gpsimd_drain=True) as block:
        @block.tensor
        def _(pe):
            for i, (lhs, rhs) in enumerate(terms):
                mm = pe.matmul(M.psA[:, 0:P], lhs, rhs, start=(i == 0), stop=(i == len(terms) - 1))
            mm.then_inc(done.sem, 1)

        @block.vector
        def _(dve):
            link = Chain(dve, chain_c)
            if bias is not None:
                link(dve.tensor_tensor(M.x[:, :], M.x[:, :], bias, ALU.add))
            dve.wait_ge(done.sem, done.at(1))
            dve.tensor_tensor(M.x[:, :], M.x[:, :], M.psA[:, 0:P], ALU.add)
            link.end()
    done.passed(1)


def cross0(nc, M):
    q_done, k_done, v_done, q_part, q_spread, q_summed, k_hi, k_rest, k_mid, k_rest2, k_lo = (M.count("x0_" + n) for n in (
        "q", "k", "v", "q_parts", "q_spread", "q_stack_summed", "k_hi", "k_rest", "k_mid", "k_rest2", "k_lo"))
    chain_c = M.count("x0_dve_chain")
    V, att = M.at(A0_V, NT * P), M.at(A0_ATT, P)
    q, rest = M.at(A0_Q, P), M.at(A0_Q + P, P)
    qp = [M.at(A0_QPART + i * P // 2, P // 2).bitcast(BF16) for i in range(3)]
    q_stack = M.at(A0_QSTACK, 4 * P).bitcast(BF16)
    q_wide = [M.at(A0_BUF[1] + 4 * P * i, 4 * P).bitcast(BF16) for i in range(3)]
    places = M.at(A0_BUF[2], 3 * P // 2).bitcast(BF16)
    place = [places[:, P * i:P * (i + 1)] for i in range(3)]
    kp = [key_part(M, i) for i in range(3)]
    k_left = M.at(A0_BUF[0], S)
    for b in range(2):
        M.batch = b
        with nc.Block(no_gpsimd_drain=True) as block:
            @block.sync
            def _(sp):
                for part, ready in enumerate((k_hi, k_mid, k_lo)):
                    sp.wait_ge(ready.sem, ready.at(1))
                    for u in range(2):
                        stack_keys(sp, M, u, part)

            @block.tensor
            def _(pe):
                cols_in = M.count(f"ctx_cols{b}_loaded")
                pe.wait_ge(cols_in.sem, cols_in.at(16))
                if b == 0:
                    pe.matmul(M.psD[:, 0:P], M.w("x0_wq"), M.xnT[:, :], start=True, stop=True).then_inc(q_done.sem, 1)
                for a in range(0, S, 512):
                    m = min(512, S - a)
                    mm = pe.matmul(M.psS[:, a:a + m], M.w("x0_wk"), M.ctxT[b][:, a:a + m], start=True, stop=True)
                mm.then_inc(k_done.sem, 1)
                for c, bank in enumerate([M.psA, M.psB, M.psC]):
                    for j in range(4 * c, 4 * c + 4):
                        mm = pe.matmul(bank[:, (j % 4) * P:(j % 4 + 1) * P], M.ctxT[b][:, j * P:(j + 1) * P],
                                       M.w("x0_wv"), start=True, stop=True)
                    mm.then_inc(v_done.sem, 1)
                if b == 0:
                    pe.wait_ge(q_done.sem, q_done.at(2))
                pe.matmul(M.psD[0:TAIL, P:2 * P], M.ctxT[b][:, 12 * P:S], M.w("x0_wv"), start=True,
                          stop=True).then_inc(v_done.sem, 1)
                if b == 0:
                    pe.wait_ge(q_spread.sem, q_spread.at(3))
                    pe.wait_ge(k_rest.sem, k_rest.at(1))
                    for g in range(2):
                        for i in range(3):
                            mm = pe.matmul(M.psS[:, 512 * g:512 * (g + 1)], place[i], q_wide[i][:, 512 * g:512 * (g + 1)],
                                           start=(i == 0), stop=(i == 2))
                    mm.then_inc(q_summed.sem, 1)

            @block.scalar
            def _(act):
                act.wait_ge(k_done.sem, k_done.at(1))
                act.activation(kp[0], M.psS[:, 0:S], ACT.Identity, bias=M.w("x0_bk")).then_inc(k_hi.sem, 1)
                act.wait_ge(k_rest.sem, k_rest.at(1))
                act.activation(kp[1], k_left, ACT.Copy).then_inc(k_mid.sem, 1)
                act.wait_ge(k_rest2.sem, k_rest2.at(1))
                act.activation(kp[2], k_left, ACT.Copy).then_inc(k_lo.sem, 1)
                if b == 0:
                    act.wait_ge(q_summed.sem, q_summed.at(1))
                    act.activation(q_stack, M.psS[:, 0:8 * P], ACT.Copy)

            @block.vector
            def _(dve):
                link = Chain(dve, chain_c)
                if b == 0:
                    dve.wait_ge(q_done.sem, q_done.at(1))
                    dve.tensor_scalar(q, M.psD[:, 0:P], M.w("x0_bq"), 0.5, ALU.add, ALU.mult).then_inc(q_done.sem, 1)
                    dve.wait_ge(q_done.sem, q_done.at(2))
                    left = q
                    for i in range(3):
                        dve.tensor_copy(qp[i], left).then_inc(q_part.sem, 1)
                        if i < 2:
                            dve.wait_ge(q_part.sem, q_part.at(i + 1))
                            link(dve.tensor_tensor(rest, left, qp[i], ALU.subtract))
                            left = rest
                    link(dve.memset(places, 0.0))
                    for i in range(3):
                        for c, (part, _) in enumerate(PART_PAIRS):
                            if part == i:
                                rows16 = slice(16 * c, 16 * (c + 1))
                                dve.tensor_copy(place[i][:, rows16], M.w("row_places")[:, rows16])
                        dve.tensor_tensor(q_wide[i].rearrange("p (u t) -> p u t", t=P),
                                          qp[i].unsqueeze(1).broadcast_to((P, 8, P)),
                                          M.w("pair_mask").unsqueeze(2).broadcast_to((P, 8, P)),
                                          ALU.mult).then_inc(q_spread.sem, 1)
                dve.wait_ge(k_hi.sem, k_hi.at(1))
                dve.scalar_tensor_tensor(k_left, M.psS[:, 0:S], M.w("x0_bk"), kp[0], ALU.add,
                                         ALU.subtract).then_inc(k_rest.sem, 1)
                for c, bank in enumerate([M.psA, M.psB, M.psC]):
                    if c == 2:
                        dve.wait_ge(k_mid.sem, k_mid.at(1))
                        dve.tensor_tensor(k_left, k_left, kp[1], ALU.subtract).then_inc(k_rest2.sem, 1)
                    dve.wait_ge(v_done.sem, v_done.at(c + 1))
                    dve.tensor_tensor(V[:, 512 * c:512 * (c + 1)].rearrange("p (j d) -> p j d", d=P),
                                      bank[:, :].rearrange("p (j d) -> p j d", d=P),
                                      M.w("x0_bv").unsqueeze(1).broadcast_to((P, 4, P)), ALU.add)
                dve.wait_ge(v_done.sem, v_done.at(4))
                dve.tensor_tensor(V[0:TAIL, 12 * P:NT * P], M.psD[0:TAIL, P:2 * P], M.w("x0_bv", TAIL), ALU.add)
                link.end()
        if b == 0:
            q_done.passed(2)
            q_part.passed(3)
            q_spread.passed(3)
            q_summed.passed(1)
        for c in (k_done, k_hi, k_rest, k_mid, k_rest2, k_lo):
            c.passed(1)
        v_done.passed(4)

        def gather(dve, link, u):
            out = att[:, b * T:(b + 1) * T]
            for h in range(2):
                mask = M.w("head_mask")[:, 2 * u + h:2 * u + h + 1]
                src = M.psD[:, h * T:(h + 1) * T]
                if u == 0 and h == 0:
                    ins = dve.tensor_scalar(out, src, mask, None, ALU.mult)
                else:
                    ins = dve.scalar_tensor_tensor(out, src, mask, out, ALU.mult, ALU.add)
                if h == 0:
                    link(ins)
            return ins

        attend(nc, M, units=8, rows=P, tiles=CTX_TILES, subs=2,
               queries=lambda u, s: unit_queries(M, u)[:, P * s:P * (s + 1)],
               keys=lambda u, a, m: key_stack(M, u)[:, a:a + m],
               values=lambda u, j: V[0:CTX_TILES[j][1], j * P:(j + 1) * P],
               bufs=[M.at(a, S) for a in A0_BUF], pt=M.at(A0_PT, 1664), consume=gather,
               split=M.lam[:, 0:1])
        divided, spread = M.count("x0_spread_formed"), M.count("x0_spread_turned")
        L = M.at(A0_SPREAD, P)
        L4 = L.rearrange("p (u h d) -> p u h d", u=8, h=2)
        with nc.Block(no_gpsimd_drain=True) as block:
            @block.vector
            def _(dve):
                link = Chain(dve, chain_c)
                link(dve.memset(L, 0.0))
                for h in range(2):
                    r = slice(T * h, T * (h + 1))
                    dve.tensor_scalar(L4[r, :, h, :], M.row8[r, 0:8].unsqueeze(2).broadcast_to((T, 8, HD)),
                                      1.0 - LAMBDA_INIT, None, ALU.mult).then_inc(divided.sem, 1)
                dve.wait_ge(spread.sem, spread.at(1))
                out = att[:, b * T:(b + 1) * T]
                link(dve.tensor_tensor(out, out, M.psA[:, 0:T], ALU.mult))
                link.end()

            @block.tensor
            def _(pe):
                pe.wait_ge(divided.sem, divided.at(2))
                pe.matmul(M.psA[:, 0:T], L, M.w("same_token"), start=True, stop=True).then_inc(spread.sem, 1)
        divided.passed(2)
        spread.passed(1)
    project_out(nc, M, "x0", [(att, M.w("x0_wo"))], M.w("x0_bo"))


SA_Q, SA_K, SA_T1, SA_T2 = 0, 128, 256, 384
SA_QB, SA_V, SA_S, SA_W, SA_PT, SA_ATT = 512, 2560, 2816, 3840, 4864, 6912
SA_M = 7040
assert SA_M + 9 * H <= EXPERTS0


def self_attention(nc, M, n, *, rope=None, biased, causal, scale, top=None, experts0=None):
    proj, formed, queries, scored, packed, expd, weights, turned, moved, weighed, gathered, vals = (
        M.count("sa_" + k) for k in ("projected", "qk_formed", "queries", "scored", "packed", "exponentials",
                                     "weights", "turned", "moved", "weighed", "gathered", "values"))
    chain_c = M.count("sa_dve_chain")
    pre = n + "_"
    q, k, t1, t2 = (M.at(a, P) for a in (SA_Q, SA_K, SA_T1, SA_T2))
    qb = M.at(SA_QB, H * P).rearrange("p (h t) -> p h t", t=P)
    v = M.at(SA_V, 2 * P, T)
    s = M.at(SA_S, H * T).rearrange("p (h s) -> p h s", s=T)
    w = M.at(SA_W, H * T).rearrange("p (h s) -> p h s", s=T)
    pt = M.at(SA_PT, H * P, T).rearrange("p (h t) -> p h t", t=P)
    att = M.at(SA_ATT, P)
    mx = M.at(SA_M, H)
    tops = M.at(SA_M + H, 8 * H)
    ps = M.psS[:, :].rearrange("p (h s) -> p h s", s=P)
    mask = M.w("head_mask")
    with nc.Block(no_gpsimd_drain=True) as block:
        if experts0 is not None:
            @block.sync
            def _(sp):
                sp.dma_start(M.at(EXPERTS0, ONLY0), experts0).then_inc(M.count("experts0_loaded").sem, 16)

        @block.tensor
        def _(pe):
            names = ["wq", "wk"] + (["wq_turned", "wk_turned"] if rope else [])
            for i, name in enumerate(names):
                mm = pe.matmul(M.psA[:, i * P:(i + 1) * P], M.w(pre + name), M.xnT[:, :], start=True, stop=True)
            mm.then_inc(proj.sem, 1)
            for b in range(2):
                mm = pe.matmul(M.psB[0:T, b * P:(b + 1) * P], M.xnT[:, b * T:(b + 1) * T], M.w(pre + "wv"),
                               start=True, stop=True)
            mm.then_inc(vals.sem, 1)
            pe.wait_ge(formed.sem, formed.at(1))
            for g in range(2):
                pe.wait_ge(queries.sem, queries.at(g + 1))
                for h in range(8 * g, 8 * g + 8):
                    mm = pe.matmul(ps[:, h, :], qb[:, h, :], k, start=True, stop=True)
            mm.then_inc(scored.sem, 1)
            pe.wait_ge(weights.sem, weights.at(1))
            banks = [M.psA, M.psC, M.psB, M.psD]
            for c in range(4):
                for i in range(4):
                    mm = pe.transpose(banks[c][0:T, i * P:(i + 1) * P], s[:, 4 * c + i, :], M.w("ident"))
                mm.then_inc(turned.sem, 1)
            pe.wait_ge(moved.sem, moved.at(4))
            for b in range(2):
                for g in range(2):
                    mm = pe.matmul(M.psS[:, 512 * (2 * b + g):512 * (2 * b + g + 1)], v[:, b * P:(b + 1) * P],
                                   pt[:, 8 * g:8 * g + 8, b * T:(b + 1) * T], start=True, stop=True)
                mm.then_inc(weighed.sem, 1)

        @block.scalar
        def _(act):
            act.wait_ge(packed.sem, packed.at(1))
            act.activation(s, s, ACT.Exp).then_inc(expd.sem, 1)
            banks = [M.psA, M.psC, M.psB, M.psD]
            for c in range(4):
                act.wait_ge(turned.sem, turned.at(c + 1))
                act.activation(pt[:, 4 * c:4 * c + 4, :], banks[c][0:T, :].rearrange("p (h t) -> p h t", t=P),
                               ACT.Copy).then_inc(moved.sem, 1)

        @block.gpsimd
        def _(pool):
            pool.wait_ge(formed.sem, formed.at(2))
            for g in range(2):
                hs = slice(8 * g, 8 * g + 8)
                pool.tensor_tensor(qb[:, hs, :], q.unsqueeze(1).broadcast_to((P, 8, P)),
                                   mask[:, hs].unsqueeze(2).broadcast_to((P, 8, P)), ALU.mult).then_inc(queries.sem, 1)

        @block.vector
        def _(dve):
            link = Chain(dve, chain_c)
            dve.wait_ge(proj.sem, proj.at(1))
            for i, (dst, bias) in ((1, (k, "bk")), (0, (q, "bq"))):
                src = M.psA[:, i * P:(i + 1) * P]
                if rope:
                    cos, sin = M.w("cos" + rope), M.w("sin" + rope)
                    other = M.psA[:, (2 + i) * P:(3 + i) * P]
                    if biased:
                        link(dve.scalar_tensor_tensor(t1, src, M.w(pre + bias), cos, ALU.add, ALU.mult))
                        link(dve.scalar_tensor_tensor(t2, other, M.w(pre + bias + "_turned"), sin, ALU.add, ALU.mult))
                    else:
                        link(dve.tensor_tensor(t1, src, cos, ALU.mult))
                        link(dve.tensor_tensor(t2, other, sin, ALU.mult))
                    if i == 1 or scale == 1.0:
                        dve.tensor_tensor(dst, t1, t2, ALU.add).then_inc(formed.sem, 1)
                        dve.wait_ge(formed.sem, formed.at(2 - i))
                    else:
                        link(dve.tensor_tensor(t1, t1, t2, ALU.add))
                        dve.tensor_scalar(dst, t1, scale, None, ALU.mult).then_inc(formed.sem, 1)
                else:
                    dve.tensor_scalar(dst, src, M.w(pre + bias), 1.0 if i else scale, ALU.add,
                                      ALU.mult).then_inc(formed.sem, 1)
            dve.wait_ge(vals.sem, vals.at(1))
            for b in range(2):
                src, dst = M.psB[0:T, b * P:(b + 1) * P], v[:, b * P:(b + 1) * P]
                if biased:
                    link(dve.tensor_tensor(dst, src, M.w(pre + "bv", T), ALU.add))
                else:
                    link(dve.tensor_copy(dst, src))
            dve.wait_ge(scored.sem, scored.at(1))
            seen = M.w("causal" if causal else "free")
            for b in range(2):
                r = slice(b * T, (b + 1) * T)
                link(dve.tensor_tensor(s[r], ps[r, :, r], seen[r].unsqueeze(1).broadcast_to((T, H, T)), ALU.add))
            link(dve.tensor_reduce(mx, s, AX.X, ALU.max))
            if top:
                src = s
                for _ in range(top // 8):
                    for h in range(H):
                        ins = dve.max(tops[:, 8 * h:8 * h + 8], src[:, h, :])
                    link(ins)
                    for h in range(H):
                        ins = dve.match_replace(w[:, h, :], tops[:, 8 * h:8 * h + 8], src[:, h, :], -3e38)
                    link(ins)
                    src = w
                link(dve.tensor_tensor(w, w, s, ALU.not_equal))
            dve.tensor_tensor(s, s, mx.unsqueeze(2).broadcast_to((P, H, T)), ALU.subtract).then_inc(packed.sem, 1)
            dve.wait_ge(expd.sem, expd.at(1))
            if top:
                link(dve.tensor_tensor(s, s, w, ALU.mult))
            link(dve.tensor_reduce(mx, s, AX.X, ALU.add))
            link(dve.reciprocal(mx, mx))
            dve.tensor_tensor(s, s, mx.unsqueeze(2).broadcast_to((P, H, T)), ALU.mult).then_inc(weights.sem, 1)
            for b in range(2):
                dve.wait_ge(weighed.sem, weighed.at(b + 1))
                out = M.psS[:, 1024 * b:1024 * (b + 1)].rearrange("p (h t) -> p h t", t=T)
                link(dve.tensor_tensor(w, out, mask.unsqueeze(2).broadcast_to((P, H, T)), ALU.mult))
                link(dve.tensor_reduce(att[:, b * T:(b + 1) * T], w.rearrange("p h t -> p t h"), AX.X, ALU.add))
            link.end()
    for c in (proj, scored, packed, expd, weights, vals):
        c.passed(1)
    formed.passed(2)
    queries.passed(2)
    turned.passed(4)
    moved.passed(4)
    weighed.passed(2)
    project_out(nc, M, n, [(att, M.w(pre + "wo"))], M.w(pre + "bo") if biased else None)


MO_H, MO_G, MO_GT, MO_MEAN = 0, 2048, 2176, 2304


def experts(nc, M, n, *, E, kind, up, up3, down, router, router_bias=None, b1=None, b2=None, floor=0.0, by_batch=False):
    pre = n + "_"
    logits, shifted, soft, gated, gT_ps, gT_sb, up_done, acted, prod, down_done, added, mean = (
        M.count("mo_" + k) for k in ("logits", "shifted", "softmax", "gates", "gates_turned", "gates_moved", "up",
                                     "activated", "product", "down", "added", "mean"))
    chain_c = M.count("mo_dve_chain")
    R = M.row8
    lg, top8, e16, rep, sel, g = (R[:, a:a + n_] for a, n_ in ((0, 8), (8, 8), (16, 16), (32, 16), (48, 8), (56, 8)))
    sc = R[:, 64:72]
    hT = [M.at(MO_H + 512 * i, 512) for i in range(4)]
    gT = M.at(MO_GT, P, 8)
    meanT = M.at(MO_MEAN, P)
    two = kind == "silu"
    with nc.Block(no_gpsimd_drain=True) as block:
        @block.tensor
        def _(pe):
            xr = M.xnT[:, :]
            if by_batch:
                pe.matmul(M.psB[:, 0:P], M.xn[:, :], M.w("batch_mean"), start=True, stop=True).then_inc(mean.sem, 1)
                pe.wait_ge(mean.sem, mean.at(2))
                xr = meanT
            pe.matmul(M.psA[:, 0:E], xr, router, start=True, stop=True).then_inc(logits.sem, 1)

            def raise_(e):
                if two:
                    if e >= 2:
                        pe.wait_ge(prod.sem, prod.at(e - 1))
                elif e >= 4:
                    pe.wait_ge(acted.sem, acted.at(e - 3))
                for w_, off in ((up, 0), (up3, 1))[:2 if two else 1]:
                    a = 512 * (2 * (e % 2) + off if two else e % 4)
                    for c in range(4):
                        mm = pe.matmul(M.psS[:, a + P * c:a + P * (c + 1)], w_(e, c), M.xnT[:, :], start=True,
                                       stop=True)
                mm.then_inc(up_done.sem, 1)

            if two:
                pe.wait_ge(M.count("experts0_loaded").sem, 16)
            raise_(0)
            for e in range(E):
                if e + 1 < E:
                    raise_(e + 1)
                ready = prod if two else acted
                pe.wait_ge(ready.sem, ready.at(e + 1))
                if e >= 2:
                    pe.wait_ge(added.sem, added.at(e - 1))
                bank = [M.psB, M.psC][e % 2]
                if by_batch and e == 0:
                    pe.wait_ge(mean.sem, mean.at(2))
                for c in range(4):
                    mm = pe.matmul(bank[:, 0:P], hT[e % 4][:, P * c:P * (c + 1)], down(e, c), start=(c == 0),
                                   stop=(c == 3))
                mm.then_inc(down_done.sem, 1)
            if b2 is not None:
                pe.wait_ge(gated.sem, gated.at(1))
                pe.transpose(M.psA[0:8, 128:256], g, M.w("ident")).then_inc(gT_ps.sem, 1)
                pe.wait_ge(gT_sb.sem, gT_sb.at(1))
                pe.matmul(M.psD[:, 0:P], gT, b2, start=True, stop=True).then_inc(gT_ps.sem, 1)

        @block.scalar
        def _(act):
            act.wait_ge(shifted.sem, shifted.at(1))
            act.activation(e16[:, 0:8], lg, ACT.Exp, bias=sc[:, 0:1], accum_out=sc[:, 1:2]).then_inc(soft.sem, 1)
            for e in range(E):
                act.wait_ge(up_done.sem, up_done.at(e + 1))
                if e >= 4:
                    act.wait_ge(down_done.sem, down_done.at(e - 3))
                if two:
                    act.activation(hT[e % 4], M.psS[:, 1024 * (e % 2):1024 * (e % 2) + 512],
                                   ACT.Silu).then_inc(acted.sem, 1)
                else:
                    for c in range(4):
                        fn = ACT.Relu if kind == "relu" else ACT.Gelu
                        ins = act.activation(hT[e % 4][:, P * c:P * (c + 1)],
                                             M.psS[:, 512 * (e % 4) + P * c:512 * (e % 4) + P * (c + 1)], fn,
                                             bias=b1[:, 4 * e + c:4 * e + c + 1])
                    ins.then_inc(acted.sem, 1)

        @block.vector
        def _(dve):
            link = Chain(dve, chain_c)
            link(dve.memset(lg, GONE))
            link(dve.memset(e16, -1.0))
            if by_batch:
                dve.wait_ge(mean.sem, mean.at(1))
                dve.tensor_copy(meanT, M.psB[:, 0:P]).then_inc(mean.sem, 1)
            dve.wait_ge(logits.sem, logits.at(1))
            if router_bias is not None:
                link(dve.tensor_tensor(lg[:, 0:E], M.psA[:, 0:E], router_bias, ALU.add))
            else:
                link(dve.tensor_copy(lg[:, 0:E], M.psA[:, 0:E]))
            dve.tensor_reduce(sc[:, 0:1], lg, AX.X, ALU.max, negate=True).then_inc(shifted.sem, 1)
            dve.wait_ge(soft.sem, soft.at(1))
            link(dve.reciprocal(sc[:, 2:3], sc[:, 1:2]))
            link(dve.tensor_scalar(e16[:, 0:8], e16[:, 0:8], sc[:, 2:3], None, ALU.mult))
            link(dve.max(top8, e16[:, 0:8]))
            link(dve.tensor_scalar(sc[:, 3:4], top8[:, 0:1], top8[:, 1:2], floor, ALU.add, ALU.add))
            link(dve.memset(top8[:, 2:8], -1.0))
            link(dve.match_replace(rep, top8, e16, -2.0))
            link(dve.tensor_tensor(sel, rep[:, 0:8], e16[:, 0:8], ALU.not_equal))
            link(dve.tensor_tensor(sel, sel, e16[:, 0:8], ALU.mult))
            link(dve.reciprocal(sc[:, 4:5], sc[:, 3:4]))
            dve.tensor_scalar(g, sel, sc[:, 4:5], None, ALU.mult).then_inc(gated.sem, 1)
            dve.wait_ge(gated.sem, gated.at(1))

            def add(e):
                dve.wait_ge(down_done.sem, down_done.at(e + 1))
                if e >= 1:
                    dve.wait_ge(added.sem, added.at(e))
                dve.scalar_tensor_tensor(M.x[:, :], [M.psB, M.psC][e % 2][:, 0:P], g[:, e:e + 1], M.x[:, :], ALU.mult,
                                         ALU.add).then_inc(added.sem, 1)

            for e in range(E):
                if two:
                    dve.wait_ge(acted.sem, acted.at(e + 1))
                    a = 1024 * (e % 2) + 512
                    dve.tensor_tensor(hT[e % 4], hT[e % 4], M.psS[:, a:a + 512], ALU.mult).then_inc(prod.sem, 1)
                if e >= 1:
                    add(e - 1)
            add(E - 1)
            if b2 is not None:
                dve.wait_ge(gT_ps.sem, gT_ps.at(1))
                dve.tensor_copy(gT, M.psA[0:8, 128:256]).then_inc(gT_sb.sem, 1)
                dve.wait_ge(gT_ps.sem, gT_ps.at(2))
                dve.wait_ge(added.sem, added.at(E))
                dve.tensor_tensor(M.x[:, :], M.x[:, :], M.psD[:, 0:P], ALU.add)
            link.end()
    for c in (logits, shifted, soft, gated):
        c.passed(1)
    for c in (up_done, acted, down_done, added):
        c.passed(E)
    if two:
        prod.passed(E)
    if by_batch:
        mean.passed(2)
    if b2 is not None:
        gT_ps.passed(2)
        gT_sb.passed(1)


WIDE = S + T
A1_BUF = [0, 1792]
A1_PT, A1_ROWS, A1_KT = 3584, 5376, 7168
A1_T, A1_K, A1_LAT, A1_LATT = 0, 512, 1536, 1664
A1_Q, A1_QT, A1_SQ = 1792, 2304, 3584
A1_QB = A1_KT + 4 * WIDE
A1_MASK = A1_QB + 1024
A1_UT = A1_MASK + (WIDE + 1) // 2
A1_SEEN = 2816
assert A1_UT + 8 * P <= ARENA, A1_UT + 8 * P


def cross1(nc, M, batch_seen):
    chain_c = M.count("x1_dve_chain")
    rows = M.at(A1_ROWS, 14 * P).rearrange("p (j d) -> p j d", d=P)
    kT = M.at(A1_KT, 4 * WIDE).rearrange("p (c s) -> p c s", s=WIDE)
    qb = M.at(A1_QB, 1024).rearrange("p (b c t) -> p b c t", b=2, c=4)
    lat, latT = M.at(A1_LAT, P), M.at(A1_LATT, P)
    q, qT, sq = M.at(A1_Q, 512), M.at(A1_QT, 512), M.at(A1_SQ, 512)
    mask = M.at(A1_MASK, (WIDE + 1) // 2).bitcast(BF16)[:, 0:WIDE]
    seen = M.at(A1_SEEN, (S + 3) // 4).bitcast(U8)[:, 0:S]
    UT = M.at(A1_UT, 8 * P).rearrange("p (h t) -> p h t", t=P)
    st = M.small
    var, rstd, normed, turned, moved, projected, norm2, rnorm, scaled, q_turned = (
        M.count("x1_" + k) for k in ("var", "rstd", "lat_normed", "lat_turned", "lat_moved", "q_projected",
                                     "q_norm2", "q_rnorm", "q_scaled", "q_turned"))
    with nc.Block(no_gpsimd_drain=True) as block:
        @block.vector
        def _(dve):
            link = Chain(dve, chain_c)
            link(dve.bn_stats(M.stat[:, 0:6], M.xn[:, :]))
            link(dve.bn_aggr(M.stat[:, 6:8], M.stat[:, 0:6]))
            dve.tensor_scalar(M.stat[:, 8:9], M.stat[:, 7:8], EPS, None, ALU.add).then_inc(var.sem, 1)
            link(dve.memset(qb, 0.0))
            dve.wait_ge(rstd.sem, rstd.at(1))
            link(dve.tensor_scalar(lat, M.xn[:, :], M.stat[:, 6:7], M.stat[:, 9:10], ALU.subtract, ALU.mult))
            link(dve.tensor_tensor(lat, lat, M.w("x1_lat_w"), ALU.mult))
            dve.tensor_tensor(lat, lat, M.w("x1_lat_b"), ALU.add).then_inc(normed.sem, 1)
            dve.wait_ge(projected.sem, projected.at(1))
            link(dve.tensor_copy(q, M.psS[:, 0:512]))
            link(dve.tensor_tensor(sq, q, q, ALU.mult))
            link(dve.tensor_reduce(st[:, 0:8], sq.rearrange("p (h d) -> p h d", d=64), AX.X, ALU.add))
            dve.tensor_scalar(st[:, 0:8], st[:, 0:8], 1e-24, None, ALU.max).then_inc(norm2.sem, 1)
            dve.wait_ge(rnorm.sem, rnorm.at(1))
            q3 = q.rearrange("p (h d) -> p h d", d=64)
            link(dve.tensor_tensor(q3, q3, st[:, 8:16].unsqueeze(2).broadcast_to((P, 8, 64)), ALU.mult))
            for name in ("x1_q_scale", "x1_k_scale"):
                link(dve.tensor_tensor(q3, q3, M.w(name).unsqueeze(1).broadcast_to((P, 8, 64)), ALU.mult))
            dve.tensor_scalar(q, q, 8.0, None, ALU.mult).then_inc(scaled.sem, 1)
            dve.wait_ge(q_turned.sem, q_turned.at(1))
            for h in range(2):
                r = slice(64 * h, 64 * (h + 1))
                for b in range(2):
                    src = M.psS[r, 1024:1536].rearrange("p (c t) -> p c t", t=P)[:, :, b * T:(b + 1) * T]
                    link(dve.tensor_copy(qb[r, b, :, 64 * h:64 * (h + 1)], src))
            link.end()

        @block.gpsimd
        def _(pool):
            pool.wait_ge(var.sem, var.at(1))
            pool.tensor_tensor(M.stat[:, 9:10], M.stat[:, 8:9], M.w("neg_half")[:, 0:1], ALU.pow).then_inc(rstd.sem, 1)
            pool.wait_ge(norm2.sem, norm2.at(1))
            pool.tensor_tensor(st[:, 8:16], st[:, 0:8], M.w("neg_half")[:, 0:8], ALU.pow).then_inc(rnorm.sem, 1)

        @block.tensor
        def _(pe):
            pe.wait_ge(normed.sem, normed.at(1))
            pe.transpose(M.psA[:, 0:P], lat, M.w("ident")).then_inc(turned.sem, 1)
            pe.wait_ge(moved.sem, moved.at(1))
            pe.matmul(M.psS[:, 0:512], latT, M.w("x1_wq"), start=True, stop=True).then_inc(projected.sem, 1)
            pe.wait_ge(scaled.sem, scaled.at(1))
            for c in range(4):
                mm = pe.transpose(M.psS[:, 1024 + P * c:1024 + P * (c + 1)], q[:, P * c:P * (c + 1)], M.w("ident"))
            mm.then_inc(q_turned.sem, 1)

        @block.scalar
        def _(act):
            act.wait_ge(turned.sem, turned.at(1))
            act.activation(latT, M.psA[:, 0:P], ACT.Copy).then_inc(moved.sem, 1)
    for c in (var, rstd, normed, turned, moved, projected, norm2, rnorm, scaled, q_turned):
        c.passed(1)

    cvar, crstd, crows, ct, cm, ck, csq, cn2, crn, ckn, ckt, ckm = (
        M.count("x1k_" + k) for k in ("var", "rstd", "rows", "turned", "moved", "projected", "squared", "norm2",
                                      "rnorm", "normed", "keys_turned", "keys_moved"))
    cseen = M.count("x1k_seen_loaded")
    rows_in = M.count("ctx_rows_loaded")
    for b in range(2):
        ctx3 = M.ctxN[b][:, :, :]
        bs = slice(b * T, (b + 1) * T)
        pair = [M.at(A1_T, P), M.at(A1_T + P, P)]
        kn = [M.at(A1_K, 512), M.at(A1_K + 512, 512), M.at(A1_SQ + 1024, 512)]
        with nc.Block(no_gpsimd_drain=True) as block:
            @block.sync
            def _(sp):
                sp.dma_start(seen, batch_seen(b).broadcast_to((P, S))).then_inc(cseen.sem, 16)

            @block.vector
            def _(dve):
                link = Chain(dve, chain_c)
                dve.wait_ge(rows_in.sem, rows_in.at(64))
                for j in range(NT):
                    ins = dve.bn_stats(M.row8[:, 6 * j:6 * j + 6], ctx3[:, j, :])
                link(ins)
                for j in range(NT):
                    ins = dve.bn_aggr(st[:, 2 * j:2 * j + 2], M.row8[:, 6 * j:6 * j + 6])
                link(ins)
                stv = st[:, 0:26].rearrange("p (j k) -> p k j", k=2)
                dve.tensor_scalar(st[:, 32:45], stv[:, 1, :], EPS, None, ALU.add).then_inc(cvar.sem, 1)
                dve.wait_ge(cseen.sem, cseen.at(16))
                link(dve.tensor_scalar(mask[:, 0:S], seen, -GONE, GONE, ALU.mult, ALU.add))
                link(dve.memset(mask[:, S:WIDE], 0.0))
                link(dve.tensor_copy(rows[0:T, 13, :], lat[bs, :]))
                dve.wait_ge(crstd.sem, crstd.at(1))
                r3 = rows[:, 0:NT, :]
                for j in range(NT - 1):
                    dve.tensor_scalar(rows[:, j, :], ctx3[:, j, :], st[:, 2 * j:2 * j + 1], st[:, 48 + j:49 + j],
                                      ALU.subtract, ALU.mult)
                link(dve.tensor_scalar(rows[:, NT - 1, :], ctx3[:, NT - 1, :], st[:, 2 * NT - 2:2 * NT - 1],
                                       st[:, 60:61], ALU.subtract, ALU.mult))
                link(dve.tensor_tensor(r3, r3, M.w("x1_ctx_w").unsqueeze(1).broadcast_to((P, NT, P)), ALU.mult))
                link(dve.tensor_tensor(r3, r3, M.w("x1_ctx_b").unsqueeze(1).broadcast_to((P, NT, P)), ALU.add))
                link.end()

            @block.gpsimd
            def _(pool):
                pool.wait_ge(cvar.sem, cvar.at(1))
                pool.tensor_tensor(st[:, 48:61], st[:, 32:45], M.w("neg_half")[:, 0:13], ALU.pow).then_inc(crstd.sem, 1)
        cvar.passed(1)
        cseen.passed(16)
        crstd.passed(1)
        with nc.Block(no_gpsimd_drain=True) as block:
            NK = len(KV_TILES)
            sqb = [M.at(A1_SQ, 512), M.at(A1_SQ + 512, 512)]
            banks = [M.psB, M.psC, M.psD]

            @block.tensor
            def _(pe):
                for j in range(NK + 2):
                    if j == 0:
                        pe.transpose(M.psA[:, 0:KV_TILES[0][1]], rows[:, 0, :], M.w("ident")).then_inc(ct.sem, 1)
                    if j < NK:
                        m = KV_TILES[j][1]
                        pe.wait_ge(cm.sem, cm.at(j + 1))
                        if j >= 3:
                            pe.wait_ge(ckn.sem, ckn.at(j - 2))
                        pe.matmul(banks[j % 3][0:m, :], pair[j % 2][:, 0:m], M.w("x1_wk"), start=True,
                                  stop=True).then_inc(ck.sem, 1)
                    if j + 1 < NK:
                        m = KV_TILES[j + 1][1]
                        pe.transpose(M.psA[:, 0:m], rows[0:m, j + 1, :], M.w("ident")[0:m, 0:m]).then_inc(ct.sem, 1)
                    if j >= 2:
                        i = j - 2
                        a, m = KV_TILES[i]
                        pe.wait_ge(ckn.sem, ckn.at(i + 1))
                        if i >= 2:
                            pe.wait_ge(ckm.sem, ckm.at(i - 1))
                        for c in range(4):
                            mm = pe.transpose(M.psS[:, 512 * (i % 2) + P * c:512 * (i % 2) + P * c + m],
                                              kn[i % 3][0:m, P * c:P * (c + 1)], M.w("ident")[0:m, 0:m])
                        mm.then_inc(ckt.sem, 1)

            @block.scalar
            def _(act):
                def move_rows(j):
                    m = KV_TILES[j][1]
                    act.wait_ge(ct.sem, ct.at(j + 1))
                    if j >= 2:
                        act.wait_ge(ck.sem, ck.at(j - 1))
                    act.activation(pair[j % 2][:, 0:m], M.psA[:, 0:m], ACT.Copy).then_inc(cm.sem, 1)

                move_rows(0)
                for j in range(NK + 2):
                    if j + 1 < NK:
                        move_rows(j + 1)
                    if j < NK:
                        m = KV_TILES[j][1]
                        act.wait_ge(ck.sem, ck.at(j + 1))
                        if j >= 2:
                            act.wait_ge(cn2.sem, cn2.at(j - 1))
                        act.activation(sqb[j % 2][0:m, :], banks[j % 3][0:m, :], ACT.Square).then_inc(csq.sem, 1)
                    if j >= 2:
                        a, m = KV_TILES[j - 2]
                        act.wait_ge(ckt.sem, ckt.at(j - 1))
                        src = M.psS[:, 512 * (j % 2):512 * (j % 2) + 512].rearrange("p (c s) -> p c s", s=P)
                        act.activation(kT[:, :, a:a + m], src[:, :, 0:m], ACT.Copy).then_inc(ckm.sem, 1)

            @block.gpsimd
            def _(pool):
                for j in range(NK):
                    m = KV_TILES[j][1]
                    s_ = 16 * (j % 3)
                    pool.wait_ge(cn2.sem, cn2.at(j + 1))
                    if j >= 3:
                        pool.wait_ge(ckn.sem, ckn.at(j - 2))
                    pool.tensor_tensor(st[0:m, s_ + 8:s_ + 16], st[0:m, s_:s_ + 8], M.w("neg_half")[0:m, 0:8],
                                       ALU.pow).then_inc(crn.sem, 1)

            @block.vector
            def _(dve):
                link = Chain(dve, chain_c)
                for j in range(NK + 1):
                    if j < NK:
                        m = KV_TILES[j][1]
                        s_ = 16 * (j % 3)
                        dve.wait_ge(csq.sem, csq.at(j + 1))
                        if j >= 3:
                            dve.wait_ge(crn.sem, crn.at(j - 2))
                        link(dve.tensor_reduce(st[0:m, s_:s_ + 8],
                                               sqb[j % 2][0:m, :].rearrange("p (h d) -> p h d", d=64), AX.X, ALU.add))
                        dve.tensor_scalar(st[0:m, s_:s_ + 8], st[0:m, s_:s_ + 8], 1e-24, None,
                                          ALU.max).then_inc(cn2.sem, 1)
                    if j >= 1:
                        i = j - 1
                        m = KV_TILES[i][1]
                        s_ = 16 * (i % 3)
                        dve.wait_ge(crn.sem, crn.at(i + 1))
                        if i >= 3:
                            dve.wait_ge(ckt.sem, ckt.at(i - 2))
                        dve.tensor_tensor(kn[i % 3][0:m, :].rearrange("p (h d) -> p h d", d=64),
                                          banks[i % 3][0:m, :].rearrange("p (h d) -> p h d", d=64),
                                          st[0:m, s_ + 8:s_ + 16].unsqueeze(2).broadcast_to((m, 8, 64)),
                                          ALU.mult).then_inc(ckn.sem, 1)
                link.end()
        for c in (ct, cm, ck, csq, cn2, crn, ckn, ckt, ckm):
            c.passed(NK)

        def keep_rows(dve, link, u):
            return dve.tensor_copy(UT[:, 2 * u:2 * u + 2, bs], M.psD[:, 0:P].rearrange("p (h t) -> p h t", t=T))

        if b == 0:
            keep = M.count("x1_lat_kept")
            with nc.Block(no_gpsimd_drain=True) as block:
                @block.vector
                def _(dve):
                    dve.tensor_copy(M.xn[:, :], lat).then_inc(keep.sem, 1)
            keep.passed(1)
            lat = M.xn[:, :]
        attend(nc, M, units=4, rows=P, tiles=KV_TILES, subs=1,
               queries=lambda u, s: qb[:, b, u, :],
               keys=lambda u, a, m: kT[:, u, a:a + m],
               values=lambda u, j: rows[0:KV_TILES[j][1], j, :],
               bufs=[M.at(a, 1792) for a in A1_BUF], pt=M.at(A1_PT, 14 * P), consume=keep_rows, bias=lambda u: mask)

    done, var, rstd = (M.count("x1o_" + k) for k in ("projected", "var", "rstd"))
    y = M.at(A1_LAT, P)
    with nc.Block(no_gpsimd_drain=True) as block:
        @block.tensor
        def _(pe):
            for h in range(8):
                mm = pe.matmul(M.psA[:, 0:P], UT[:, h, :], M.w("x1_vo")[:, P * h:P * (h + 1)], start=(h == 0),
                               stop=(h == 7))
            mm.then_inc(done.sem, 1)

        @block.vector
        def _(dve):
            link = Chain(dve, chain_c)
            dve.wait_ge(done.sem, done.at(1))
            link(dve.bn_stats(M.stat[:, 0:6], M.psA[:, 0:P]))
            link(dve.bn_aggr(M.stat[:, 6:8], M.stat[:, 0:6]))
            dve.tensor_scalar(M.stat[:, 8:9], M.stat[:, 7:8], EPS, None, ALU.add).then_inc(var.sem, 1)
            dve.wait_ge(rstd.sem, rstd.at(1))
            link(dve.tensor_scalar(y, M.psA[:, 0:P], M.stat[:, 6:7], M.stat[:, 9:10], ALU.subtract, ALU.mult))
            link(dve.tensor_tensor(y, y, M.w("x1_out_w"), ALU.mult))
            link(dve.tensor_tensor(y, y, M.w("x1_out_b"), ALU.add))
            link(dve.tensor_tensor(M.x[:, :], M.x[:, :], y, ALU.add))
            link.end()

        @block.gpsimd
        def _(pool):
            pool.wait_ge(var.sem, var.at(1))
            pool.tensor_tensor(M.stat[:, 9:10], M.stat[:, 8:9], M.w("neg_half")[:, 0:1], ALU.pow).then_inc(rstd.sem, 1)
    for c in (done, var, rstd):
        c.passed(1)


def recurrence(nc, M):
    proj, shifted, expd, scanned, turned = (
        M.count("rc_" + k) for k in ("projected", "shifted", "exponential", "scanned", "turned"))
    chain_c = M.count("rc_dve_chain")
    z, inj, out = M.at(0, P), M.at(P, P), M.at(2 * P, P)
    with nc.Block(no_gpsimd_drain=True) as block:
        @block.tensor
        def _(pe):
            pe.matmul(M.psA[:, 0:P], M.w("rc_wd"), M.xnT[:, :], start=True, stop=True)
            pe.matmul(M.psA[:, P:2 * P], M.w("rc_wi"), M.xnT[:, :], start=True, stop=True).then_inc(proj.sem, 1)
            pe.wait_ge(scanned.sem, scanned.at(1))
            pe.transpose(M.psB[:, 0:P], out, M.w("ident")).then_inc(turned.sem, 1)

        @block.scalar
        def _(act):
            act.wait_ge(shifted.sem, shifted.at(1))
            act.activation(z, z, ACT.Exp, scale=-1.0).then_inc(expd.sem, 1)

        @block.vector
        def _(dve):
            link = Chain(dve, chain_c)
            dve.wait_ge(proj.sem, proj.at(1))
            dve.tensor_scalar(z, M.psA[:, 0:P], M.w("rc_bd"), None, ALU.add).then_inc(shifted.sem, 1)
            link(dve.tensor_scalar(inj, M.psA[:, P:2 * P], M.w("rc_bi"), None, ALU.add))
            dve.wait_ge(expd.sem, expd.at(1))
            link(dve.tensor_scalar(z, z, 1.0, None, ALU.add))
            link(dve.reciprocal(z, z))
            link(dve.tensor_tensor_scan(out[:, 0:T], z[:, 0:T], inj[:, 0:T], 0.0, ALU.mult, ALU.add))
            dve.tensor_tensor_scan(out[:, T:P], z[:, T:P], inj[:, T:P], 0.0, ALU.mult, ALU.add).then_inc(scanned.sem, 1)
            dve.wait_ge(turned.sem, turned.at(1))
            dve.tensor_tensor(M.x[:, :], M.x[:, :], M.psB[:, 0:P], ALU.add)
            link.end()
    for c in (proj, shifted, expd, scanned, turned):
        c.passed(1)


A3_BUF = [0, 1664]
A3_PT, A3_Q, A3_UT, A3_MASKS = 3328, 4992, 7040, 9088
A3_MASKED = A3_MASKS + 4 * S
assert A3_MASKED + 2 * ((S + 3) // 4) <= ARENA


def fold_queries(nc, M, weights, heads, qp, beside=None):
    done = M.count("fold_queries")
    with nc.Block(no_gpsimd_drain=True) as block:
        if beside is not None:
            beside(block)

        @block.tensor
        def _(pe):
            for h in range(heads):
                mm = pe.matmul(M.psS[:, h * P:(h + 1) * P], weights[:, h * P:(h + 1) * P], M.xnT[:, :],
                               start=True, stop=True)
            mm.then_inc(done.sem, 1)

        @block.scalar
        def _(act):
            act.wait_ge(done.sem, done.at(1))
            act.activation(qp.rearrange("p (b h t) -> p h b t", b=2, t=T),
                           M.psS[:, 0:heads * P].rearrange("p (h b t) -> p h b t", b=2, t=T), ACT.Copy)
    done.passed(1)


def cross2(nc, M):
    qp, UT = M.at(A3_Q, P), M.at(A3_UT, P)
    fold_queries(nc, M, M.w("x2_qk"), 1, qp)
    attend(nc, M, units=2, rows=T, tiles=CTX_TILES, subs=1,
           queries=lambda u, s: qp[:, u * T:(u + 1) * T], keys=lambda u, a, m: M.ctxT[u][:, a:a + m],
           values=lambda u, j: M.ctxN[u][0:CTX_TILES[j][1], j, :],
           bufs=[M.at(a, 1664) for a in A3_BUF], pt=M.at(A3_PT, 1664),
           consume=lambda dve, link, u: dve.tensor_copy(UT[:, u * T:(u + 1) * T], M.psD[:, 0:T]))
    project_out(nc, M, "x2", [(UT, M.w("x2_wv"))])


def cross3(nc, M, batch_masked):
    qp = M.at(A3_Q, H * P)
    UT = M.at(A3_UT, H * P).rearrange("p (h t) -> p h t", t=P)
    loaded = [M.count(f"x3_mask{b}_loaded") for b in range(2)]
    keep, gone = ([M.at(A3_MASKS + (2 * k + b) * S, S) for b in range(2)] for k in range(2))
    masked = [M.at(A3_MASKED + b * ((S + 3) // 4), (S + 3) // 4).bitcast(U8)[:, 0:S] for b in range(2)]

    def load_masks(block):
        @block.sync
        def _(sp):
            for b in range(2):
                for h in range(2):
                    sp.dma_start(masked[b][h * T:(h + 1) * T], batch_masked(b)).then_inc(loaded[b].sem, 16)

        @block.vector
        def _(dve):
            for b in range(2):
                dve.wait_ge(loaded[b].sem, loaded[b].at(32))
                dve.tensor_scalar(keep[b], masked[b], -1.0, 1.0, ALU.mult, ALU.add)
                dve.tensor_scalar(gone[b], masked[b], -8e9, None, ALU.mult)
    fold_queries(nc, M, M.w("x3_qk"), H, qp, beside=load_masks)
    for c in loaded:
        c.passed(32)

    def keep_rows(dve, link, u):
        b, p = u // 8, u % 8
        return dve.tensor_copy(UT[:, 2 * p:2 * p + 2, b * T:(b + 1) * T],
                               M.psD[:, 0:P].rearrange("p (h t) -> p h t", t=T))

    attend(nc, M, units=16, rows=P, tiles=CTX_TILES, subs=1,
           queries=lambda u, s: qp[:, u * P:(u + 1) * P], keys=lambda u, a, m: M.ctxT[u // 8][:, a:a + m],
           values=lambda u, j: M.ctxN[u // 8][0:CTX_TILES[j][1], j, :],
           bufs=[M.at(a, 1664) for a in A3_BUF], pt=M.at(A3_PT, 1664), consume=keep_rows,
           bias=lambda u: gone[u // 8], keep=lambda u: keep[u // 8], scale=0.125)
    vo = M.w("x3_vo")
    project_out(nc, M, "x3", [(UT[:, h, :], vo[:, P * h:P * (h + 1)]) for h in range(H)])


def quantised(nc, M):
    low, low_moved, done = (M.count("qf_" + k) for k in ("low_rank", "low_rank_moved", "done"))
    chain_c = M.count("qf_dve_chain")
    xa = M.at(0, P, 16)
    with nc.Block(no_gpsimd_drain=True) as block:
        @block.tensor
        def _(pe):
            pe.matmul(M.psB[0:16, 0:P], M.w("qf_a"), M.xnT[:, :], start=True, stop=True).then_inc(low.sem, 1)
            pe.matmul(M.psA[:, 0:P], M.xnT[:, :], M.w("qf_w"), start=True, stop=False)
            pe.wait_ge(low_moved.sem, low_moved.at(1))
            pe.matmul(M.psA[:, 0:P], xa, M.w("qf_b", 16), start=False, stop=True).then_inc(done.sem, 1)

        @block.vector
        def _(dve):
            link = Chain(dve, chain_c)
            link(dve.tensor_tensor(M.x[:, :], M.x[:, :], M.w("qf_bias"), ALU.add))
            dve.wait_ge(low.sem, low.at(1))
            dve.tensor_copy(xa, M.psB[0:16, 0:P]).then_inc(low_moved.sem, 1)
            dve.wait_ge(done.sem, done.at(1))
            dve.tensor_tensor(M.x[:, :], M.x[:, :], M.psA[:, 0:P], ALU.add)
            link.end()
    for c in (low, low_moved, done):
        c.passed(1)


def prepare(nc, M, blob, folds):
    loaded, folded, moved, exps, absmax, allmax, half = (
        M.count("pr_" + k) for k in ("loaded", "folded", "moved", "exponentials", "absmax", "allmax", "dots"))
    chain_c = M.count("pr_dve_chain")
    n_blob = blob.shape[1]
    cols = folds.shape[1]
    fold = M.at(0, cols)
    q3, k3, v3, o3, v1, o1 = (fold[0:64, a:b] for a, b in (
        (0, 2048), (2048, 4096), (4096, 6144), (6144, 8192), (8192, 9216), (9216, 10240)))
    jobs = [(q3, k3, M.w("x3_qk"), H), (v3, o3, M.w("x3_vo"), H), (v1, o1, M.w("x1_vo"), 8)]
    with nc.Block(no_gpsimd_drain=True) as block:
        @block.sync
        def _(sp):
            sp.dma_start(fold, folds).then_inc(loaded.sem, 16)
            sp.dma_start(M.weights[:, 0:n_blob], blob).then_inc(loaded.sem, 16)

        @block.tensor
        def _(pe):
            pe.wait_ge(loaded.sem, loaded.at(32))
            for i, (lhs, rhs, _, heads) in enumerate(jobs):
                if i:
                    pe.wait_ge(moved.sem, moved.at(i))
                for h in range(heads):
                    c = slice(h * P, (h + 1) * P)
                    mm = pe.matmul(M.psS[:, c], lhs[:, c], rhs[:, c], start=True, stop=True)
                mm.then_inc(folded.sem, 1)
            pe.matmul(M.psA[:, 0:P], fold[:, 10240:10240 + P], fold[:, 10240 + P:10240 + 2 * P], start=True,
                      stop=True).then_inc(folded.sem, 1)

        @block.scalar
        def _(act):
            for i, (_, _, dst, heads) in enumerate(jobs):
                act.wait_ge(folded.sem, folded.at(i + 1))
                act.activation(dst, M.psS[:, 0:heads * P], ACT.Copy).then_inc(moved.sem, 1)
            act.wait_ge(folded.sem, folded.at(4))
            act.activation(M.w("x2_qk"), M.psA[:, 0:P], ACT.Copy)
            act.wait_ge(half.sem, half.at(1))
            act.activation(M.small[:, 2:4], M.small[:, 0:2], ACT.Exp).then_inc(exps.sem, 1)

        @block.gpsimd
        def _(pool):
            pool.wait_ge(absmax.sem, absmax.at(1))
            pool.partition_all_reduce(M.small[:, 9:10], M.small[:, 8:9], P, bass.bass_isa.ReduceOp.max).then_inc(allmax.sem, 1)

        @block.vector
        def _(dve):
            link = Chain(dve, chain_c)
            for b in range(2):
                link(dve.memset(M.ctxN[b][:, NT - 1, :], 0.0))
            dve.wait_ge(loaded.sem, loaded.at(32))
            lam = M.w("x0_lambda").rearrange("p (a b d) -> p a b d", a=2, b=2)
            link(dve.tensor_tensor(M.small[:, 16:24].rearrange("p (a d) -> p a d", a=2), lam[:, :, 0, :],
                                   lam[:, :, 1, :], ALU.mult))
            dve.tensor_reduce(M.small[:, 0:2], M.small[:, 16:24].rearrange("p (a d) -> p a d", a=2), AX.X,
                              ALU.add).then_inc(half.sem, 1)
            dve.wait_ge(exps.sem, exps.at(1))
            link(dve.tensor_tensor(M.small[:, 4:5], M.small[:, 3:4], M.small[:, 2:3], ALU.subtract))
            link(dve.tensor_scalar(M.lam[:, :], M.small[:, 4:5], LAMBDA_INIT, None, ALU.subtract))
            w = M.w("qf_w")
            dve.tensor_reduce(M.small[:, 8:9], w, AX.X, ALU.max, apply_absolute_value=True).then_inc(absmax.sem, 1)
            dve.wait_ge(allmax.sem, allmax.at(1))
            link(dve.tensor_scalar(M.small[:, 10:11], M.small[:, 9:10], 1.0 / 7.0, None, ALU.mult))
            link(dve.reciprocal(M.small[:, 11:12], M.small[:, 10:11]))
            half_ulp = 1.5 * 2.0 ** 23
            link(dve.tensor_scalar(w, w, M.small[:, 11:12], half_ulp, ALU.mult, ALU.add))
            link(dve.tensor_scalar(w, w, half_ulp, 7.0, ALU.subtract, ALU.min))
            link(dve.tensor_scalar(w, w, -8.0, M.small[:, 10:11], ALU.max, ALU.mult))
            link.end()
    loaded.passed(32)
    folded.passed(4)
    moved.passed(3)
    for c in (exps, absmax, allmax, half):
        c.passed(1)


def load_pair(nc, M, i, A):
    x_in, rows_in = M.count("x_loaded"), M.count("ctx_rows_loaded")
    with nc.Block(no_gpsimd_drain=True) as block:
        @block.sync
        def _(sp):
            sp.dma_start(M.x[:, :], A["x"][bass.ds(i, 1)].rearrange("o t d -> (o t) d")).then_inc(x_in.sem, 16)
            for b in range(2):
                sp.dma_start(M.ctxT[b][:, :], A["ctxT"][bass.ds(2 * i + b, 1)].rearrange("o d s -> (o d) s")).then_inc(
                    M.count(f"ctx_cols{b}_loaded").sem, 16)
            for b in range(2):
                ctx = A["ctx"][bass.ds(2 * i + b, 1)].rearrange("o s d -> (o s) d")
                sp.dma_start(M.ctxN[b][:, 0:12, :], ctx[0:12 * P].rearrange("(j p) d -> p j d", p=P)).then_inc(rows_in.sem, 16)
                sp.dma_start(M.ctxN[b][0:TAIL, 12, :], ctx[12 * P:S]).then_inc(rows_in.sem, 16)
            sp.wait_ge(x_in.sem, x_in.at(16))
    x_in.passed(16)


def store_pair(nc, M, i, out):
    stored = M.count("pair_stored")
    with nc.Block(no_gpsimd_drain=True) as block:
        @block.sync
        def _(sp):
            sp.dma_start(out[bass.ds(i, 1)].rearrange("o t d -> (o t) d"), M.x[:, :]).then_inc(stored.sem, 16)
            sp.wait_ge(stored.sem, stored.at(16))
            sp.wait_ge(M.count("ctx_rows_loaded").sem, 64)
            for b in range(2):
                sp.wait_ge(M.count(f"ctx_cols{b}_loaded").sem, 16)
    stored.passed(16)


def restart(nc, M):
    for c in M.counts.values():
        nc.gpsimd.sem_clear(c.sem)
        c.base = 0
    nc.all_engine_barrier(sem_only=True)


def program(nc, A, regions, out, upto=12):
    with ExitStack() as ctx:
        M = Machine(nc, ctx, regions, None)
        M.lam = M.sbuf("lambda_share", [P, 1])
        prepare(nc, M, A["weights"], A["folds"])
        restart(nc, M)

        def wide(name):
            return lambda e, c: M.w(name)[:, 512 * e + P * c:512 * e + P * (c + 1)]

        def first(k):
            return lambda e, c: M.at(EXPERTS0 + 2048 * k + 512 * e + P * c, P)

        layers = [
            lambda i: cross0(nc, M),
            lambda i: self_attention(nc, M, "a0", rope="0", biased=False, causal=False, scale=1.0,
                                     experts0=A["experts0"]),
            lambda i: experts(nc, M, "m0", E=4, kind="silu", up=first(0), up3=first(1), down=first(2),
                            router=M.w("m0_router"), router_bias=M.w("m0_router_b")),
            lambda i: cross1(nc, M, lambda b: A["seen"][bass.ds(2 * i + b, 1)]),
            lambda i: recurrence(nc, M),
            lambda i: experts(nc, M, "m1", E=8, kind="relu", up=wide("m1_up"), up3=None, down=wide("m1_down"),
                            router=M.w("m1_router"), b1=M.w("m1_b1"), b2=M.w("m1_b2", 8), floor=1e-9),
            lambda i: cross2(nc, M),
            lambda i: self_attention(nc, M, "a2", rope="1", biased=True, causal=True, scale=1.0 / math.sqrt(HD)),
            lambda i: experts(nc, M, "m2", E=8, kind="gelu", up=wide("m2_up"), up3=None, down=wide("m2_down"),
                            router=M.w("m2_router"), b1=M.w("m2_b1"), b2=M.w("m2_b2", 8), by_batch=True),
            lambda i: cross3(nc, M, lambda b: A["masked"][bass.ds(2 * i + b, 1)].rearrange("o t s -> (o t) s")),
            lambda i: self_attention(nc, M, "a3", biased=True, causal=True, scale=1.0 / math.sqrt(HD), top=32),
            lambda i: quantised(nc, M),
        ]
        with nc.Fori(0, A["x"].shape[0]) as i:
            load_pair(nc, M, i, A)
            for n, layer in enumerate(layers[:upto]):
                layer_norm(nc, M)
                layer(i)
            store_pair(nc, M, i, out)
            restart(nc, M)


def layout(w):
    import numpy as np
    T_ = lambda a: np.ascontiguousarray(np.asarray(a).T)
    row = lambda a, p=P: np.broadcast_to(np.asarray(a)[None, :], (p, np.asarray(a).shape[0]))
    col = lambda a: np.asarray(a)[:, None]
    idx = np.arange(P)
    swap0 = (idx // HD) * HD + (idx % HD ^ 1)
    swap1 = (idx // HD) * HD + (idx % HD + HD // 2) % HD
    qkv0 = np.asarray(w["L0_attn_w_qkv"]).reshape(H, 3, HD, P)
    wq0, wk0, wv0 = (qkv0[:, j].reshape(P, P) for j in range(3))
    ip, ib = np.asarray(w["L0_xattn_in_proj_weight"]), np.asarray(w["L0_xattn_in_proj_bias"])
    up = lambda a: np.asarray(a).transpose(1, 0, 2).reshape(P, -1)
    down = lambda a: np.asarray(a).reshape(-1, 4, P, P).transpose(2, 0, 1, 3).reshape(P, -1)
    b1 = lambda a: np.asarray(a).reshape(8, 4, P).transpose(2, 0, 1).reshape(P, 32)
    head_t = lambda a, h: np.asarray(a).reshape(P, h, 64).transpose(2, 1, 0).reshape(64, -1)
    head_r = lambda a, h: np.asarray(a).reshape(h, 64, P).transpose(1, 0, 2).reshape(64, -1)
    wkv = np.asarray(w["L1_xattn_Wkv"])
    blocks = dict(constants())
    blocks.update({
        "x0_wq": T_(ip[0:P]), "x0_wk": T_(ip[P:2 * P]), "x0_wv": T_(ip[2 * P:]), "x0_wo": T_(w["L0_xattn_out_proj_weight"]),
        "x0_bq": col(ib[0:P]), "x0_bk": col(ib[P:2 * P]), "x0_bv": row(ib[2 * P:]),
        "x0_bo": row(w["L0_xattn_out_proj_bias"]),
        "x0_lambda": np.concatenate([row(w["L0_xattn_lambda_" + k]) for k in ("q1", "k1", "q2", "k2")], axis=1),
        "a0_wq": T_(wq0), "a0_wk": T_(wk0), "a0_wv": T_(wv0), "a0_wq_turned": T_(wq0[swap0]),
        "a0_wk_turned": T_(wk0[swap0]), "a0_wo": T_(w["L0_attn_w_out"]),
        "m0_router": w["L0_ffn_router_w"], "m0_router_b": row(w["L0_ffn_router_b"]),
        "x1_ctx_w": row(w["L1_xattn_ln_x_w"]), "x1_ctx_b": row(w["L1_xattn_ln_x_b"]),
        "x1_lat_w": row(w["L1_xattn_ln_l_w"]), "x1_lat_b": row(w["L1_xattn_ln_l_b"]),
        "x1_wq": w["L1_xattn_Wq"], "x1_wk": wkv[:, 0:512],
        "x1_q_scale": row(w["L1_xattn_q_scale"]), "x1_k_scale": row(w["L1_xattn_k_scale"]),
        "x1_out_w": row(w["L1_xattn_ln_o_w"]), "x1_out_b": row(w["L1_xattn_ln_o_b"]),
        "rc_wd": T_(w["L1_attn_W_decay"]), "rc_wi": T_(w["L1_attn_W_input"]),
        "rc_bd": col(w["L1_attn_b_decay"]), "rc_bi": col(w["L1_attn_b_input"]),
        "m1_router": T_(w["L1_ffn_router_w"]), "m1_up": up(np.asarray(w["L1_ffn_w1"]).transpose(0, 2, 1)),
        "m1_down": down(np.asarray(w["L1_ffn_w2"]).transpose(0, 2, 1)), "m1_b1": b1(w["L1_ffn_b1"]),
        "m1_b2": w["L1_ffn_b2"],
        "x2_wv": T_(w["L2_xattn_Wv"]),
        "m2_router": w["L2_ffn_gate_w"], "m2_up": up(w["L2_ffn_w1"]), "m2_down": down(w["L2_ffn_w2"]),
        "m2_b1": b1(w["L2_ffn_b1"]), "m2_b2": w["L2_ffn_b2"],
        "qf_w": w["L3_ffn_kernel"], "qf_a": w["L3_ffn_a"], "qf_b": w["L3_ffn_b"], "qf_bias": row(w["L3_ffn_bias"]),
    })
    for n, L in (("a2", "L2_attn_"), ("a3", "L3_attn_")):
        blocks.update({n + "_w" + k: T_(w[L + "W" + k]) for k in "qkvo"})
        blocks.update({n + "_b" + k: col(w[L + "b" + k]) for k in "qk"})
        blocks.update({n + "_b" + k: row(w[L + "b" + k]) for k in "vo"})
    for k in "qk":
        blocks["a2_w" + k + "_turned"] = T_(np.asarray(w["L2_attn_W" + k])[swap1])
        blocks["a2_b" + k + "_turned"] = col(np.asarray(w["L2_attn_b" + k])[swap1])
    regions, a = {}, 0
    for name, block in blocks.items():
        regions[name] = (a, np.asarray(block).shape[1])
        a += np.asarray(block).shape[1]
    blob = np.zeros((P, a), np.float32)
    for name, block in blocks.items():
        block = np.asarray(block)
        s, n = regions[name]
        blob[0:block.shape[0], s:s + n] = block
    for name, n in (("x3_qk", H * P), ("x3_vo", H * P), ("x1_vo", 8 * P), ("x2_qk", P)):
        regions[name] = (a, n)
        a += n
    narrow = np.concatenate([head_t(w["L3_xattn_W_Q"], H), head_t(w["L3_xattn_W_K"], H), head_t(w["L3_xattn_W_V"], H),
                             head_r(w["L3_xattn_W_O"], H), head_t(wkv[:, 512:], 8), head_r(w["L1_xattn_Wo"], 8)], axis=1)
    folds = np.zeros((P, narrow.shape[1] + 2 * P), np.float32)
    folds[0:64, 0:narrow.shape[1]] = narrow
    folds[:, narrow.shape[1]:] = np.concatenate([w["L2_xattn_Wq"], w["L2_xattn_Wk"]], axis=1)
    experts0 = np.concatenate([up(w["L0_ffn_w1"]), up(w["L0_ffn_w3"]), down(w["L0_ffn_w2"])], axis=1)
    return regions, blob, folds, experts0


UPTO = 12


def kernel(**inputs):
    import numpy as np
    import concourse.bacc as bacc
    from concourse import mybir
    from concourse.bass_utils import run_bass_kernel_spmd

    w = {k: np.asarray(v) for k, v in inputs.items()}
    regions, blob, folds, experts0 = layout(w)
    ctx = w["ctx_1024"]
    n = w["x"].shape[0] // 2
    arrays = {
        "x": np.ascontiguousarray(w["x"].reshape(n, P, P)),
        "ctx": ctx, "ctxT": np.ascontiguousarray(ctx.transpose(0, 2, 1)),
        "seen": w["mask_BxS2_bk0"], "masked": w["mask_BxSxS2_bk1"],
        "weights": blob, "folds": folds, "experts0": experts0,
    }
    nc = bacc.Bacc("TRN2", target_bir_lowering=False, num_devices=1)
    A = {k: nc.dram_tensor("in_" + k, v.shape, mybir.dt.from_np(v.dtype), kind="ExternalInput").ap()
         for k, v in arrays.items()}
    out = nc.dram_tensor("out", (n, P, P), mybir.dt.float32, kind="ExternalOutput").ap()
    program(nc, A, regions, out, UPTO)
    r = run_bass_kernel_spmd(nc, [{"in_" + k: np.ascontiguousarray(v) for k, v in arrays.items()}], core_ids=[0])
    return r.results[0]["out"].reshape(2 * n, T, P)
```

```python
import math
from contextlib import ExitStack

import numpy as np

import concourse.bass as bass
from concourse import mybir

F32 = mybir.dt.float32
U8 = mybir.dt.uint8
BF16 = mybir.dt.bfloat16
ACT = mybir.ActivationFunctionType
ALU = mybir.AluOpType
AX = mybir.AxisListType

P = 128
B, T, S = 16, 64, 1601
H, HD = 16, 8
NT = 13
TAIL = S - 12 * P
EPS = 1e-5
LAMBDA_INIT = 0.2
GONE = -1e30

CTX_TILES = [(P * j, P) for j in range(12)] + [(12 * P, TAIL)]
KV_TILES = CTX_TILES + [(S, T)]


def rotations():
    f = np.float32
    row = np.arange(P) % HD
    tok = np.arange(P) % T
    theta0 = np.power(f(10000.0), (f(2.0) * (row // 2).astype(f) / f(HD)).astype(f)).astype(f)
    ang0 = (tok.astype(f)[None, :] / theta0[:, None]).astype(f)
    sign0 = np.where(row % 2 == 0, -1, 1).astype(f)[:, None]
    half = HD // 2
    theta1 = (f(1.0) / np.power(f(10000.0), (2 * (row % half)).astype(f) / f(HD)).astype(f)).astype(f)
    ang1 = ((tok + 1).astype(f)[None, :] * theta1[:, None]).astype(f)
    sign1 = np.where(row < half, -1, 1).astype(f)[:, None]
    return (np.cos(ang0), np.sin(ang0) * sign0, np.cos(ang1), np.sin(ang1) * sign1)


def constants():
    f = np.float32
    row = np.arange(P)
    cos0, sin0, cos1, sin1 = rotations()
    head = (row[:, None] // HD == np.arange(H)[None, :]).astype(f)
    c = np.arange(4)
    sub = ((row[:, None] % 16) // (HD // 2) == (2 * (c % 2) + c // 2)[None, :]).astype(f)
    t = row % T
    causal = np.where(np.arange(T)[None, :] <= t[:, None], 0.0, GONE).astype(f)
    same = (row[:, None] // T == row[None, :] // T).astype(f) / f(T)
    return {
        "ident": np.eye(P, dtype=f), "head_mask": head, "sub_mask": sub, "causal": causal,
        "batch_mean": same, "neg_half": np.full((P, 16), -0.5, f),
        "row_places": (row[:, None] % 16 == row[None, :] % 16).astype(f),
        "pair_mask": (row[:, None] // 16 == np.arange(8)[None, :]).astype(f),
        "same_token": (t[:, None] == np.arange(T)[None, :]).astype(f),
        "cos0": cos0, "sin0": sin0, "cos1": cos1, "sin1": sin1,
    }


class Count:

    def __init__(self, sem):
        self.sem, self.base = sem, 0

    def at(self, n):
        return self.base + n

    def passed(self, n):
        self.base += n


class Chain:

    def __init__(self, engine, count):
        self.engine, self.count, self.n = engine, count, 0

    def __call__(self, ins):
        self.n += 1
        ins.then_inc(self.count.sem, 1)
        self.engine.wait_ge(self.count.sem, self.count.at(self.n))

    def end(self):
        self.count.passed(self.n)


class Machine:

    def __init__(self, nc, ctx, regions):
        self.nc, self.ctx = nc, ctx
        self.counts = {}
        self.regions = regions
        sb, ps = self.sbuf, self.psum
        self.weights = sb("weights", [P, max(a + n for a, n in regions.values())])
        self.lam = sb("lambda_share", [P, 1])
        self.x = sb("x_state", [P, P])
        self.x_next = sb("x_next_pair", [P, P])
        self.xn = sb("x_normed", [P, P])
        self.xnT = sb("x_normed_T", [P, P])
        self.stat = sb("stat", [P, 16])
        self.small = sb("small", [P, 64])
        self.row8 = sb("row_numbers", [P, 96])
        self.ctxN = [sb(f"ctx_rows{b}", [P, NT, P]) for b in range(2)]
        self.ctxT = [sb(f"ctx_cols{b}", [P, S]) for b in range(2)]
        self.arena = sb("arena", [P, ARENA])
        self.psS = ps("scores_banks", [P, 2048])
        self.psA = ps("bank_a", [P, 512])
        self.psB = ps("bank_b", [P, 512])
        self.psC = ps("bank_c", [P, 512])
        self.psD = ps("bank_d", [P, 512])

    def sbuf(self, name, shape, dt=F32):
        return self.ctx.enter_context(self.nc.sbuf_tensor(name, shape, dt))

    def psum(self, name, shape):
        return self.ctx.enter_context(self.nc.psum_tensor(name, shape, F32))

    def count(self, name):
        if name not in self.counts:
            self.counts[name] = Count(self.ctx.enter_context(self.nc.semaphore(name)))
        return self.counts[name]

    def w(self, name, rows=P):
        a, n = self.regions[name]
        return self.weights[0:rows, a:a + n]

    def at(self, start, n, rows=P):
        return self.arena[0:rows, start:start + n]


ARENA = 16768
EXPERTS0 = 10624
ONLY0 = 4 * (4 * 3 * P)


class LayerNorm:

    def __init__(self, M):
        self.M = M
        self.var, self.rstd, self.normed, self.turned, self.moved = (
            M.count(n) for n in ("ln_var", "ln_rstd", "ln_normed", "ln_turned", "ln_moved"))
        self.chain = M.count("ln_dve_chain")

    def on_vector(self, dve):
        M = self.M
        link = Chain(dve, self.chain)
        link(dve.bn_stats(M.stat[:, 0:6], M.x[:, :]))
        link(dve.bn_aggr(M.stat[:, 6:8], M.stat[:, 0:6]))
        dve.tensor_scalar(M.stat[:, 8:9], M.stat[:, 7:8], EPS, None, ALU.add).then_inc(self.var.sem, 1)
        dve.wait_ge(self.rstd.sem, self.rstd.at(1))
        dve.tensor_scalar(M.xn[:, :], M.x[:, :], M.stat[:, 6:7], M.stat[:, 9:10],
                          ALU.subtract, ALU.mult).then_inc(self.normed.sem, 1)
        link.end()

    def on_gpsimd(self, pool):
        M = self.M
        pool.wait_ge(self.var.sem, self.var.at(1))
        pool.tensor_tensor(M.stat[:, 9:10], M.stat[:, 8:9], M.w("neg_half")[:, 0:1], ALU.pow).then_inc(self.rstd.sem, 1)

    def on_tensor(self, pe):
        M = self.M
        pe.wait_ge(self.normed.sem, self.normed.at(1))
        pe.transpose(M.psA[:, 0:P], M.xn[:, :], M.w("ident")).then_inc(self.turned.sem, 1)
        pe.wait_ge(self.moved.sem, self.moved.at(1))

    def on_scalar(self, act):
        act.wait_ge(self.turned.sem, self.turned.at(1))
        act.activation(self.M.xnT[:, :], self.M.psA[:, 0:P], ACT.Copy).then_inc(self.moved.sem, 1)

    def end(self, turned=True):
        for c in (self.var, self.rstd, self.normed) + ((self.turned, self.moved) if turned else ()):
            c.passed(1)


def attend(nc, M, *, units, rows, tiles, subs, queries, keys, values, bufs, pt, consume, bias=None, keep=None,
           scale=1.0, split=None):
    width = tiles[-1][0] + tiles[-1][1]
    chunks = [list(range(4 * c, 4 * c + 4)) for c in range(3)] + [[j] for j in range(12, len(tiles))]
    NC = len(chunks)
    scores, used, negmax, probs, weights, turned, moved, weighed, consumed, formed = (
        M.count(n) for n in ("at_scores", "at_scores_used", "at_negmax", "at_probs", "at_weights", "at_turned",
                             "at_moved", "at_weighed", "at_consumed", "at_queries_formed"))
    chain_c = M.count("at_dve_chain")
    stacked = [M.count(f"at_keys_stacked{i}") for i in range(2)]
    banks = [M.psA, M.psB, M.psC]
    small = M.small

    def buf(u, s):
        return bufs[(u * subs + s) % (2 * subs)][0:rows, 0:width]

    def col(kind, u, s):
        i = 16 * kind + 2 * (u % 4) + s
        return small[0:rows, i:i + 1]

    def total(u, s):
        return M.row8[0:rows, u:u + 1] if subs == 2 and s == 0 else col(1, u, s)

    with nc.Block(no_gpsimd_drain=True) as block:
        @block.tensor
        def _(pe):
            def score(u, s):
                n = u * subs + s
                if n >= 1:
                    pe.wait_ge(used.sem, used.at(n))
                if split is not None and s == 0:
                    pe.wait_ge(formed.sem, formed.at(u + 1))
                    pe.wait_ge(stacked[u % 2].sem, stacked[u % 2].at(128 * (u // 2 + 1)))
                for a in range(0, width, 512):
                    m = min(512, width - a)
                    mm = pe.matmul(M.psS[0:rows, a:a + m], queries(u, s), keys(u, a, m), start=True, stop=True)
                mm.then_inc(scores.sem, 1)

            def turn(u):
                pe.wait_ge(weights.sem, weights.at(u + 1))
                for c, js in enumerate(chunks):
                    g = u * NC + c
                    if g >= 3:
                        pe.wait_ge(moved.sem, moved.at(g - 2))
                    for i, j in enumerate(js):
                        a, m = tiles[j]
                        mm = pe.transpose(banks[g % 3][0:m, i * P:i * P + rows], buf(u, 0)[:, a:a + m],
                                          M.w("ident")[0:rows, 0:rows])
                    mm.then_inc(turned.sem, 1)

            def weigh(u):
                if u >= 1:
                    pe.wait_ge(consumed.sem, consumed.at(u))
                for c, js in enumerate(chunks):
                    pe.wait_ge(moved.sem, moved.at(u * NC + c + 1))
                    for j in js:
                        m = tiles[j][1]
                        mm = pe.matmul(M.psD[:, 0:rows], values(u, j), pt[0:m, j * P:j * P + rows],
                                       start=(j == 0), stop=(j == len(tiles) - 1))
                mm.then_inc(weighed.sem, 1)

            for u in range(units + 2):
                if u < units:
                    score(u, 0)
                if u >= 2:
                    weigh(u - 2)
                if u < units and subs == 2:
                    score(u, 1)
                if 1 <= u <= units:
                    turn(u - 1)

        @block.scalar
        def _(act):
            def exponential(u, s):
                act.wait_ge(negmax.sem, negmax.at(u * subs + s + 1))
                act.activation(buf(u, s), buf(u, s), ACT.Exp, bias=col(0, u, s), scale=scale,
                               accum_out=total(u, s)).then_inc(probs.sem, 1)

            def move(u):
                for c, js in enumerate(chunks):
                    g = u * NC + c
                    m = tiles[js[0]][1]
                    act.wait_ge(turned.sem, turned.at(g + 1))
                    if u >= 1 and c == 0:
                        act.wait_ge(weighed.sem, weighed.at(u))
                    src = banks[g % 3][0:m, 0:len(js) * P].rearrange("p (j r) -> p j r", r=P)[:, :, 0:rows]
                    dst = pt[0:m, js[0] * P:(js[-1] + 1) * P].rearrange("p (j r) -> p j r", r=P)[:, :, 0:rows]
                    act.activation(dst, src, ACT.Copy).then_inc(moved.sem, 1)

            for u in range(units + 1):
                if u < units and subs == 2:
                    exponential(u, 0)
                if u >= 1:
                    move(u - 1)
                if u < units:
                    exponential(u, subs - 1)

        @block.vector
        def _(dve):
            link = Chain(dve, chain_c)

            def maximum(u, s):
                n = u * subs + s
                dve.wait_ge(scores.sem, scores.at(n + 1))
                if s == 0 and u >= 2:
                    dve.wait_ge(turned.sem, turned.at(NC * (u - 1)))
                if s == 1 and u >= 2:
                    dve.wait_ge(weights.sem, weights.at(u - 1))
                ps = M.psS[0:rows, 0:width]
                if keep is not None:
                    dve.tensor_tensor(buf(u, s), ps, keep(u), ALU.mult).then_inc(used.sem, 1)
                    dve.wait_ge(used.sem, used.at(n + 1))
                    link(dve.tensor_tensor_reduce(buf(u, s), buf(u, s), bias(u), 1.0, -3e38, ALU.add, ALU.max,
                                                  col(2, u, s)))
                else:
                    if bias is not None:
                        ins = dve.tensor_tensor_reduce(buf(u, s), ps, bias(u), 1.0, -3e38, ALU.add, ALU.max, col(2, u, s))
                    else:
                        ins = dve.tensor_scalar(buf(u, s), ps, 1.0, None, ALU.mult, ALU.max, accum_out=col(2, u, s))
                    ins.then_inc(used.sem, 1)
                    dve.wait_ge(used.sem, used.at(n + 1))
                dve.tensor_scalar(col(0, u, s), col(2, u, s), -scale, None, ALU.mult).then_inc(negmax.sem, 1)

            def weight(u):
                dve.wait_ge(probs.sem, probs.at(subs * (u + 1)))
                if subs == 1:
                    link(dve.reciprocal(col(1, u, 0), col(1, u, 0)))
                    dve.tensor_scalar(buf(u, 0), buf(u, 0), col(1, u, 0), None, ALU.mult).then_inc(weights.sem, 1)
                else:
                    link(dve.reciprocal(col(1, u, 1), col(1, u, 1)))
                    link(dve.tensor_scalar(col(2, u, 1), total(u, 0), col(1, u, 1), split, ALU.mult, ALU.mult))
                    dve.scalar_tensor_tensor(buf(u, 0), buf(u, 1), col(2, u, 1), buf(u, 0), ALU.mult,
                                             ALU.add).then_inc(weights.sem, 1)

            for u in range(units + 2):
                if u < units and subs == 2:
                    maximum(u, 0)
                if 1 <= u <= units:
                    weight(u - 1)
                if u < units:
                    maximum(u, subs - 1)
                if u >= 2:
                    dve.wait_ge(weighed.sem, weighed.at(u - 1))
                    consume(dve, link, u - 2).then_inc(consumed.sem, 1)
            link.end()

        if split is not None:
            @block.sync
            def _(sp):
                for u in range(1, units):
                    if u >= 2:
                        sp.wait_ge(scores.sem, scores.at(2 * (u - 1)))
                    for part in range(3):
                        stack_keys(sp, M, u, part)

            @block.gpsimd
            def _(pool):
                for u in range(units):
                    if u >= 2:
                        pool.wait_ge(scores.sem, scores.at(2 * (u - 1)))
                    src, mask, dst = split_operands(M, u)
                    pool.tensor_tensor(dst, src, mask, ALU.mult).then_inc(formed.sem, 1)
    scores.passed(units * subs)
    used.passed(units * subs)
    negmax.passed(units * subs)
    probs.passed(units * subs)
    weights.passed(units)
    turned.passed(units * NC)
    moved.passed(units * NC)
    weighed.passed(units)
    consumed.passed(units)
    if split is not None:
        formed.passed(units)
        for c in stacked:
            c.passed(128 * units // 2)


A0_BUF = [0, S, 2 * S, 3 * S]
A0_PT = 4 * S
A0_V = A0_PT + NT * P
HALF_S = (S + 1) // 2
A0_KPART = [A0_V + NT * P + i * HALF_S for i in range(3)]
A0_KSTACK = [A0_KPART[2] + (i + 1) * HALF_S for i in range(2)]
A0_Q = A0_KSTACK[1] + HALF_S
A0_QPART = A0_Q + 2 * P
A0_QSTACK = A0_QPART + 3 * P // 2
A0_QB = A0_QSTACK + 4 * P
A0_ATT = A0_QB + 2 * P
A0_SPREAD = A0_ATT + P
assert A0_SPREAD + P <= ARENA

PART_PAIRS = [(0, 0), (1, 0), (2, 0), (0, 1), (1, 1), (2, 1), (0, 2), (1, 2)]


def split_operands(M, u):
    stack = M.at(A0_QSTACK, 4 * P).bitcast(BF16)
    src = stack[:, u * P + M.batch * T:u * P + (M.batch + 1) * T].unsqueeze(1).broadcast_to((P, 4, T))
    mask = M.w("sub_mask").unsqueeze(2).broadcast_to((P, 4, T))
    return src, mask, unit_queries(M, u).rearrange("p (c t) -> p c t", t=T)


def unit_queries(M, u):
    return M.at(A0_QB + P * (u % 2), P).bitcast(BF16)


def key_stack(M, u):
    return M.at(A0_KSTACK[u % 2], HALF_S).bitcast(BF16)[:, 0:S]


def stack_keys(sp, M, u, part):
    for c, (_, k) in enumerate(PART_PAIRS):
        if k == part:
            sp.dma_start(key_stack(M, u)[16 * c:16 * (c + 1), :],
                         key_part(M, part)[16 * u:16 * (u + 1), :]).then_inc(M.count(f"at_keys_stacked{u % 2}").sem, 16)


def key_part(M, i):
    return M.at(A0_KPART[i], HALF_S).bitcast(BF16)[:, 0:S]


def project_out(nc, M, name, terms, bias=None):
    done = M.count("out_projected")
    chain_c = M.count("out_dve_chain")
    with nc.Block(no_gpsimd_drain=True) as block:
        @block.tensor
        def _(pe):
            for i, (lhs, rhs) in enumerate(terms):
                mm = pe.matmul(M.psA[:, 0:P], lhs, rhs, start=(i == 0), stop=(i == len(terms) - 1))
            mm.then_inc(done.sem, 1)

        @block.vector
        def _(dve):
            link = Chain(dve, chain_c)
            if bias is not None:
                link(dve.tensor_tensor(M.x[:, :], M.x[:, :], bias, ALU.add))
            dve.wait_ge(done.sem, done.at(1))
            dve.tensor_tensor(M.x[:, :], M.x[:, :], M.psA[:, 0:P], ALU.add)
            link.end()
    done.passed(1)


def cross0(nc, M):
    q_done, k_done, v_done, q_part, q_spread, q_spread2, q_summed, k_hi, k_rest, k_mid, k_rest2, k_lo = (M.count("x0_" + n) for n in (
        "q", "k", "v", "q_parts", "q_spread", "q_spread2", "q_stack_summed", "k_hi", "k_rest", "k_mid", "k_rest2", "k_lo"))
    chain_c = M.count("x0_dve_chain")
    V, att = M.at(A0_V, NT * P), M.at(A0_ATT, P)
    q, rest = M.at(A0_Q, P), M.at(A0_Q + P, P)
    qp = [M.at(A0_QPART + i * P // 2, P // 2).bitcast(BF16) for i in range(3)]
    q_stack = M.at(A0_QSTACK, 4 * P).bitcast(BF16)
    q_wide = [M.at(A0_BUF[1] + 4 * P * i, 4 * P).bitcast(BF16) for i in range(3)]
    places = M.at(A0_BUF[2], 3 * P // 2).bitcast(BF16)
    place = [places[:, P * i:P * (i + 1)] for i in range(3)]
    kp = [key_part(M, i) for i in range(3)]
    k_left = M.at(A0_BUF[0], S)
    sides = [(0, 1024), (1024, S)]
    norm = LayerNorm(M)

    def widen_queries(engine, i):
        return engine.tensor_tensor(q_wide[i].rearrange("p (u t) -> p u t", t=P),
                                    qp[i].unsqueeze(1).broadcast_to((P, 8, P)),
                                    M.w("pair_mask").unsqueeze(2).broadcast_to((P, 8, P)), ALU.mult)

    for b in range(2):
        M.batch = b
        with nc.Block(no_gpsimd_drain=True) as block:
            @block.sync
            def _(sp):
                for part, ready in enumerate((k_hi, k_mid, k_lo)):
                    sp.wait_ge(ready.sem, ready.at(2))
                    stack_keys(sp, M, 0, part)

            @block.tensor
            def _(pe):
                for n, (first, end) in enumerate(sides):
                    for a in range(first, end, 512):
                        m = min(512, end - a)
                        mm = pe.matmul(M.psS[:, a:a + m], M.w("x0_wk"), M.ctxT[b][:, a:a + m], start=True, stop=True)
                    mm.then_inc(k_done.sem, 1)
                    if b == 0 and n == 0:
                        norm.on_tensor(pe)
                        pe.matmul(M.psD[:, 0:P], M.w("x0_wq"), M.xnT[:, :], start=True,
                                  stop=True).then_inc(q_done.sem, 1)
                for c, bank in enumerate([M.psA, M.psB, M.psC]):
                    for j in range(4 * c, 4 * c + 4):
                        mm = pe.matmul(bank[:, (j % 4) * P:(j % 4 + 1) * P], M.ctxT[b][:, j * P:(j + 1) * P],
                                       M.w("x0_wv"), start=True, stop=True)
                    mm.then_inc(v_done.sem, 1)
                if b == 0:
                    pe.wait_ge(q_done.sem, q_done.at(2))
                pe.matmul(M.psD[0:TAIL, P:2 * P], M.ctxT[b][:, 12 * P:S], M.w("x0_wv"), start=True,
                          stop=True).then_inc(v_done.sem, 1)
                if b == 0:
                    pe.wait_ge(q_spread.sem, q_spread.at(2))
                    pe.wait_ge(q_spread2.sem, q_spread2.at(1))
                    pe.wait_ge(k_rest.sem, k_rest.at(2))
                    for g in range(2):
                        for i in range(3):
                            mm = pe.matmul(M.psS[:, 512 * g:512 * (g + 1)], place[i], q_wide[i][:, 512 * g:512 * (g + 1)],
                                           start=(i == 0), stop=(i == 2))
                    mm.then_inc(q_summed.sem, 1)

            @block.scalar
            def _(act):
                if b == 0:
                    norm.on_scalar(act)
                for n, (a, e) in enumerate(sides):
                    act.wait_ge(k_done.sem, k_done.at(n + 1))
                    act.activation(kp[0][:, a:e], M.psS[:, a:e], ACT.Identity, bias=M.w("x0_bk")).then_inc(k_hi.sem, 1)
                for part, left_of, ready in ((1, k_rest, k_mid), (2, k_rest2, k_lo)):
                    for n, (a, e) in enumerate(sides):
                        act.wait_ge(left_of.sem, left_of.at(n + 1))
                        act.activation(kp[part][:, a:e], k_left[:, a:e], ACT.Copy).then_inc(ready.sem, 1)
                for c, bank in enumerate([M.psA, M.psB, M.psC]):
                    act.wait_ge(v_done.sem, v_done.at(c + 1))
                    act.activation(V[:, 512 * c:512 * (c + 1)], bank[:, :], ACT.Copy)
                act.wait_ge(v_done.sem, v_done.at(4))
                act.activation(V[0:TAIL, 12 * P:NT * P], M.psD[0:TAIL, P:2 * P], ACT.Copy)
                if b == 0:
                    act.wait_ge(q_summed.sem, q_summed.at(1))
                    act.activation(q_stack, M.psS[:, 0:8 * P], ACT.Copy)

            @block.vector
            def _(dve):
                link = Chain(dve, chain_c)
                if b == 0:
                    norm.on_vector(dve)
                    link(dve.memset(places, 0.0))
                    for i in range(3):
                        for c, (part, _) in enumerate(PART_PAIRS):
                            if part == i:
                                rows16 = slice(16 * c, 16 * (c + 1))
                                dve.tensor_copy(place[i][:, rows16], M.w("row_places")[:, rows16])
                    dve.wait_ge(q_done.sem, q_done.at(1))
                    dve.tensor_scalar(q, M.psD[:, 0:P], M.w("x0_bq"), 0.5, ALU.add, ALU.mult).then_inc(q_done.sem, 1)
                for n, (a, e) in enumerate(sides):
                    dve.wait_ge(k_hi.sem, k_hi.at(n + 1))
                    dve.scalar_tensor_tensor(k_left[:, a:e], M.psS[:, a:e], M.w("x0_bk"), kp[0][:, a:e], ALU.add,
                                             ALU.subtract).then_inc(k_rest.sem, 1)
                if b == 0:
                    dve.wait_ge(q_done.sem, q_done.at(2))
                    left = q
                    for i in range(3):
                        dve.tensor_copy(qp[i], left).then_inc(q_part.sem, 1)
                        if i < 2:
                            dve.wait_ge(q_part.sem, q_part.at(i + 1))
                            link(dve.tensor_tensor(rest, left, qp[i], ALU.subtract))
                            left = rest
                for n, (a, e) in enumerate(sides):
                    dve.wait_ge(k_mid.sem, k_mid.at(n + 1))
                    dve.tensor_tensor(k_left[:, a:e], k_left[:, a:e], kp[1][:, a:e],
                                      ALU.subtract).then_inc(k_rest2.sem, 1)
                if b == 0:
                    for i in range(2):
                        widen_queries(dve, i).then_inc(q_spread.sem, 1)
                link.end()

            if b == 0:
                @block.gpsimd
                def _(pool):
                    norm.on_gpsimd(pool)
                    pool.wait_ge(q_part.sem, q_part.at(3))
                    widen_queries(pool, 2).then_inc(q_spread2.sem, 1)
        if b == 0:
            norm.end()
            q_done.passed(2)
            q_part.passed(3)
            q_spread.passed(2)
            q_spread2.passed(1)
            q_summed.passed(1)
        for c in (k_done, k_hi, k_rest, k_mid, k_rest2, k_lo):
            c.passed(2)
        v_done.passed(4)

        def gather(dve, link, u):
            out = att[:, b * T:(b + 1) * T]
            for h in range(2):
                mask = M.w("head_mask")[:, 2 * u + h:2 * u + h + 1]
                src = M.psD[:, h * T:(h + 1) * T]
                if u == 0 and h == 0:
                    ins = dve.tensor_scalar(out, src, mask, None, ALU.mult)
                else:
                    ins = dve.scalar_tensor_tensor(out, src, mask, out, ALU.mult, ALU.add)
                if h == 0:
                    link(ins)
            return ins

        attend(nc, M, units=8, rows=P, tiles=CTX_TILES, subs=2,
               queries=lambda u, s: unit_queries(M, u)[:, P * s:P * (s + 1)],
               keys=lambda u, a, m: key_stack(M, u)[:, a:a + m],
               values=lambda u, j: V[0:CTX_TILES[j][1], j * P:(j + 1) * P],
               bufs=[M.at(a, S) for a in A0_BUF], pt=M.at(A0_PT, 1664), consume=gather,
               split=M.lam[:, 0:1])
        divided, spread = M.count("x0_spread_formed"), M.count("x0_spread_turned")
        L = M.at(A0_SPREAD, P)
        L4 = L.rearrange("p (u h d) -> p u h d", u=8, h=2)
        with nc.Block(no_gpsimd_drain=True) as block:
            @block.vector
            def _(dve):
                link = Chain(dve, chain_c)
                link(dve.memset(L, 0.0))
                link(dve.reciprocal(M.row8[:, 0:8], M.row8[:, 0:8]))
                for h in range(2):
                    r = slice(T * h, T * (h + 1))
                    dve.tensor_scalar(L4[r, :, h, :], M.row8[r, 0:8].unsqueeze(2).broadcast_to((T, 8, HD)),
                                      1.0 - LAMBDA_INIT, None, ALU.mult).then_inc(divided.sem, 1)
                dve.wait_ge(spread.sem, spread.at(1))
                out = att[:, b * T:(b + 1) * T]
                link(dve.tensor_tensor(out, out, M.psA[:, 0:T], ALU.mult))
                link(dve.tensor_scalar(out, out, M.w("x0_bv"), None, ALU.add))
                link.end()

            @block.tensor
            def _(pe):
                pe.wait_ge(divided.sem, divided.at(2))
                pe.matmul(M.psA[:, 0:T], L, M.w("same_token"), start=True, stop=True).then_inc(spread.sem, 1)
        divided.passed(2)
        spread.passed(1)
    project_out(nc, M, "x0", [(att, M.w("x0_wo"))], M.w("x0_bo"))


SA_Q, SA_K, SA_T1, SA_T2 = 0, 128, 256, 384
SA_QB, SA_V, SA_S, SA_W, SA_PT, SA_ATT = 512, 2560, 2816, 3840, 4864, 6912
SA_M = 7168
assert SA_M + 9 * H <= EXPERTS0


def self_attention(nc, M, n, *, rope=None, biased, causal, scale, top=None, load=None):
    proj, formed, queries, queries2, scored, packed, expd, weights, turned, moved, weighed, vals, divided, out_turned, \
        out_moved, out_done = (
            M.count("sa_" + k) for k in ("projected", "qk_formed", "queries", "queries2", "scored", "packed",
                                         "exponentials", "weights", "turned", "moved", "weighed", "values", "divided",
                                         "out_turned", "out_moved", "out_projected"))
    chain_c = M.count("sa_dve_chain")
    pre = n + "_"
    q, k, t1, t2 = (M.at(a, P) for a in (SA_Q, SA_K, SA_T1, SA_T2))
    qb = M.at(SA_QB, H * P).rearrange("p (h t) -> p h t", t=P)
    v = M.at(SA_V, 2 * P, T).rearrange("p (h b d) -> p h b d", b=2, d=HD)
    s = M.at(SA_S, H * T).rearrange("p (h s) -> p h s", s=T)
    w = M.at(SA_W, H * T).rearrange("p (h s) -> p h s", s=T)
    pt = M.at(SA_PT, H * P, T).rearrange("p (h t) -> p h t", t=P)
    att, attT = M.at(SA_ATT, P), M.at(SA_ATT + P, P)
    mx = M.at(SA_M, H)
    tops = M.at(SA_M + H, 8 * H)
    ps = M.psS[:, 0:H * T].rearrange("p (h s) -> p h s", s=T)
    outs = M.psS[:, 1536:1536 + 2 * P].rearrange("p (h b d) -> p h b d", b=2, d=HD)
    mask = M.w("head_mask")

    def spread_queries(engine, g):
        hs = slice(8 * g, 8 * g + 8)
        return engine.tensor_tensor(qb[:, hs, :], q.unsqueeze(1).broadcast_to((P, 8, P)),
                                    mask[:, hs].unsqueeze(2).broadcast_to((P, 8, P)), ALU.mult)

    norm = LayerNorm(M)
    with nc.Block(no_gpsimd_drain=True) as block:
        if load is not None:
            @block.sync
            def _(sp):
                load(sp)

        @block.tensor
        def _(pe):
            norm.on_tensor(pe)
            names = ["wq", "wk"] + (["wq_turned", "wk_turned"] if rope else [])
            for i, name in enumerate(names):
                mm = pe.matmul(M.psA[:, i * P:(i + 1) * P], M.w(pre + name), M.xnT[:, :], start=True, stop=True)
            mm.then_inc(proj.sem, 1)
            for b in range(2):
                mm = pe.matmul(M.psB[0:T, b * P:(b + 1) * P], M.xnT[:, b * T:(b + 1) * T], M.w(pre + "wv"),
                               start=True, stop=True)
            mm.then_inc(vals.sem, 1)
            pe.wait_ge(formed.sem, formed.at(1))
            for g in range(2):
                half = [queries, queries2][g]
                pe.wait_ge(half.sem, half.at(1))
                for h in range(8 * g, 8 * g + 8):
                    for b in range(2):
                        r = slice(b * T, (b + 1) * T)
                        mm = pe.matmul(ps[r, h, :], qb[:, h, r], k[:, r], start=True, stop=True)
            mm.then_inc(scored.sem, 1)
            banks = [M.psA, M.psC, M.psB, M.psD]
            for c in range(4):
                ready = weights if top else expd
                pe.wait_ge(ready.sem, ready.at(1 if top else c // 2 + 1))
                for i in range(4):
                    mm = pe.transpose(banks[c][0:T, i * P:(i + 1) * P], s[:, 4 * c + i, :], M.w("ident"))
                mm.then_inc(turned.sem, 1)
            for h in range(H):
                if h % 4 == 0:
                    pe.wait_ge(moved.sem, moved.at(h // 4 + 1))
                mm = pe.matmul(outs[:, h], pt[:, h, :], v[:, h], start=True, stop=True)
            mm.then_inc(weighed.sem, 1)
            pe.wait_ge(divided.sem, divided.at(2))
            pe.transpose(M.psA[:, 0:P], att, M.w("ident")).then_inc(out_turned.sem, 1)
            pe.wait_ge(out_moved.sem, out_moved.at(1))
            pe.matmul(M.psC[:, 0:P], attT, M.w(pre + "wo"), start=True, stop=True).then_inc(out_done.sem, 1)

        @block.scalar
        def _(act):
            norm.on_scalar(act)
            act.wait_ge(packed.sem, packed.at(1))
            for g in range(2):
                hs = slice(8 * g, 8 * g + 8)
                act.activation(s[:, hs, :], s[:, hs, :], ACT.Exp).then_inc(expd.sem, 1)
            banks = [M.psA, M.psC, M.psB, M.psD]
            for c in range(4):
                act.wait_ge(turned.sem, turned.at(c + 1))
                act.activation(pt[:, 4 * c:4 * c + 4, :], banks[c][0:T, :].rearrange("p (h t) -> p h t", t=P),
                               ACT.Copy).then_inc(moved.sem, 1)
            act.wait_ge(out_turned.sem, out_turned.at(1))
            act.activation(attT, M.psA[:, 0:P], ACT.Copy).then_inc(out_moved.sem, 1)

        @block.gpsimd
        def _(pool):
            norm.on_gpsimd(pool)
            pool.wait_ge(formed.sem, formed.at(2))
            spread_queries(pool, 1).then_inc(queries2.sem, 1)

        @block.vector
        def _(dve):
            norm.on_vector(dve)
            link = Chain(dve, chain_c)
            dve.wait_ge(proj.sem, proj.at(1))
            for i, (dst, bias) in ((1, (k, "bk")), (0, (q, "bq"))):
                src = M.psA[:, i * P:(i + 1) * P]
                if rope:
                    cos, sin = M.w("cos" + rope), M.w("sin" + rope)
                    other = M.psA[:, (2 + i) * P:(3 + i) * P]
                    if biased:
                        link(dve.scalar_tensor_tensor(t1, src, M.w(pre + bias), cos, ALU.add, ALU.mult))
                        link(dve.scalar_tensor_tensor(t2, other, M.w(pre + bias + "_turned"), sin, ALU.add, ALU.mult))
                    else:
                        link(dve.tensor_tensor(t1, src, cos, ALU.mult))
                        link(dve.tensor_tensor(t2, other, sin, ALU.mult))
                    if i == 1 or scale == 1.0:
                        dve.tensor_tensor(dst, t1, t2, ALU.add).then_inc(formed.sem, 1)
                        dve.wait_ge(formed.sem, formed.at(2 - i))
                    else:
                        link(dve.tensor_tensor(t1, t1, t2, ALU.add))
                        dve.tensor_scalar(dst, t1, scale, None, ALU.mult).then_inc(formed.sem, 1)
                else:
                    dve.tensor_scalar(dst, src, M.w(pre + bias), 1.0 if i else scale, ALU.add,
                                      ALU.mult).then_inc(formed.sem, 1)
            dve.wait_ge(formed.sem, formed.at(2))
            spread_queries(dve, 0).then_inc(queries.sem, 1)
            dve.wait_ge(vals.sem, vals.at(1))
            for b in range(2):
                src, dst = M.psB[0:T, b * P:(b + 1) * P].rearrange("p (h d) -> p h d", d=HD), v[:, :, b, :]
                if biased:
                    dve.tensor_tensor(dst, src, M.w(pre + "bv", T).rearrange("p (h d) -> p h d", d=HD), ALU.add)
                else:
                    dve.tensor_copy(dst, src)
            dve.wait_ge(scored.sem, scored.at(1))
            if causal:
                link(dve.tensor_tensor(s, ps, M.w("causal").unsqueeze(1).broadcast_to((P, H, T)), ALU.add))
            else:
                link(dve.tensor_copy(s, ps))
            link(dve.tensor_reduce(mx, s, AX.X, ALU.max))
            if top:
                src = s
                for _ in range(top // 8):
                    for h in range(H):
                        ins = dve.max(tops[:, 8 * h:8 * h + 8], src[:, h, :])
                    link(ins)
                    for h in range(H):
                        ins = dve.match_replace(w[:, h, :], tops[:, 8 * h:8 * h + 8], src[:, h, :], -3e38)
                    link(ins)
                    src = w
                link(dve.tensor_tensor(w, w, s, ALU.not_equal))
            dve.tensor_tensor(s, s, mx.unsqueeze(2).broadcast_to((P, H, T)), ALU.subtract).then_inc(packed.sem, 1)
            dve.wait_ge(expd.sem, expd.at(2))
            if top:
                dve.tensor_tensor(s, s, w, ALU.mult).then_inc(weights.sem, 1)
                dve.wait_ge(weights.sem, weights.at(1))
            link(dve.tensor_reduce(mx, s, AX.X, ALU.add))
            link(dve.reciprocal(mx, mx))
            if biased:
                link(dve.tensor_tensor(M.x[:, :], M.x[:, :], M.w(pre + "bo"), ALU.add))
            dve.wait_ge(weighed.sem, weighed.at(1))
            for b in range(2):
                r = slice(b * T, (b + 1) * T)
                dve.tensor_tensor(att[r].rearrange("p (h d) -> p h d", d=HD), outs[r, :, b, :],
                                  mx[r].unsqueeze(2).broadcast_to((T, H, HD)), ALU.mult).then_inc(divided.sem, 1)
            dve.wait_ge(out_done.sem, out_done.at(1))
            dve.tensor_tensor(M.x[:, :], M.x[:, :], M.psC[:, 0:P], ALU.add)
            link.end()
    norm.end()
    for c in (proj, queries, queries2, scored, packed, weighed, vals, out_turned, out_moved, out_done):
        c.passed(1)
    if top:
        weights.passed(1)
    for c in (expd, divided):
        c.passed(2)
    formed.passed(2)
    turned.passed(4)
    moved.passed(4)


def load_experts0(sp, M, weights):
    sp.dma_start(M.at(EXPERTS0, ONLY0), weights).then_inc(M.count("experts0_loaded").sem, 16)


MO_H, MO_GT, MO_MEAN = 0, 2176, 2304


def experts(nc, M, n, *, E, kind, up, up3, down, router, router_bias=None, b1=None, b2=None, floor=0.0, by_batch=False):
    pre = n + "_"
    logits, shifted, soft, gated, gT_ps, gT_sb, up_done, acted, prod, down_done, added, mean = (
        M.count("mo_" + k) for k in ("logits", "shifted", "softmax", "gates", "gates_turned", "gates_moved", "up",
                                     "activated", "product", "down", "added", "mean"))
    chain_c = M.count("mo_dve_chain")
    R = M.row8
    lg, top8, e16, rep, sel, g = (R[:, a:a + n_] for a, n_ in ((0, 8), (8, 8), (16, 16), (32, 16), (48, 8), (56, 8)))
    sc = R[:, 64:72]
    hT = [M.at(MO_H + 512 * i, 512) for i in range(4)]
    gT = M.at(MO_GT, P, 8)
    meanT = M.at(MO_MEAN, P)
    two = kind == "silu"
    norm = LayerNorm(M)
    with nc.Block(no_gpsimd_drain=True) as block:
        @block.gpsimd
        def _(pool):
            norm.on_gpsimd(pool)

        @block.tensor
        def _(pe):
            norm.on_tensor(pe)
            xr = M.xnT[:, :]
            if by_batch:
                pe.matmul(M.psB[:, 0:P], M.xn[:, :], M.w("batch_mean"), start=True, stop=True).then_inc(mean.sem, 1)
                pe.wait_ge(mean.sem, mean.at(2))
                xr = meanT
            pe.matmul(M.psA[:, 0:E], xr, router, start=True, stop=True).then_inc(logits.sem, 1)

            def raise_(e):
                if two:
                    if e >= 2:
                        pe.wait_ge(prod.sem, prod.at(e - 1))
                elif e >= 4:
                    pe.wait_ge(acted.sem, acted.at(e - 3))
                for w_, off in ((up, 0), (up3, 1))[:2 if two else 1]:
                    a = 512 * (2 * (e % 2) + off if two else e % 4)
                    for c in range(4):
                        mm = pe.matmul(M.psS[:, a + P * c:a + P * (c + 1)], w_(e, c), M.xnT[:, :], start=True,
                                       stop=True)
                mm.then_inc(up_done.sem, 1)

            if two:
                pe.wait_ge(M.count("experts0_loaded").sem, 16)
            raise_(0)
            for e in range(E):
                if e + 1 < E:
                    raise_(e + 1)
                ready = prod if two else acted
                pe.wait_ge(ready.sem, ready.at(e + 1))
                if e >= 2:
                    pe.wait_ge(added.sem, added.at(e - 1))
                bank = [M.psB, M.psC][e % 2]
                if by_batch and e == 0:
                    pe.wait_ge(mean.sem, mean.at(2))
                for c in range(4):
                    mm = pe.matmul(bank[:, 0:P], hT[e % 4][:, P * c:P * (c + 1)], down(e, c), start=(c == 0),
                                   stop=(c == 3))
                mm.then_inc(down_done.sem, 1)
            if b2 is not None:
                pe.wait_ge(gated.sem, gated.at(1))
                pe.transpose(M.psA[0:8, 128:256], g, M.w("ident")).then_inc(gT_ps.sem, 1)
                pe.wait_ge(gT_sb.sem, gT_sb.at(1))
                pe.matmul(M.psD[:, 0:P], gT, b2, start=True, stop=True).then_inc(gT_ps.sem, 1)

        @block.scalar
        def _(act):
            norm.on_scalar(act)
            act.wait_ge(shifted.sem, shifted.at(1))
            act.activation(e16[:, 0:8], lg, ACT.Exp, bias=sc[:, 0:1], accum_out=sc[:, 1:2]).then_inc(soft.sem, 1)
            for e in range(E):
                act.wait_ge(up_done.sem, up_done.at(e + 1))
                if e >= 4:
                    act.wait_ge(down_done.sem, down_done.at(e - 3))
                if two:
                    act.activation(hT[e % 4], M.psS[:, 1024 * (e % 2):1024 * (e % 2) + 512],
                                   ACT.Silu).then_inc(acted.sem, 1)
                else:
                    for c in range(4):
                        fn = ACT.Relu if kind == "relu" else ACT.Gelu
                        ins = act.activation(hT[e % 4][:, P * c:P * (c + 1)],
                                             M.psS[:, 512 * (e % 4) + P * c:512 * (e % 4) + P * (c + 1)], fn,
                                             bias=b1[:, 4 * e + c:4 * e + c + 1])
                    ins.then_inc(acted.sem, 1)

        @block.vector
        def _(dve):
            norm.on_vector(dve)
            link = Chain(dve, chain_c)
            link(dve.memset(lg, GONE))
            link(dve.memset(e16, -1.0))
            if by_batch:
                dve.wait_ge(mean.sem, mean.at(1))
                dve.tensor_copy(meanT, M.psB[:, 0:P]).then_inc(mean.sem, 1)
            dve.wait_ge(logits.sem, logits.at(1))
            if router_bias is not None:
                link(dve.tensor_tensor(lg[:, 0:E], M.psA[:, 0:E], router_bias, ALU.add))
            else:
                link(dve.tensor_copy(lg[:, 0:E], M.psA[:, 0:E]))
            dve.tensor_reduce(sc[:, 0:1], lg, AX.X, ALU.max, negate=True).then_inc(shifted.sem, 1)
            dve.wait_ge(soft.sem, soft.at(1))
            link(dve.reciprocal(sc[:, 2:3], sc[:, 1:2]))
            link(dve.tensor_scalar(e16[:, 0:8], e16[:, 0:8], sc[:, 2:3], None, ALU.mult))
            link(dve.max(top8, e16[:, 0:8]))
            link(dve.tensor_scalar(sc[:, 3:4], top8[:, 0:1], top8[:, 1:2], floor, ALU.add, ALU.add))
            link(dve.memset(top8[:, 2:8], -1.0))
            link(dve.match_replace(rep, top8, e16, -2.0))
            link(dve.tensor_tensor(sel, rep[:, 0:8], e16[:, 0:8], ALU.not_equal))
            link(dve.tensor_tensor(sel, sel, e16[:, 0:8], ALU.mult))
            link(dve.reciprocal(sc[:, 4:5], sc[:, 3:4]))
            dve.tensor_scalar(g, sel, sc[:, 4:5], None, ALU.mult).then_inc(gated.sem, 1)
            dve.wait_ge(gated.sem, gated.at(1))

            def add(e):
                dve.wait_ge(down_done.sem, down_done.at(e + 1))
                if e >= 1:
                    dve.wait_ge(added.sem, added.at(e))
                dve.scalar_tensor_tensor(M.x[:, :], [M.psB, M.psC][e % 2][:, 0:P], g[:, e:e + 1], M.x[:, :], ALU.mult,
                                         ALU.add).then_inc(added.sem, 1)

            for e in range(E):
                if two:
                    dve.wait_ge(acted.sem, acted.at(e + 1))
                    a = 1024 * (e % 2) + 512
                    dve.tensor_tensor(hT[e % 4], hT[e % 4], M.psS[:, a:a + 512], ALU.mult).then_inc(prod.sem, 1)
                if e >= 1:
                    add(e - 1)
            add(E - 1)
            if b2 is not None:
                dve.wait_ge(gT_ps.sem, gT_ps.at(1))
                dve.tensor_copy(gT, M.psA[0:8, 128:256]).then_inc(gT_sb.sem, 1)
                dve.wait_ge(gT_ps.sem, gT_ps.at(2))
                dve.wait_ge(added.sem, added.at(E))
                dve.tensor_tensor(M.x[:, :], M.x[:, :], M.psD[:, 0:P], ALU.add)
            link.end()
    norm.end()
    for c in (logits, shifted, soft, gated):
        c.passed(1)
    for c in (up_done, acted, down_done, added):
        c.passed(E)
    if two:
        prod.passed(E)
    if by_batch:
        mean.passed(2)
    if b2 is not None:
        gT_ps.passed(2)
        gT_sb.passed(1)


WIDE = S + T
A1_BUF = [0, 1792]
A1_PT, A1_ROWS, A1_KT = 3584, 5376, 7168
A1_T, A1_K, A1_LAT, A1_LATT = 0, 512, 1536, 1664
A1_Q, A1_SQ = 1792, 3584
A1_QB = A1_KT + 4 * WIDE
A1_MASK = A1_QB + 1024
A1_UT = A1_MASK + (WIDE + 1) // 2
A1_SEEN = 2816
A1_STATS = [A1_SQ + 1536, A1_UT + 8 * P]
assert A1_STATS[1] + 3 * NT <= ARENA and A1_STATS[0] + 3 * NT <= A1_ROWS


def cross1(nc, M, batch_seen):
    chain_c = M.count("x1_dve_chain")
    rows = M.at(A1_ROWS, 14 * P).rearrange("p (j d) -> p j d", d=P)
    kT = M.at(A1_KT, 4 * WIDE).rearrange("p (c s) -> p c s", s=WIDE)
    qb = M.at(A1_QB, 1024).rearrange("p (b c t) -> p b c t", b=2, c=4)
    lat, latT = M.xn[:, :], M.at(A1_LATT, P)
    q, sq = M.at(A1_Q, 512), M.at(A1_SQ, 512)
    mask = M.at(A1_MASK, (WIDE + 1) // 2).bitcast(BF16)[:, 0:WIDE]
    seen = M.at(A1_SEEN, (S + 3) // 4).bitcast(U8)[:, 0:S]
    UT = M.at(A1_UT, 8 * P).rearrange("p (h t) -> p h t", t=P)
    st = M.small
    stats = [M.at(a, 2 * NT) for a in A1_STATS]
    deviations = [M.at(a + 2 * NT, NT) for a in A1_STATS]
    var, rstd, normed, turned, moved, projected, norm2, rnorm, scaled, q_turned, cvar, crstd = (
        M.count("x1_" + k) for k in ("var", "rstd", "lat_normed", "lat_turned", "lat_moved", "q_projected",
                                     "q_norm2", "q_rnorm", "q_scaled", "q_turned", "ctx_var", "ctx_rstd"))
    norm = LayerNorm(M)
    with nc.Block(no_gpsimd_drain=True) as block:
        @block.vector
        def _(dve):
            link = Chain(dve, chain_c)

            def context_stats(b):
                for j in range(NT):
                    ins = dve.bn_stats(M.row8[:, 6 * j:6 * j + 6], M.ctxN[b][:, j, :])
                link(ins)
                for j in range(NT):
                    ins = dve.bn_aggr(stats[b][:, 2 * j:2 * j + 2], M.row8[:, 6 * j:6 * j + 6])
                link(ins)
                dve.tensor_scalar(deviations[b], stats[b].rearrange("p (j k) -> p k j", k=2)[:, 1, :], EPS, None,
                                  ALU.add).then_inc(cvar.sem, 1)

            norm.on_vector(dve)
            dve.wait_ge(norm.normed.sem, norm.normed.at(1))
            link(dve.bn_stats(M.stat[:, 0:6], M.xn[:, :]))
            link(dve.bn_aggr(M.stat[:, 6:8], M.stat[:, 0:6]))
            dve.tensor_scalar(M.stat[:, 8:9], M.stat[:, 7:8], EPS, None, ALU.add).then_inc(var.sem, 1)
            link(dve.memset(qb, 0.0))
            dve.wait_ge(rstd.sem, rstd.at(1))
            link(dve.tensor_scalar(lat, M.xn[:, :], M.stat[:, 6:7], M.stat[:, 9:10], ALU.subtract, ALU.mult))
            link(dve.tensor_tensor(lat, lat, M.w("x1_lat_w"), ALU.mult))
            dve.tensor_tensor(lat, lat, M.w("x1_lat_b"), ALU.add).then_inc(normed.sem, 1)
            context_stats(0)
            dve.wait_ge(projected.sem, projected.at(1))
            link(dve.tensor_copy(q, M.psS[:, 0:512]))
            link(dve.tensor_tensor(sq, q, q, ALU.mult))
            link(dve.tensor_reduce(st[:, 0:8], sq.rearrange("p (h d) -> p h d", d=64), AX.X, ALU.add))
            dve.tensor_scalar(st[:, 0:8], st[:, 0:8], 1e-24, None, ALU.max).then_inc(norm2.sem, 1)
            context_stats(1)
            dve.wait_ge(rnorm.sem, rnorm.at(1))
            q3 = q.rearrange("p (h d) -> p h d", d=64)
            link(dve.tensor_tensor(q3, q3, st[:, 8:16].unsqueeze(2).broadcast_to((P, 8, 64)), ALU.mult))
            dve.tensor_tensor(q3, q3, M.w("x1_q_scale").unsqueeze(1).broadcast_to((P, 8, 64)),
                              ALU.mult).then_inc(scaled.sem, 1)
            dve.wait_ge(q_turned.sem, q_turned.at(1))
            for h in range(2):
                r = slice(64 * h, 64 * (h + 1))
                for b in range(2):
                    src = M.psS[r, 1024:1536].rearrange("p (c t) -> p c t", t=P)[:, :, b * T:(b + 1) * T]
                    link(dve.tensor_copy(qb[r, b, :, 64 * h:64 * (h + 1)], src))
            link.end()

        @block.gpsimd
        def _(pool):
            norm.on_gpsimd(pool)
            pool.wait_ge(var.sem, var.at(1))
            pool.tensor_tensor(M.stat[:, 9:10], M.stat[:, 8:9], M.w("neg_half")[:, 0:1], ALU.pow).then_inc(rstd.sem, 1)
            for b in range(2):
                pool.wait_ge(cvar.sem, cvar.at(b + 1))
                pool.tensor_tensor(deviations[b], deviations[b], M.w("neg_half")[:, 0:NT],
                                   ALU.pow).then_inc(crstd.sem, 1)
                if b == 0:
                    pool.wait_ge(norm2.sem, norm2.at(1))
                    pool.tensor_tensor(st[:, 8:16], st[:, 0:8], M.w("neg_half")[:, 0:8], ALU.pow).then_inc(rnorm.sem, 1)

        @block.tensor
        def _(pe):
            pe.wait_ge(normed.sem, normed.at(1))
            pe.transpose(M.psA[:, 0:P], lat, M.w("ident")).then_inc(turned.sem, 1)
            pe.wait_ge(moved.sem, moved.at(1))
            pe.matmul(M.psS[:, 0:512], latT, M.w("x1_wq"), start=True, stop=True).then_inc(projected.sem, 1)
            pe.wait_ge(scaled.sem, scaled.at(1))
            for c in range(4):
                mm = pe.transpose(M.psS[:, 1024 + P * c:1024 + P * (c + 1)], q[:, P * c:P * (c + 1)], M.w("ident"))
            mm.then_inc(q_turned.sem, 1)

        @block.scalar
        def _(act):
            act.wait_ge(turned.sem, turned.at(1))
            act.activation(latT, M.psA[:, 0:P], ACT.Copy).then_inc(moved.sem, 1)
    for c in (var, rstd, normed, turned, moved, projected, norm2, rnorm, scaled, q_turned):
        c.passed(1)
    cvar.passed(2)
    norm.end(turned=False)

    crows, ct, cm, ck, csq, cn2, crn, ckn, ckt, ckm = (
        M.count("x1k_" + k) for k in ("rows", "turned", "moved", "projected", "squared", "norm2",
                                      "rnorm", "normed", "keys_turned", "keys_moved"))
    cseen = M.count("x1k_seen_loaded")
    for b in range(2):
        ctx3 = M.ctxN[b][:, :, :]
        bs = slice(b * T, (b + 1) * T)
        pair = [M.at(A1_T, P), M.at(A1_T + P, P)]
        kn = [M.at(A1_K, 512), M.at(A1_K + 512, 512), M.at(A1_SQ + 1024, 512)]
        with nc.Block(no_gpsimd_drain=True) as block:
            NK = len(KV_TILES)
            sqb = [M.at(A1_SQ, 512), M.at(A1_SQ + 512, 512)]
            banks = [M.psB, M.psC, M.psD]

            @block.sync
            def _(sp):
                sp.dma_start(seen, batch_seen(b).broadcast_to((P, S))).then_inc(cseen.sem, 16)

            @block.tensor
            def _(pe):
                for j in range(NK + 2):
                    if j == 0:
                        pe.wait_ge(crows.sem, crows.at(1))
                        pe.transpose(M.psA[:, 0:KV_TILES[0][1]], rows[:, 0, :], M.w("ident")).then_inc(ct.sem, 1)
                    if j < NK:
                        m = KV_TILES[j][1]
                        pe.wait_ge(cm.sem, cm.at(j + 1))
                        if j >= 3:
                            pe.wait_ge(ckn.sem, ckn.at(j - 2))
                        pe.matmul(banks[j % 3][0:m, :], pair[j % 2][:, 0:m], M.w("x1_wk"), start=True,
                                  stop=True).then_inc(ck.sem, 1)
                    if j + 1 < NK:
                        m = KV_TILES[j + 1][1]
                        pe.wait_ge(crows.sem, crows.at(j + 2))
                        pe.transpose(M.psA[:, 0:m], rows[0:m, j + 1, :], M.w("ident")[0:m, 0:m]).then_inc(ct.sem, 1)
                    if j >= 2:
                        i = j - 2
                        a, m = KV_TILES[i]
                        pe.wait_ge(ckn.sem, ckn.at(i + 1))
                        if i >= 2:
                            pe.wait_ge(ckm.sem, ckm.at(i - 1))
                        for c in range(4):
                            mm = pe.transpose(M.psS[:, 512 * (i % 2) + P * c:512 * (i % 2) + P * c + m],
                                              kn[i % 3][0:m, P * c:P * (c + 1)], M.w("ident")[0:m, 0:m])
                        mm.then_inc(ckt.sem, 1)

            @block.scalar
            def _(act):
                def move_rows(j):
                    m = KV_TILES[j][1]
                    act.wait_ge(ct.sem, ct.at(j + 1))
                    if j >= 2:
                        act.wait_ge(ck.sem, ck.at(j - 1))
                    act.activation(pair[j % 2][:, 0:m], M.psA[:, 0:m], ACT.Copy).then_inc(cm.sem, 1)

                move_rows(0)
                for j in range(NK + 2):
                    if j + 1 < NK:
                        move_rows(j + 1)
                    if j < NK:
                        m = KV_TILES[j][1]
                        act.wait_ge(ck.sem, ck.at(j + 1))
                        if j >= 2:
                            act.wait_ge(cn2.sem, cn2.at(j - 1))
                        act.activation(sqb[j % 2][0:m, :], banks[j % 3][0:m, :], ACT.Square).then_inc(csq.sem, 1)
                    if j >= 2:
                        a, m = KV_TILES[j - 2]
                        act.wait_ge(ckt.sem, ckt.at(j - 1))
                        src = M.psS[:, 512 * (j % 2):512 * (j % 2) + 512].rearrange("p (c s) -> p c s", s=P)
                        act.activation(kT[:, :, a:a + m], src[:, :, 0:m], ACT.Copy).then_inc(ckm.sem, 1)

            @block.gpsimd
            def _(pool):
                for j in range(NK):
                    m = KV_TILES[j][1]
                    s_ = 16 * (j % 3)
                    pool.wait_ge(cn2.sem, cn2.at(j + 1))
                    if j >= 3:
                        pool.wait_ge(ckn.sem, ckn.at(j - 2))
                    pool.tensor_tensor(st[0:m, s_ + 8:s_ + 16], st[0:m, s_:s_ + 8], M.w("neg_half")[0:m, 0:8],
                                       ALU.pow).then_inc(crn.sem, 1)

            @block.vector
            def _(dve):
                link = Chain(dve, chain_c)

                def normalise_rows(j):
                    if j == NK - 1:
                        dve.tensor_copy(rows[0:T, j, :], lat[bs, :]).then_inc(crows.sem, 1)
                        return
                    link(dve.scalar_tensor_tensor(rows[:, j, :], ctx3[:, j, :], stats[b][:, 2 * j:2 * j + 1],
                                                  M.w("x1_ctx_w"), ALU.subtract, ALU.mult))
                    dve.scalar_tensor_tensor(rows[:, j, :], rows[:, j, :], deviations[b][:, j:j + 1],
                                             M.w("x1_ctx_b"), ALU.mult, ALU.add).then_inc(crows.sem, 1)

                dve.wait_ge(crstd.sem, crstd.at(b + 1))
                normalise_rows(0)
                normalise_rows(1)
                for j in range(NK + 1):
                    if j + 2 < NK:
                        normalise_rows(j + 2)
                    if j == 4:
                        dve.wait_ge(cseen.sem, cseen.at(16))
                        dve.tensor_scalar(mask[:, 0:S], seen, -GONE, GONE, ALU.mult, ALU.add)
                        dve.memset(mask[:, S:WIDE], 0.0)
                    if j < NK:
                        m = KV_TILES[j][1]
                        s_ = 16 * (j % 3)
                        dve.wait_ge(csq.sem, csq.at(j + 1))
                        if j >= 3:
                            dve.wait_ge(crn.sem, crn.at(j - 2))
                        link(dve.tensor_reduce(st[0:m, s_:s_ + 8],
                                               sqb[j % 2][0:m, :].rearrange("p (h d) -> p h d", d=64), AX.X, ALU.add))
                        dve.tensor_scalar(st[0:m, s_:s_ + 8], st[0:m, s_:s_ + 8], 1e-24, None,
                                          ALU.max).then_inc(cn2.sem, 1)
                    if j >= 1:
                        i = j - 1
                        m = KV_TILES[i][1]
                        s_ = 16 * (i % 3)
                        dve.wait_ge(crn.sem, crn.at(i + 1))
                        if i >= 3:
                            dve.wait_ge(ckt.sem, ckt.at(i - 2))
                        dve.tensor_tensor(kn[i % 3][0:m, :].rearrange("p (h d) -> p h d", d=64),
                                          banks[i % 3][0:m, :].rearrange("p (h d) -> p h d", d=64),
                                          st[0:m, s_ + 8:s_ + 16].unsqueeze(2).broadcast_to((m, 8, 64)),
                                          ALU.mult).then_inc(ckn.sem, 1)
                link.end()
        cseen.passed(16)
        for c in (crows, ct, cm, ck, csq, cn2, crn, ckn, ckt, ckm):
            c.passed(NK)

        def keep_rows(dve, link, u):
            return dve.tensor_copy(UT[:, 2 * u:2 * u + 2, bs], M.psD[:, 0:P].rearrange("p (h t) -> p h t", t=T))

        attend(nc, M, units=4, rows=P, tiles=KV_TILES, subs=1,
               queries=lambda u, s: qb[:, b, u, :],
               keys=lambda u, a, m: kT[:, u, a:a + m],
               values=lambda u, j: rows[0:KV_TILES[j][1], j, :],
               bufs=[M.at(a, 1792) for a in A1_BUF], pt=M.at(A1_PT, 14 * P), consume=keep_rows, bias=lambda u: mask)

    crstd.passed(2)
    done, var, rstd = (M.count("x1o_" + k) for k in ("projected", "var", "rstd"))
    y = M.at(A1_LAT, P)
    with nc.Block(no_gpsimd_drain=True) as block:
        @block.tensor
        def _(pe):
            for h in range(8):
                mm = pe.matmul(M.psA[:, 0:P], UT[:, h, :], M.w("x1_vo")[:, P * h:P * (h + 1)], start=(h == 0),
                               stop=(h == 7))
            mm.then_inc(done.sem, 1)

        @block.vector
        def _(dve):
            link = Chain(dve, chain_c)
            dve.wait_ge(done.sem, done.at(1))
            link(dve.bn_stats(M.stat[:, 0:6], M.psA[:, 0:P]))
            link(dve.bn_aggr(M.stat[:, 6:8], M.stat[:, 0:6]))
            dve.tensor_scalar(M.stat[:, 8:9], M.stat[:, 7:8], EPS, None, ALU.add).then_inc(var.sem, 1)
            dve.wait_ge(rstd.sem, rstd.at(1))
            link(dve.tensor_scalar(y, M.psA[:, 0:P], M.stat[:, 6:7], M.stat[:, 9:10], ALU.subtract, ALU.mult))
            link(dve.tensor_tensor(y, y, M.w("x1_out_w"), ALU.mult))
            link(dve.tensor_tensor(y, y, M.w("x1_out_b"), ALU.add))
            link(dve.tensor_tensor(M.x[:, :], M.x[:, :], y, ALU.add))
            link.end()

        @block.gpsimd
        def _(pool):
            pool.wait_ge(var.sem, var.at(1))
            pool.tensor_tensor(M.stat[:, 9:10], M.stat[:, 8:9], M.w("neg_half")[:, 0:1], ALU.pow).then_inc(rstd.sem, 1)
    for c in (done, var, rstd):
        c.passed(1)


def recurrence(nc, M):
    proj, shifted, expd, scanned, turned = (
        M.count("rc_" + k) for k in ("projected", "shifted", "exponential", "scanned", "turned"))
    chain_c = M.count("rc_dve_chain")
    z, inj, out = M.at(0, P), M.at(P, P), M.at(2 * P, P)
    norm = LayerNorm(M)
    with nc.Block(no_gpsimd_drain=True) as block:
        @block.gpsimd
        def _(pool):
            norm.on_gpsimd(pool)

        @block.tensor
        def _(pe):
            norm.on_tensor(pe)
            pe.matmul(M.psA[:, 0:P], M.w("rc_wd"), M.xnT[:, :], start=True, stop=True)
            pe.matmul(M.psA[:, P:2 * P], M.w("rc_wi"), M.xnT[:, :], start=True, stop=True).then_inc(proj.sem, 1)
            pe.wait_ge(scanned.sem, scanned.at(1))
            pe.transpose(M.psB[:, 0:P], out, M.w("ident")).then_inc(turned.sem, 1)

        @block.scalar
        def _(act):
            norm.on_scalar(act)
            act.wait_ge(shifted.sem, shifted.at(1))
            act.activation(z, z, ACT.Exp, scale=-1.0).then_inc(expd.sem, 1)

        @block.vector
        def _(dve):
            norm.on_vector(dve)
            link = Chain(dve, chain_c)
            dve.wait_ge(proj.sem, proj.at(1))
            dve.tensor_scalar(z, M.psA[:, 0:P], M.w("rc_bd"), None, ALU.add).then_inc(shifted.sem, 1)
            link(dve.tensor_scalar(inj, M.psA[:, P:2 * P], M.w("rc_bi"), None, ALU.add))
            dve.wait_ge(expd.sem, expd.at(1))
            link(dve.tensor_scalar(z, z, 1.0, None, ALU.add))
            link(dve.reciprocal(z, z))
            link(dve.tensor_tensor_scan(out[:, 0:T], z[:, 0:T], inj[:, 0:T], 0.0, ALU.mult, ALU.add))
            dve.tensor_tensor_scan(out[:, T:P], z[:, T:P], inj[:, T:P], 0.0, ALU.mult, ALU.add).then_inc(scanned.sem, 1)
            dve.wait_ge(turned.sem, turned.at(1))
            dve.tensor_tensor(M.x[:, :], M.x[:, :], M.psB[:, 0:P], ALU.add)
            link.end()
    norm.end()
    for c in (proj, shifted, expd, scanned, turned):
        c.passed(1)


A3_BUF = [0, 1664]
A3_PT, A3_Q, A3_UT, A3_MASKS = 3328, 4992, 7040, 9088
A3_MASKED = A3_MASKS + 4 * S
assert A3_MASKED + 2 * ((S + 3) // 4) <= ARENA


def fold_queries(nc, M, weights, heads, qp, load=None, spread=None):
    done = M.count("fold_queries")
    norm = LayerNorm(M)
    with nc.Block(no_gpsimd_drain=True) as block:
        if load is not None:
            @block.sync
            def _(sp):
                load(sp)

        @block.gpsimd
        def _(pool):
            norm.on_gpsimd(pool)

        @block.vector
        def _(dve):
            norm.on_vector(dve)
            if spread is not None:
                spread(dve)

        @block.tensor
        def _(pe):
            norm.on_tensor(pe)
            for h in range(heads):
                mm = pe.matmul(M.psS[:, h * P:(h + 1) * P], weights[:, h * P:(h + 1) * P], M.xnT[:, :],
                               start=True, stop=True)
            mm.then_inc(done.sem, 1)

        @block.scalar
        def _(act):
            norm.on_scalar(act)
            act.wait_ge(done.sem, done.at(1))
            act.activation(qp.rearrange("p (b h t) -> p h b t", b=2, t=T),
                           M.psS[:, 0:heads * P].rearrange("p (h b t) -> p h b t", b=2, t=T), ACT.Copy)
    done.passed(1)
    norm.end()


def cross2(nc, M):
    qp, UT = M.at(A3_Q, P), M.at(A3_UT, P)
    fold_queries(nc, M, M.w("x2_qk"), 1, qp)
    attend(nc, M, units=2, rows=T, tiles=CTX_TILES, subs=1,
           queries=lambda u, s: qp[:, u * T:(u + 1) * T], keys=lambda u, a, m: M.ctxT[u][:, a:a + m],
           values=lambda u, j: M.ctxN[u][0:CTX_TILES[j][1], j, :],
           bufs=[M.at(a, 1664) for a in A3_BUF], pt=M.at(A3_PT, 1664),
           consume=lambda dve, link, u: dve.tensor_copy(UT[:, u * T:(u + 1) * T], M.psD[:, 0:T]))
    project_out(nc, M, "x2", [(UT, M.w("x2_wv"))])


def cross3(nc, M, batch_masked):
    qp = M.at(A3_Q, H * P)
    UT = M.at(A3_UT, H * P).rearrange("p (h t) -> p h t", t=P)
    loaded = [M.count(f"x3_mask{b}_loaded") for b in range(2)]
    keep, gone = ([M.at(A3_MASKS + (2 * k + b) * S, S) for b in range(2)] for k in range(2))
    masked = [M.at(A3_MASKED + b * ((S + 3) // 4), (S + 3) // 4).bitcast(U8)[:, 0:S] for b in range(2)]

    def load_masks(sp):
        for b in range(2):
            for h in range(2):
                sp.dma_start(masked[b][h * T:(h + 1) * T], batch_masked(b)).then_inc(loaded[b].sem, 16)

    def spread_masks(dve):
        for b in range(2):
            dve.wait_ge(loaded[b].sem, loaded[b].at(32))
            dve.tensor_scalar(keep[b], masked[b], -1.0, 1.0, ALU.mult, ALU.add)
            dve.tensor_scalar(gone[b], masked[b], -8e9, None, ALU.mult)
    fold_queries(nc, M, M.w("x3_qk"), H, qp, load=load_masks, spread=spread_masks)
    for c in loaded:
        c.passed(32)

    def keep_rows(dve, link, u):
        b, p = u // 8, u % 8
        return dve.tensor_copy(UT[:, 2 * p:2 * p + 2, b * T:(b + 1) * T],
                               M.psD[:, 0:P].rearrange("p (h t) -> p h t", t=T))

    attend(nc, M, units=16, rows=P, tiles=CTX_TILES, subs=1,
           queries=lambda u, s: qp[:, u * P:(u + 1) * P], keys=lambda u, a, m: M.ctxT[u // 8][:, a:a + m],
           values=lambda u, j: M.ctxN[u // 8][0:CTX_TILES[j][1], j, :],
           bufs=[M.at(a, 1664) for a in A3_BUF], pt=M.at(A3_PT, 1664), consume=keep_rows,
           bias=lambda u: gone[u // 8], keep=lambda u: keep[u // 8], scale=0.125)
    vo = M.w("x3_vo")
    project_out(nc, M, "x3", [(UT[:, h, :], vo[:, P * h:P * (h + 1)]) for h in range(H)])


def quantised(nc, M):
    low, low_moved, done = (M.count("qf_" + k) for k in ("low_rank", "low_rank_moved", "done"))
    chain_c = M.count("qf_dve_chain")
    xa = M.at(0, P, 16)
    norm = LayerNorm(M)
    with nc.Block(no_gpsimd_drain=True) as block:
        @block.gpsimd
        def _(pool):
            norm.on_gpsimd(pool)

        @block.scalar
        def _(act):
            norm.on_scalar(act)

        @block.tensor
        def _(pe):
            norm.on_tensor(pe)
            pe.matmul(M.psB[0:16, 0:P], M.w("qf_a"), M.xnT[:, :], start=True, stop=True).then_inc(low.sem, 1)
            pe.matmul(M.psA[:, 0:P], M.xnT[:, :], M.w("qf_w"), start=True, stop=False)
            pe.wait_ge(low_moved.sem, low_moved.at(1))
            pe.matmul(M.psA[:, 0:P], xa, M.w("qf_b", 16), start=False, stop=True).then_inc(done.sem, 1)

        @block.vector
        def _(dve):
            norm.on_vector(dve)
            dve.wait_ge(norm.normed.sem, norm.normed.at(1))
            link = Chain(dve, chain_c)
            link(dve.tensor_tensor(M.x[:, :], M.x[:, :], M.w("qf_bias"), ALU.add))
            dve.wait_ge(low.sem, low.at(1))
            dve.tensor_copy(xa, M.psB[0:16, 0:P]).then_inc(low_moved.sem, 1)
            dve.wait_ge(done.sem, done.at(1))
            dve.tensor_tensor(M.x[:, :], M.x[:, :], M.psA[:, 0:P], ALU.add)
            link.end()
    norm.end()
    for c in (low, low_moved, done):
        c.passed(1)


def prepare(nc, M, A):
    loaded, folded, moved, exps, absmax, allmax, half = (
        M.count("pr_" + k) for k in ("loaded", "folded", "moved", "exponentials", "absmax", "allmax", "dots"))
    chain_c = M.count("pr_dve_chain")
    cleared, pair = M.count("pr_tails_cleared"), M.count("pair_loaded")
    blob, folds = A["weights"], A["folds"]
    n_blob = blob.shape[1]
    cols = folds.shape[1]
    fold = M.at(0, cols)
    q3, k3, v3, o3, v1, o1 = (fold[0:64, a:b] for a, b in (
        (0, 2048), (2048, 4096), (4096, 6144), (6144, 8192), (8192, 9216), (9216, 10240)))
    jobs = [(q3, k3, M.w("x3_qk"), H), (v3, o3, M.w("x3_vo"), H), (v1, o1, M.w("x1_vo"), 8)]
    with nc.Block(no_gpsimd_drain=True) as block:
        @block.sync
        def _(sp):
            sp.dma_start(fold, folds).then_inc(loaded.sem, 16)
            sp.dma_start(M.weights[:, 0:n_blob], blob).then_inc(loaded.sem, 16)
            sp.wait_ge(cleared.sem, cleared.at(2))
            load_pair(sp, M, 0, A)
            sp.wait_ge(pair.sem, pair.at(16 * PAIR_LOADS))

        @block.tensor
        def _(pe):
            pe.wait_ge(loaded.sem, loaded.at(32))
            for i, (lhs, rhs, _, heads) in enumerate(jobs):
                if i:
                    pe.wait_ge(moved.sem, moved.at(i))
                for h in range(heads):
                    c = slice(h * P, (h + 1) * P)
                    mm = pe.matmul(M.psS[:, c], lhs[:, c], rhs[:, c], start=True, stop=True)
                mm.then_inc(folded.sem, 1)
            pe.matmul(M.psA[:, 0:P], fold[:, 10240:10240 + P], fold[:, 10240 + P:10240 + 2 * P], start=True,
                      stop=True).then_inc(folded.sem, 1)

        @block.scalar
        def _(act):
            for i, (_, _, dst, heads) in enumerate(jobs):
                act.wait_ge(folded.sem, folded.at(i + 1))
                act.activation(dst, M.psS[:, 0:heads * P], ACT.Copy).then_inc(moved.sem, 1)
            act.wait_ge(folded.sem, folded.at(4))
            act.activation(M.w("x2_qk"), M.psA[:, 0:P], ACT.Copy)
            act.wait_ge(half.sem, half.at(1))
            act.activation(M.small[:, 2:4], M.small[:, 0:2], ACT.Exp).then_inc(exps.sem, 1)

        @block.gpsimd
        def _(pool):
            pool.wait_ge(absmax.sem, absmax.at(1))
            pool.partition_all_reduce(M.small[:, 9:10], M.small[:, 8:9], P, bass.bass_isa.ReduceOp.max).then_inc(allmax.sem, 1)

        @block.vector
        def _(dve):
            link = Chain(dve, chain_c)
            for b in range(2):
                dve.memset(M.ctxN[b][:, NT - 1, :], 0.0).then_inc(cleared.sem, 1)
            dve.wait_ge(loaded.sem, loaded.at(32))
            link(dve.scalar_tensor_tensor(M.w("x1_q_scale"), M.w("x1_q_scale"), 8.0, M.w("x1_k_scale"), ALU.mult,
                                          ALU.mult))
            lam = M.w("x0_lambda").rearrange("p (a b d) -> p a b d", a=2, b=2)
            link(dve.tensor_tensor(M.small[:, 16:24].rearrange("p (a d) -> p a d", a=2), lam[:, :, 0, :],
                                   lam[:, :, 1, :], ALU.mult))
            dve.tensor_reduce(M.small[:, 0:2], M.small[:, 16:24].rearrange("p (a d) -> p a d", a=2), AX.X,
                              ALU.add).then_inc(half.sem, 1)
            dve.wait_ge(exps.sem, exps.at(1))
            link(dve.tensor_tensor(M.small[:, 4:5], M.small[:, 3:4], M.small[:, 2:3], ALU.subtract))
            link(dve.tensor_scalar(M.lam[:, :], M.small[:, 4:5], LAMBDA_INIT, None, ALU.subtract))
            link(dve.tensor_scalar(M.small[:, 5:6], M.lam[:, :], 1.0, 1.0 - LAMBDA_INIT, ALU.add, ALU.mult))
            link(dve.tensor_tensor(M.w("x0_bv"), M.w("x0_bv"), M.small[:, 5:6], ALU.mult))
            w = M.w("qf_w")
            dve.tensor_reduce(M.small[:, 8:9], w, AX.X, ALU.max, apply_absolute_value=True).then_inc(absmax.sem, 1)
            dve.wait_ge(allmax.sem, allmax.at(1))
            link(dve.tensor_scalar(M.small[:, 10:11], M.small[:, 9:10], 1.0 / 7.0, None, ALU.mult))
            link(dve.reciprocal(M.small[:, 11:12], M.small[:, 10:11]))
            half_ulp = 1.5 * 2.0 ** 23
            link(dve.tensor_scalar(w, w, M.small[:, 11:12], half_ulp, ALU.mult, ALU.add))
            link(dve.tensor_scalar(w, w, half_ulp, 7.0, ALU.subtract, ALU.min))
            link(dve.tensor_scalar(w, w, -8.0, M.small[:, 10:11], ALU.max, ALU.mult))
            link.end()
    loaded.passed(32)
    cleared.passed(2)
    pair.passed(16 * PAIR_LOADS)
    folded.passed(4)
    moved.passed(3)
    for c in (exps, absmax, allmax, half):
        c.passed(1)


PAIR_LOADS = 7


def load_pair(sp, M, i, A):
    loaded = M.count("pair_loaded")
    sp.dma_start(M.x_next[:, :], A["x"][bass.ds(i, 1)].rearrange("o t d -> (o t) d")).then_inc(loaded.sem, 16)
    for b in range(2):
        sp.dma_start(M.ctxT[b][:, :], A["ctxT"][bass.ds(2 * i + b, 1)].rearrange("o d s -> (o d) s")).then_inc(loaded.sem, 16)
        ctx = A["ctx"][bass.ds(2 * i + b, 1)].rearrange("o s d -> (o s) d")
        sp.dma_start(M.ctxN[b][:, 0:12, :], ctx[0:12 * P].rearrange("(j p) d -> p j d", p=P)).then_inc(loaded.sem, 16)
        sp.dma_start(M.ctxN[b][0:TAIL, 12, :], ctx[12 * P:S]).then_inc(loaded.sem, 16)


def take_latents(nc, M):
    with nc.Block(no_gpsimd_drain=True) as block:
        @block.vector
        def _(dve):
            dve.tensor_copy(M.x[:, :], M.x_next[:, :])


def store_pair(nc, M, i, out):
    stored, loaded = M.count("pair_stored"), M.count("pair_loaded")
    with nc.Block(no_gpsimd_drain=True) as block:
        @block.sync
        def _(sp):
            sp.dma_start(out[bass.ds(i, 1)].rearrange("o t d -> (o t) d"), M.x[:, :]).then_inc(stored.sem, 16)
            sp.wait_ge(stored.sem, stored.at(16))
            sp.wait_ge(loaded.sem, loaded.at(16 * PAIR_LOADS))
    stored.passed(16)
    loaded.passed(16 * PAIR_LOADS)


def restart(nc, M):
    numbers = sorted(c.sem.num for c in M.counts.values())
    first = last = numbers[0]
    for n in numbers[1:] + [None]:
        if n is None or n != last + 1:
            nc.gpsimd.sem_clear(range(first, last + 1))
            first = n
        last = n
    for c in M.counts.values():
        c.base = 0
    nc.all_engine_barrier(sem_only=True)


def program(nc, A, regions, out, upto=12):
    with ExitStack() as ctx:
        M = Machine(nc, ctx, regions)
        prepare(nc, M, A)
        restart(nc, M)

        def wide(name):
            return lambda e, c: M.w(name)[:, 512 * e + P * c:512 * e + P * (c + 1)]

        def first(k):
            return lambda e, c: M.at(EXPERTS0 + 2048 * k + 512 * e + P * c, P)

        layers = [
            lambda i: cross0(nc, M),
            lambda i: self_attention(nc, M, "a0", rope="0", biased=False, causal=False, scale=1.0,
                                     load=lambda sp: load_experts0(sp, M, A["experts0"])),
            lambda i: experts(nc, M, "m0", E=4, kind="silu", up=first(0), up3=first(1), down=first(2),
                            router=M.w("m0_router"), router_bias=M.w("m0_router_b")),
            lambda i: cross1(nc, M, lambda b: A["seen"][bass.ds(2 * i + b, 1)]),
            lambda i: recurrence(nc, M),
            lambda i: experts(nc, M, "m1", E=8, kind="relu", up=wide("m1_up"), up3=None, down=wide("m1_down"),
                            router=M.w("m1_router"), b1=M.w("m1_b1"), b2=M.w("m1_b2", 8), floor=1e-9),
            lambda i: cross2(nc, M),
            lambda i: self_attention(nc, M, "a2", rope="1", biased=True, causal=True, scale=1.0 / math.sqrt(HD)),
            lambda i: experts(nc, M, "m2", E=8, kind="gelu", up=wide("m2_up"), up3=None, down=wide("m2_down"),
                            router=M.w("m2_router"), b1=M.w("m2_b1"), b2=M.w("m2_b2", 8), by_batch=True),
            lambda i: cross3(nc, M, lambda b: A["masked"][bass.ds(2 * i + b, 1)].rearrange("o t s -> (o t) s")),
            lambda i: self_attention(nc, M, "a3", biased=True, causal=True, scale=1.0 / math.sqrt(HD), top=32,
                                     load=lambda sp: load_pair(sp, M, i + 1, A)),
            lambda i: quantised(nc, M),
        ]
        with nc.Fori(0, out.shape[0]) as i:
            take_latents(nc, M)
            for n, layer in enumerate(layers[:upto]):
                layer(i)
            store_pair(nc, M, i, out)
            restart(nc, M)


def layout(w):
    import numpy as np
    T_ = lambda a: np.ascontiguousarray(np.asarray(a).T)
    row = lambda a, p=P: np.broadcast_to(np.asarray(a)[None, :], (p, np.asarray(a).shape[0]))
    col = lambda a: np.asarray(a)[:, None]
    idx = np.arange(P)
    swap0 = (idx // HD) * HD + (idx % HD ^ 1)
    swap1 = (idx // HD) * HD + (idx % HD + HD // 2) % HD
    qkv0 = np.asarray(w["L0_attn_w_qkv"]).reshape(H, 3, HD, P)
    wq0, wk0, wv0 = (qkv0[:, j].reshape(P, P) for j in range(3))
    ip, ib = np.asarray(w["L0_xattn_in_proj_weight"]), np.asarray(w["L0_xattn_in_proj_bias"])
    up = lambda a: np.asarray(a).transpose(1, 0, 2).reshape(P, -1)
    down = lambda a: np.asarray(a).reshape(-1, 4, P, P).transpose(2, 0, 1, 3).reshape(P, -1)
    b1 = lambda a: np.asarray(a).reshape(8, 4, P).transpose(2, 0, 1).reshape(P, 32)
    head_t = lambda a, h: np.asarray(a).reshape(P, h, 64).transpose(2, 1, 0).reshape(64, -1)
    head_r = lambda a, h: np.asarray(a).reshape(h, 64, P).transpose(1, 0, 2).reshape(64, -1)
    wkv = np.asarray(w["L1_xattn_Wkv"])
    blocks = dict(constants())
    blocks.update({
        "x0_wq": T_(ip[0:P]), "x0_wk": T_(ip[P:2 * P]), "x0_wv": T_(ip[2 * P:]), "x0_wo": T_(w["L0_xattn_out_proj_weight"]),
        "x0_bq": col(ib[0:P]), "x0_bk": col(ib[P:2 * P]), "x0_bv": col(ib[2 * P:]),
        "x0_bo": row(w["L0_xattn_out_proj_bias"]),
        "x0_lambda": np.concatenate([row(w["L0_xattn_lambda_" + k]) for k in ("q1", "k1", "q2", "k2")], axis=1),
        "a0_wq": T_(wq0), "a0_wk": T_(wk0), "a0_wv": T_(wv0), "a0_wq_turned": T_(wq0[swap0]),
        "a0_wk_turned": T_(wk0[swap0]), "a0_wo": T_(w["L0_attn_w_out"]),
        "m0_router": w["L0_ffn_router_w"], "m0_router_b": row(w["L0_ffn_router_b"]),
        "x1_ctx_w": row(w["L1_xattn_ln_x_w"]), "x1_ctx_b": row(w["L1_xattn_ln_x_b"]),
        "x1_lat_w": row(w["L1_xattn_ln_l_w"]), "x1_lat_b": row(w["L1_xattn_ln_l_b"]),
        "x1_wq": w["L1_xattn_Wq"], "x1_wk": wkv[:, 0:512],
        "x1_q_scale": row(w["L1_xattn_q_scale"]), "x1_k_scale": row(w["L1_xattn_k_scale"]),
        "x1_out_w": row(w["L1_xattn_ln_o_w"]), "x1_out_b": row(w["L1_xattn_ln_o_b"]),
        "rc_wd": T_(w["L1_attn_W_decay"]), "rc_wi": T_(w["L1_attn_W_input"]),
        "rc_bd": col(w["L1_attn_b_decay"]), "rc_bi": col(w["L1_attn_b_input"]),
        "m1_router": T_(w["L1_ffn_router_w"]), "m1_up": up(np.asarray(w["L1_ffn_w1"]).transpose(0, 2, 1)),
        "m1_down": down(np.asarray(w["L1_ffn_w2"]).transpose(0, 2, 1)), "m1_b1": b1(w["L1_ffn_b1"]),
        "m1_b2": w["L1_ffn_b2"],
        "x2_wv": T_(w["L2_xattn_Wv"]),
        "m2_router": w["L2_ffn_gate_w"], "m2_up": up(w["L2_ffn_w1"]), "m2_down": down(w["L2_ffn_w2"]),
        "m2_b1": b1(w["L2_ffn_b1"]), "m2_b2": w["L2_ffn_b2"],
        "qf_w": w["L3_ffn_kernel"], "qf_a": w["L3_ffn_a"], "qf_b": w["L3_ffn_b"], "qf_bias": row(w["L3_ffn_bias"]),
    })
    for n, L in (("a2", "L2_attn_"), ("a3", "L3_attn_")):
        blocks.update({n + "_w" + k: T_(w[L + "W" + k]) for k in "qkvo"})
        blocks.update({n + "_b" + k: col(w[L + "b" + k]) for k in "qk"})
        blocks.update({n + "_b" + k: row(w[L + "b" + k]) for k in "vo"})
    for k in "qk":
        blocks["a2_w" + k + "_turned"] = T_(np.asarray(w["L2_attn_W" + k])[swap1])
        blocks["a2_b" + k + "_turned"] = col(np.asarray(w["L2_attn_b" + k])[swap1])
    regions, a = {}, 0
    for name, block in blocks.items():
        regions[name] = (a, np.asarray(block).shape[1])
        a += np.asarray(block).shape[1]
    blob = np.zeros((P, a), np.float32)
    for name, block in blocks.items():
        block = np.asarray(block)
        s, n = regions[name]
        blob[0:block.shape[0], s:s + n] = block
    for name, n in (("x3_qk", H * P), ("x3_vo", H * P), ("x1_vo", 8 * P), ("x2_qk", P)):
        regions[name] = (a, n)
        a += n
    narrow = np.concatenate([head_t(w["L3_xattn_W_Q"], H), head_t(w["L3_xattn_W_K"], H), head_t(w["L3_xattn_W_V"], H),
                             head_r(w["L3_xattn_W_O"], H), head_t(wkv[:, 512:], 8), head_r(w["L1_xattn_Wo"], 8)], axis=1)
    folds = np.zeros((P, narrow.shape[1] + 2 * P), np.float32)
    folds[0:64, 0:narrow.shape[1]] = narrow
    folds[:, narrow.shape[1]:] = np.concatenate([w["L2_xattn_Wq"], w["L2_xattn_Wk"]], axis=1)
    experts0 = np.concatenate([up(w["L0_ffn_w1"]), up(w["L0_ffn_w3"]), down(w["L0_ffn_w2"])], axis=1)
    return regions, blob, folds, experts0


UPTO = 12


def kernel(**inputs):
    import numpy as np
    import concourse.bacc as bacc
    from concourse import mybir
    from concourse.bass_utils import run_bass_kernel_spmd

    w = {k: np.asarray(v) for k, v in inputs.items()}
    regions, blob, folds, experts0 = layout(w)
    ctx = w["ctx_1024"]
    n = w["x"].shape[0] // 2
    ctx = np.concatenate([ctx, np.zeros_like(ctx[0:2])])
    arrays = {
        "x": np.concatenate([w["x"].reshape(n, P, P), np.zeros((1, P, P), w["x"].dtype)]),
        "ctx": ctx, "ctxT": np.ascontiguousarray(ctx.transpose(0, 2, 1)),
        "seen": w["mask_BxS2_bk0"], "masked": w["mask_BxSxS2_bk1"],
        "weights": blob, "folds": folds, "experts0": experts0,
    }
    nc = bacc.Bacc("TRN2", target_bir_lowering=False, num_devices=1)
    A = {k: nc.dram_tensor("in_" + k, v.shape, mybir.dt.from_np(v.dtype), kind="ExternalInput").ap()
         for k, v in arrays.items()}
    out = nc.dram_tensor("out", (n, P, P), mybir.dt.float32, kind="ExternalOutput").ap()
    program(nc, A, regions, out, UPTO)
    r = run_bass_kernel_spmd(nc, [{"in_" + k: np.ascontiguousarray(v) for k, v in arrays.items()}], core_ids=[0])
    return r.results[0]["out"].reshape(2 * n, T, P)
```
